# Optimizing a Trainium2 kernel written in Bass

```python
import numpy as np
import jax
import jax.numpy as jnp

def _softmax(x, axis=-1):
    return jax.nn.softmax(x, axis=axis)

def _gelu(x):
    return jax.nn.gelu(x, approximate=True)

def _silu(x):
    return jax.nn.silu(x)

def _sigmoid(x):
    return jax.nn.sigmoid(x)

def _layernorm(x, axis=-1, eps=1e-05):
    m = jnp.mean(x, axis=axis, keepdims=True)
    v = jnp.var(x, axis=axis, keepdims=True)
    return (x - m) / jnp.sqrt(v + eps)

def _scatter_add(tgt, idx, src, axis=0):
    return tgt.at[idx].add(src)

def _segment_sum(src, seg, n):
    return jax.ops.segment_sum(src, seg, n)
kernel_name = 'mk_macaron_d1_jaxref_r8_2bc386'

def setup_inputs(seed: int=0):
    np.random.seed(seed)
    _w = jnp.asarray

    def _L0_attn_setup():
        import jax, jax.numpy as jnp
        import numpy as np
        H = 256
        NH = 16
        D = 128
        K = 4

        def _causal_depthwise_conv(x, w, b):
            S = x.shape[1]
            xp = jnp.pad(x, ((0, 0), (K - 1, 0), (0, 0)))
            y = b
            for j in range(K):
                y = y + xp[:, j:j + S, :] * w[:, j]
            return y

        def _forward(x, Wq, Wk, Wv, Wa, ba, Wb, bb, Wg, Wo, qcw, qcb, kcw, kcb, vcw, vcb, ln_w, ln_b):
            B, S, _ = x.shape
            q = _causal_depthwise_conv(x @ Wq, qcw, qcb)
            k = _causal_depthwise_conv(x @ Wk, kcw, kcb)
            v = _causal_depthwise_conv(x @ Wv, vcw, vcb)
            q = jax.nn.silu(q).reshape(B, S, NH, D)
            k = jax.nn.silu(k).reshape(B, S, NH, D) * D ** (-0.5)
            v = jax.nn.silu(v).reshape(B, S, NH, D)
            alpha = jax.nn.sigmoid(x @ Wa + ba)
            beta = jax.nn.sigmoid(x @ Wb + bb)
            qt = jnp.moveaxis(q, 1, 0)
            kt = jnp.moveaxis(k, 1, 0)
            vt = jnp.moveaxis(v, 1, 0)
            at = jnp.moveaxis(alpha, 1, 0)
            bt = jnp.moveaxis(beta, 1, 0)

            def step(St, inp):
                q_, k_, v_, a_, b_ = inp
                sk = jnp.einsum('bhij,bhj->bhi', St, k_)
                err = sk - v_
                Sn = a_[..., None, None] * St - b_[..., None, None] * err[..., None] * k_[..., None, :]
                o_ = jnp.einsum('bhij,bhj->bhi', Sn, q_)
                return (Sn, o_)
            S0 = jnp.zeros((B, NH, D, D), dtype=x.dtype)
            _, o = jax.lax.scan(step, S0, (qt, kt, vt, at, bt))
            o = jnp.moveaxis(o, 0, 1)
            mu = jnp.mean(o, axis=-1, keepdims=True)
            var = jnp.mean(jnp.square(o - mu), axis=-1, keepdims=True)
            o = (o - mu) * jax.lax.rsqrt(var + 1e-05) * ln_w + ln_b
            g = jax.nn.sigmoid(x @ Wg).reshape(B, S, NH, D)
            o = (o * g).reshape(B, S, NH * D)
            return o @ Wo
        key = jax.random.key(seed)
        ks = jax.random.split(key, 18)
        s = 0.02
        B, S = (2, 256)
        return {'x': jax.random.normal(ks[0], (B, S, H), dtype=jnp.float32), 'Wq': jax.random.normal(ks[1], (H, NH * D), dtype=jnp.float32) * s, 'Wk': jax.random.normal(ks[2], (H, NH * D), dtype=jnp.float32) * s, 'Wv': jax.random.normal(ks[3], (H, NH * D), dtype=jnp.float32) * s, 'Wa': jax.random.normal(ks[4], (H, NH), dtype=jnp.float32) * s, 'ba': jax.random.normal(ks[5], (NH,), dtype=jnp.float32) * s, 'Wb': jax.random.normal(ks[6], (H, NH), dtype=jnp.float32) * s, 'bb': jax.random.normal(ks[7], (NH,), dtype=jnp.float32) * s, 'Wg': jax.random.normal(ks[8], (H, NH * D), dtype=jnp.float32) * s, 'Wo': jax.random.normal(ks[9], (NH * D, H), dtype=jnp.float32) * s, 'qcw': jax.random.normal(ks[10], (NH * D, K), dtype=jnp.float32) * s, 'qcb': jax.random.normal(ks[11], (NH * D,), dtype=jnp.float32) * s, 'kcw': jax.random.normal(ks[12], (NH * D, K), dtype=jnp.float32) * s, 'kcb': jax.random.normal(ks[13], (NH * D,), dtype=jnp.float32) * s, 'vcw': jax.random.normal(ks[14], (NH * D, K), dtype=jnp.float32) * s, 'vcb': jax.random.normal(ks[15], (NH * D,), dtype=jnp.float32) * s, 'ln_w': jnp.ones((D,), dtype=jnp.float32), 'ln_b': jnp.zeros((D,), dtype=jnp.float32)}
    _L0_attn_in = _L0_attn_setup()

    def _L0_ffn_setup():
        import jax, jax.numpy as jnp
        import numpy as np
        B, S, H, I = (1, 64, 256, 768)

        def _quantized_matmul(x, w, scale):
            wq = w.astype(jnp.float8_e4m3fn).astype(x.dtype)
            y = jnp.einsum('bsi,io->bso', x, wq)
            return y * scale
        key = jax.random.key(seed)
        ks = jax.random.split(key, 7)
        return {'x': jax.random.normal(ks[0], (B, S, H), dtype=jnp.float32), 'gate_w': jax.random.normal(ks[1], (H, I), dtype=jnp.float32) * 0.02, 'up_w': jax.random.normal(ks[2], (H, I), dtype=jnp.float32) * 0.02, 'down_w': jax.random.normal(ks[3], (I, H), dtype=jnp.float32) * 0.02, 'gate_scale': jax.random.uniform(ks[4], (I,), dtype=jnp.float32, minval=0.5, maxval=1.5), 'up_scale': jax.random.uniform(ks[5], (I,), dtype=jnp.float32, minval=0.5, maxval=1.5), 'down_scale': jax.random.uniform(ks[6], (H,), dtype=jnp.float32, minval=0.5, maxval=1.5)}
    _L0_ffn_in = _L0_ffn_setup()
    _d = {'L0_attn_x': _L0_attn_in['x'], 'L0_attn_Wq': _L0_attn_in['Wq'], 'L0_attn_Wk': _L0_attn_in['Wk'], 'L0_attn_Wv': _L0_attn_in['Wv'], 'L0_attn_Wa': _L0_attn_in['Wa'], 'L0_attn_ba': _L0_attn_in['ba'], 'L0_attn_Wb': _L0_attn_in['Wb'], 'L0_attn_bb': _L0_attn_in['bb'], 'L0_attn_Wg': _L0_attn_in['Wg'], 'L0_attn_Wo': _L0_attn_in['Wo'], 'L0_attn_qcw': _L0_attn_in['qcw'], 'L0_attn_qcb': _L0_attn_in['qcb'], 'L0_attn_kcw': _L0_attn_in['kcw'], 'L0_attn_kcb': _L0_attn_in['kcb'], 'L0_attn_vcw': _L0_attn_in['vcw'], 'L0_attn_vcb': _L0_attn_in['vcb'], 'L0_attn_ln_w': _L0_attn_in['ln_w'], 'L0_attn_ln_b': _L0_attn_in['ln_b'], 'L0_ffn_gate_w': _L0_ffn_in['gate_w'], 'L0_ffn_up_w': _L0_ffn_in['up_w'], 'L0_ffn_down_w': _L0_ffn_in['down_w'], 'L0_ffn_gate_scale': _L0_ffn_in['gate_scale'], 'L0_ffn_up_scale': _L0_ffn_in['up_scale'], 'L0_ffn_down_scale': _L0_ffn_in['down_scale']}
    _x0 = _d['L0_attn_x']
    _d['L0_attn_x'] = jax.random.normal(jax.random.fold_in(jax.random.key(seed), 1), (8, 512, 256), dtype=_x0.dtype)
    del _x0
    return _d

def reference(L0_attn_x, L0_attn_Wq, L0_attn_Wk, L0_attn_Wv, L0_attn_Wa, L0_attn_ba, L0_attn_Wb, L0_attn_bb, L0_attn_Wg, L0_attn_Wo, L0_attn_qcw, L0_attn_qcb, L0_attn_kcw, L0_attn_kcb, L0_attn_vcw, L0_attn_vcb, L0_attn_ln_w, L0_attn_ln_b, L0_ffn_gate_w, L0_ffn_up_w, L0_ffn_down_w, L0_ffn_gate_scale, L0_ffn_up_scale, L0_ffn_down_scale):

    def _L0_attn_ref(x, Wq, Wk, Wv, Wa, ba, Wb, bb, Wg, Wo, qcw, qcb, kcw, kcb, vcw, vcb, ln_w, ln_b):
        import jax, jax.numpy as jnp
        import numpy as np
        H = 256
        NH = 16
        D = 128
        K = 4

        def _causal_depthwise_conv(x, w, b):
            S = x.shape[1]
            xp = jnp.pad(x, ((0, 0), (K - 1, 0), (0, 0)))
            y = b
            for j in range(K):
                y = y + xp[:, j:j + S, :] * w[:, j]
            return y

        def _forward(x, Wq, Wk, Wv, Wa, ba, Wb, bb, Wg, Wo, qcw, qcb, kcw, kcb, vcw, vcb, ln_w, ln_b):
            B, S, _ = x.shape
            q = _causal_depthwise_conv(x @ Wq, qcw, qcb)
            k = _causal_depthwise_conv(x @ Wk, kcw, kcb)
            v = _causal_depthwise_conv(x @ Wv, vcw, vcb)
            q = jax.nn.silu(q).reshape(B, S, NH, D)
            k = jax.nn.silu(k).reshape(B, S, NH, D) * D ** (-0.5)
            v = jax.nn.silu(v).reshape(B, S, NH, D)
            alpha = jax.nn.sigmoid(x @ Wa + ba)
            beta = jax.nn.sigmoid(x @ Wb + bb)
            qt = jnp.moveaxis(q, 1, 0)
            kt = jnp.moveaxis(k, 1, 0)
            vt = jnp.moveaxis(v, 1, 0)
            at = jnp.moveaxis(alpha, 1, 0)
            bt = jnp.moveaxis(beta, 1, 0)

            def step(St, inp):
                q_, k_, v_, a_, b_ = inp
                sk = jnp.einsum('bhij,bhj->bhi', St, k_)
                err = sk - v_
                Sn = a_[..., None, None] * St - b_[..., None, None] * err[..., None] * k_[..., None, :]
                o_ = jnp.einsum('bhij,bhj->bhi', Sn, q_)
                return (Sn, o_)
            S0 = jnp.zeros((B, NH, D, D), dtype=x.dtype)
            _, o = jax.lax.scan(step, S0, (qt, kt, vt, at, bt))
            o = jnp.moveaxis(o, 0, 1)
            mu = jnp.mean(o, axis=-1, keepdims=True)
            var = jnp.mean(jnp.square(o - mu), axis=-1, keepdims=True)
            o = (o - mu) * jax.lax.rsqrt(var + 1e-05) * ln_w + ln_b
            g = jax.nn.sigmoid(x @ Wg).reshape(B, S, NH, D)
            o = (o * g).reshape(B, S, NH * D)
            return o @ Wo
        return _forward(x, Wq, Wk, Wv, Wa, ba, Wb, bb, Wg, Wo, qcw, qcb, kcw, kcb, vcw, vcb, ln_w, ln_b)

    def _L0_ffn_ref(x, gate_w, up_w, down_w, gate_scale, up_scale, down_scale):
        import jax, jax.numpy as jnp
        import numpy as np
        B, S, H, I = (1, 64, 256, 768)

        def _quantized_matmul(x, w, scale):
            wq = w.astype(jnp.float8_e4m3fn).astype(x.dtype)
            y = jnp.einsum('bsi,io->bso', x, wq)
            return y * scale
        gate = jax.nn.silu(_quantized_matmul(x, gate_w, gate_scale))
        up = _quantized_matmul(x, up_w, up_scale)
        fuse = gate * up
        return _quantized_matmul(fuse, down_w, down_scale)
    x = L0_attn_x
    x = x + 0.5 * _L0_ffn_ref(_layernorm(x, axis=-1), L0_ffn_gate_w, L0_ffn_up_w, L0_ffn_down_w, L0_ffn_gate_scale, L0_ffn_up_scale, L0_ffn_down_scale)
    x = x + _L0_attn_ref(_layernorm(x, axis=-1), L0_attn_Wq, L0_attn_Wk, L0_attn_Wv, L0_attn_Wa, L0_attn_ba, L0_attn_Wb, L0_attn_bb, L0_attn_Wg, L0_attn_Wo, L0_attn_qcw, L0_attn_qcb, L0_attn_kcw, L0_attn_kcb, L0_attn_vcw, L0_attn_vcb, L0_attn_ln_w, L0_attn_ln_b)
    x = x + 0.5 * _L0_ffn_ref(_layernorm(x, axis=-1), L0_ffn_gate_w, L0_ffn_up_w, L0_ffn_down_w, L0_ffn_gate_scale, L0_ffn_up_scale, L0_ffn_down_scale)
    return x

_drawn_inputs = setup_inputs


def setup_inputs(seed=0):
    import zlib

    import numpy as np

    out = dict(_drawn_inputs(seed))
    spreads = {'L0_attn_ln_w': (1.0, 0.6), 'L0_attn_ln_b': (0.0, 0.512)}
    factors = {'L0_attn_Wq': 8.0,
     'L0_attn_Wk': 8.0,
     'L0_attn_Wv': 8.0,
     'L0_attn_Wa': 8.0,
     'L0_attn_ba': 57.68,
     'L0_attn_Wb': 8.0,
     'L0_attn_bb': 64.0,
     'L0_attn_Wg': 7.536,
     'L0_attn_qcw': 8.0,
     'L0_attn_qcb': 8.0,
     'L0_attn_kcw': 8.0,
     'L0_attn_kcb': 8.0,
     'L0_attn_vcw': 8.0,
     'L0_attn_vcb': 8.0,
     'L0_ffn_gate_scale': 5.292,
     'L0_ffn_up_scale': 6.158,
     'L0_ffn_down_scale': 5.962}
    for name, (base, spread) in spreads.items():
        noise = np.random.default_rng([zlib.crc32(name.encode()), seed]).standard_normal(out[name].shape)
        drawn = base * np.exp(spread * noise) if base else spread * noise
        out[name] = jnp.asarray(drawn.astype(out[name].dtype))
    for name, factor in factors.items():
        out[name] = (out[name] * factor).astype(out[name].dtype)
    return out
```

```python
from contextlib import ExitStack

import numpy as np

import concourse.bass as bass
from concourse import mybir

F32 = mybir.dt.float32
F16 = mybir.dt.float16
I32 = mybir.dt.int32
ALU = mybir.AluOpType
ACT = mybir.ActivationFunctionType

B, S, H = 8, 512, 256
NH, D, TAPS = 16, 128, 4
FF = 768
P = 128
KT = H // P
MT = FF // P
C = 128
NC = S // C
G = 2
U = B // G
STEPS = NH * G * NC
SPH = G * NC
WS = 64.0
LEVELS = [2, 4, 8, 16, 32, 64]
NL = len(LEVELS)
EPS = 1e-5
CX = C + 1


def need(eng, sem, value):
    if isinstance(value, int) and value <= 0:
        return
    eng.wait_ge(sem, value)


def even(ap, m):
    return ap.rearrange("p u (b two m) -> p u b two m", two=2, m=m)[:, :, :, 0, :]


def odd(ap, m):
    return ap.rearrange("p u (b two m) -> p u b two m", two=2, m=m)[:, :, :, 1, :]


def halves(ap, m, which):
    return ap.rearrange("p (b two m) -> p b two m", two=2, m=m)[:, :, which, :]


def ffn_phase(nc, first, x_in, y_out, stream, z16, scratch, w):
    with ExitStack() as ctx:
        tag = "f1_" if first else "f3_"

        def sb(name, shape, dt=F32):
            return ctx.enter_context(nc.sbuf_tensor(tag + name, shape, dt))

        def sem(name):
            return ctx.enter_context(nc.semaphore(tag + name))

        bank = [ctx.enter_context(nc.psum_tensor(f"{tag}bank{i}", [P, 512], F32)) for i in range(8)]
        ident = sb("ident", [P, P])
        avg = sb("avg", [P, P])
        gs = sb("gs", [P, MT]); us = sb("us", [P, MT]); ds_ = sb("ds", [P, KT]); hds = sb("hds", [P, KT])
        wq16 = sb("wq16", [P, 3 * KT * FF], F16)
        gate16 = wq16[:, 0:KT * FF].rearrange("p (k n) -> p k n", k=KT)
        up16 = wq16[:, KT * FF:2 * KT * FF].rearrange("p (k n) -> p k n", k=KT)
        down16 = wq16[:, 2 * KT * FF:].rearrange("p (m n) -> p m n", m=MT)
        tok = sb("tok", [P, 2, 4, H])
        xb = sb("xb", [P, 2, KT, S])
        xc = sb("xc", [P, KT, S]); sq = sb("sq", [P, KT, S])
        ve = sb("ve", [P, S]); rs = sb("rs", [P, S]); nhalf = sb("nhalf", [P, S])
        zh = sb("zh", [P, KT, S], F16); zl = sb("zl", [P, KT, S], F16)
        sg = sb("sg", [P, 2, S]); hid = sb("hid", [P, 2, S])
        hh = sb("hh", [P, 2, S], F16); hl = sb("hl", [P, 2, S], F16)
        wraw = sb("wraw", [P, 3 * KT * FF]) if first else None
        wexp = sb("wexp", [P, KT * FF]) if first else None
        if first:
            wab = sb("wab", [P, KT, 2 * NH]); wab64 = sb("wab64", [P, KT, 2 * NH])
            wabh = sb("wabh", [P, KT, 2 * NH], F16); wabl = sb("wabl", [P, KT, 2 * NH], F16)
            bab = sb("bab", [2 * NH, 1])
            ab = sb("ab", [2 * NH, 2, NC, CX]); gx = sb("gx", [NH, 2, NC, CX])
            zero = sb("zero", [NH, C])
            bcol = sb("bcol", [P, NH, G, NC, U])

        s_w = sem("dma_weights"); s_x = [sem("dma_tokens0"), sem("dma_tokens1")]
        s_out = [sem("dma_out0"), sem("dma_out1")]; s_save = sem("dma_saved")
        s_const = sem("constants"); s_q = sem("quantise_step"); s_wab = sem("wab_step")
        s_wd = sem("weights_ready")
        p_tr = sem("pe_transposed"); p_mean = sem("pe_mean"); p_var = sem("pe_var")
        p_gate = sem("pe_gate"); p_up = sem("pe_up"); p_down = sem("pe_down")
        p_ab = sem("pe_ab"); p_abt = sem("pe_abt"); p_ot = sem("pe_out_transposed")
        a_x = sem("act_x"); a_sq = sem("act_sq"); a_ve = sem("act_ve"); a_zh = sem("act_zh")
        a_sg = sem("act_silu"); a_hh = sem("act_hh"); a_ab = sem("act_ab"); a_ot = sem("act_out")
        d_xc = sem("dve_centered"); d_z = sem("dve_z"); d_zl = sem("dve_zl"); d_h = sem("dve_hidden")
        d_y = sem("dve_y"); d_g = sem("dve_g"); d_b = sem("dve_bcol")
        g_rs = sem("pool_rstd"); g_hl = sem("pool_hl"); g_xs = sem("pool_stream")
        LN = 2 if first else 1

        x_tok = None if x_in is None else x_in.rearrange("b (t p) c -> b p t c", p=P)
        y_tok = None if y_out is None else y_out.rearrange("b (t p) c -> b p t c", p=P)
        a_rows, g_rows, b_cols, w_saved = scratch
        a_to = a_rows.rearrange("(h g c) (j x) -> g j h c x", h=NH, g=G, x=CX)
        g_to = g_rows.rearrange("(h g c) (j x) -> g j h c x", h=NH, g=G, x=CX)

        block = ctx.enter_context(nc.Block())

        @block.sync
        def _(sp):
            if first:
                sp.dma_start(wraw[:, 0:KT * FF].rearrange("p (k n) -> p k n", k=KT),
                             w["gate_w"].rearrange("(k p) n -> p k n", p=P)).then_inc(s_w, 16)
                sp.dma_start(wraw[:, KT * FF:2 * KT * FF].rearrange("p (k n) -> p k n", k=KT),
                             w["up_w"].rearrange("(k p) n -> p k n", p=P)).then_inc(s_w, 16)
                sp.dma_start(wraw[:, 2 * KT * FF:].rearrange("p (m n) -> p m n", m=MT),
                             w["down_w"].rearrange("(m p) n -> p m n", p=P)).then_inc(s_w, 16)
                sp.dma_start(wab[:, :, 0:NH], w["Wa"].rearrange("(k p) n -> p k n", p=P)).then_inc(s_w, 16)
                sp.dma_start(wab[:, :, NH:], w["Wb"].rearrange("(k p) n -> p k n", p=P)).then_inc(s_w, 16)
                sp.dma_start(bab[0:NH, :], w["ba"].rearrange("(p o) -> p o", o=1)).then_inc(s_w, 16)
                sp.dma_start(bab[NH:, :], w["bb"].rearrange("(p o) -> p o", o=1)).then_inc(s_w, 16)
            else:
                sp.dma_start(wq16[:, :], w_saved).then_inc(s_w, 16)
            sp.dma_start(gs[:, :], w["gate_scale"].rearrange("(m p) -> p m", p=P), allow_slow_non_contiguous=True).then_inc(s_w, 16)
            sp.dma_start(us[:, :], w["up_scale"].rearrange("(m p) -> p m", p=P), allow_slow_non_contiguous=True).then_inc(s_w, 16)
            sp.dma_start(ds_[:, :], w["down_scale"].rearrange("(m p) -> p m", p=P), allow_slow_non_contiguous=True).then_inc(s_w, 16)
            if first:
                with sp.Fori(0, B // 2) as it:
                    for g in range(2):
                        sp.wait_ge(p_tr, 2 * it)
                        sp.dma_start(tok[:, g], x_tok[bass.ds(it * 2 + g, 1)].rearrange("o p t c -> (o p) t c"))\
                            .then_inc(s_x[g], 16)
                sp.wait_ge(d_b, B)
                sp.dma_start(b_cols, bcol[:, :, :, :, :].rearrange("p h g c j -> p (h g c j)")).then_inc(s_save, 16)
                sp.wait_ge(s_wd, 1)
                sp.dma_start(w_saved, wq16[:, :]).then_inc(s_save, 16)
                sp.wait_ge(s_save, 32)
            for g in range(2):
                sp.wait_ge(s_out[g], (32 if first else 16) * B // 2)

        @block.gpsimd
        def _(pool):
            nc.gpsimd.memset(ident[:, :], 0.0).then_inc(s_const, 1)
            nc.gpsimd.memset(avg[:, :], 1.0 / H).then_inc(s_const, 1)
            nc.gpsimd.memset(nhalf[:, :], -0.5).then_inc(s_const, 1)
            if first:
                nc.gpsimd.memset(zero[:, :], 0.0)
                nc.gpsimd.memset(ab[:, :, :, :], 0.0)
                nc.gpsimd.memset(gx[:, :, :, :], 1.0)
            pool.wait_ge(s_const, 1)
            nc.gpsimd.affine_select(out=ident[:, :], in_=ident[:, :], compare_op=ALU.not_equal, fill=1.0,
                                    base=0, pattern=[[-1, P]], channel_multiplier=1).then_inc(s_const, 1)
            pool.wait_ge(s_const, 4)
            with pool.Fori(0, B // 2) as it:
                for g in range(2):
                    blk = it * 2 + g

                    def rstd(i):
                        pool.wait_ge(a_ve, LN * blk + i + 1)
                        pool.wait_ge(d_z, 2 * (LN * blk + i))
                        nc.gpsimd.tensor_tensor(rs[:, :], ve[:, :], nhalf[:, :], ALU.pow).then_inc(g_rs, 1)

                    rstd(0)
                    for m in range(MT):
                        q = MT * blk + m
                        pool.wait_ge(a_hh, q + 1)
                        pool.wait_ge(p_down, MT * blk + max(m - 1, 0))
                        nc.gpsimd.tensor_tensor(hl[:, m % 2], hid[:, m % 2], hh[:, m % 2],
                                                ALU.subtract).then_inc(g_hl, 1)
                    if first:
                        rstd(1)

        @block.vector
        def _(dve):
            qn = [0]

            def chain(ins):
                qn[0] += 1
                ins.then_inc(s_q, 1)
                dve.wait_ge(s_q, qn[0])

            n_dma = 10 if first else 4
            dve.wait_ge(s_w, 16 * n_dma)
            chain(nc.vector.tensor_scalar(hds[:, :], ds_[:, :], 0.5, None, ALU.mult))
            if first:
                chain(nc.vector.tensor_scalar(wab64[:, :, :], wab[:, :, :], WS, None, ALU.mult))
                chain(nc.vector.tensor_copy(wabh[:, :, :], wab64[:, :, :]))
                chain(nc.vector.tensor_tensor(wabl[:, :, :], wab64[:, :, :], wabh[:, :, :], ALU.subtract))
                for i in range(3):
                    r = wraw[:, i * KT * FF:(i + 1) * KT * FF]
                    e = wexp[:, :]
                    chain(nc.vector.tensor_scalar(e.bitcast(I32), r.bitcast(I32), 0x7F800000, None, ALU.bitwise_and))
                    chain(nc.vector.tensor_scalar(e, e, 2.0 ** -6, 1.5 * 2.0 ** 20, ALU.max, ALU.mult))
                    chain(nc.vector.tensor_tensor(r, r, e, ALU.add))
                    chain(nc.vector.tensor_tensor(r, r, e, ALU.subtract))
                    chain(nc.vector.tensor_scalar(e.bitcast(I32), r.bitcast(I32), 0x7FFFFFFF, None, ALU.bitwise_and))
                    chain(nc.vector.tensor_scalar(e, e, 448.0, 448.0, ALU.max, ALU.subtract))
                    chain(nc.vector.tensor_scalar(e, e, 3e38, 0.0, ALU.mult, ALU.mult))
                    chain(nc.vector.tensor_tensor(wq16[:, i * KT * FF:(i + 1) * KT * FF], r, e, ALU.add))
            nc.vector.tensor_copy(gs[:, 0:1], gs[:, 0:1]).then_inc(s_wd, 1)
            dve.wait_ge(s_const, 4)
            with dve.Fori(0, B // 2) as it:
                for g in range(2):
                    blk = it * 2 + g

                    def norm(i, src):
                        e = LN * blk + i
                        dve.wait_ge(p_mean, e + 1)
                        dve.wait_ge(a_sq, 2 * e)
                        if i == 0:
                            dve.wait_ge(a_x, KT * (blk + 1))
                        dve.wait_ge(d_z, 2 * e)
                        for k in range(KT):
                            nc.vector.tensor_tensor(xc[:, k], src[:, k], bank[0][:, :],
                                                    ALU.subtract).then_inc(d_xc, 1)
                        dve.wait_ge(g_rs, e + 1)
                        dve.wait_ge(a_sq, 2 * (e + 1))
                        dve.wait_ge(d_xc, 2 * (e + 1))
                        dve.wait_ge(a_zh, e)
                        dve.wait_ge(d_zl, 2 * e)
                        dve.wait_ge(p_var, e + 1)
                        for k in range(KT):
                            nc.vector.tensor_tensor(sq[:, k], xc[:, k], rs[:, :], ALU.mult).then_inc(d_z, 1)
                        dve.wait_ge(a_zh, e + 1)
                        for k in range(KT):
                            nc.vector.tensor_tensor(zl[:, k], sq[:, k], zh[:, k], ALU.subtract).then_inc(d_zl, 1)

                    x = xb[:, g]
                    norm(0, x)
                    for m in range(MT):
                        q = MT * blk + m
                        dve.wait_ge(p_up, q + 1)
                        dve.wait_ge(a_sg, q + 1)
                        dve.wait_ge(g_hl, MT * blk + max(m - 1, 0))
                        nc.vector.scalar_tensor_tensor(out=hid[:, m % 2], in0=bank[4 + m % 2][:, :],
                                                       scalar=us[:, m:m + 1], in1=sg[:, m % 2],
                                                       op0=ALU.mult, op1=ALU.mult).then_inc(d_h, 1)
                    dve.wait_ge(p_down, MT * (blk + 1))
                    for k in range(KT):
                        nc.vector.scalar_tensor_tensor(out=x[:, k], in0=bank[6 + k][:, :],
                                                       scalar=hds[:, k:k + 1], in1=x[:, k],
                                                       op0=ALU.mult, op1=ALU.add).then_inc(d_y, 1)
                    if first:
                        dve.wait_ge(d_y, 2 * (blk + 1))
                        norm(1, x)
                        dve.wait_ge(a_ab, blk + 1)
                        dve.wait_ge(s_out[g], it * 32)
                        for c in range(NC):
                            nc.vector.tensor_tensor_scan(gx[:, g, c, 1:CX], ab[0:NH, g, c, 1:CX], zero[:, :],
                                                         1.0, ALU.mult, ALU.add).then_inc(d_g, 1)
                        dve.wait_ge(p_abt, blk + 1)
                        nc.vector.tensor_scalar(
                            bcol[:, :, g, :, bass.ds(it, 1)].rearrange("p h c o -> p h (c o)"),
                            bank[3][:, 0:NC * 2 * NH].rearrange("p (c r) -> p r c", c=NC)[:, NH:, :],
                            1.0 / D, None, ALU.mult).then_inc(d_b, 1)

        @block.scalar
        def _(act):
            act.wait_ge(s_w, 16 * (10 if first else 4))
            act.wait_ge(s_wd, 1)
            with act.Fori(0, B // 2) as it:
                for g in range(2):
                    blk = it * 2 + g

                    def sl(ap):
                        return ap.rearrange("p (b s) -> p b s", b=B)[:, bass.ds(blk, 1), :]\
                            .rearrange("p o s -> p (o s)")

                    x = xb[:, g]
                    if first:
                        act.wait_ge(p_tr, blk + 1)
                        act.wait_ge(d_y, 4 * it)
                        act.wait_ge(a_ot, 4 * blk)
                    else:
                        act.wait_ge(p_ot, 4 * it)
                    for k in range(KT):
                        src = bank[k][:, :] if first else sl(stream[:, k])
                        nc.scalar.activation(x[:, k], src, ACT.Copy).then_inc(a_x, 1)

                    def norm(i):
                        e = LN * blk + i
                        act.wait_ge(d_xc, 2 * (e + 1))
                        act.wait_ge(d_zl, 2 * e)
                        act.wait_ge(a_zh, e)
                        for k in range(KT):
                            nc.scalar.activation(sq[:, k], xc[:, k], ACT.Square).then_inc(a_sq, 1)
                        act.wait_ge(p_var, e + 1)
                        act.wait_ge(g_rs, e)
                        nc.scalar.activation(ve[:, :], bank[1][:, :], ACT.Copy, bias=EPS).then_inc(a_ve, 1)
                        act.wait_ge(d_z, 2 * (e + 1))
                        if first:
                            act.wait_ge(p_ab, blk)
                            if i == 1:
                                act.wait_ge(p_up, MT * (blk + 1))
                        else:
                            act.wait_ge(p_up, MT * blk)
                        nc.scalar.activation(zh[:, :, :], sq[:, :, :], ACT.Copy).then_inc(a_zh, 1)

                    norm(0)

                    def high(m):
                        q = MT * blk + m
                        act.wait_ge(d_h, q + 1)
                        act.wait_ge(p_down, MT * blk + max(m - 1, 0))
                        nc.scalar.activation(hh[:, m % 2], hid[:, m % 2], ACT.Copy).then_inc(a_hh, 1)

                    for m in range(MT):
                        q = MT * blk + m
                        act.wait_ge(p_gate, q + 1)
                        act.wait_ge(d_h, MT * blk + max(m - 1, 0))
                        nc.scalar.activation(sg[:, m % 2], bank[2 + m % 2][:, :], ACT.Silu,
                                             scale=gs[:, m:m + 1]).then_inc(a_sg, 1)
                        if m:
                            high(m - 1)
                    high(MT - 1)
                    if first:
                        act.wait_ge(d_y, KT * (blk + 1))
                        for k in range(KT):
                            nc.scalar.activation(sl(stream[:, k]), x[:, k], ACT.Copy).then_inc(a_ot, 1)
                        norm(1)
                        act.wait_ge(d_zl, 2 * (2 * blk + 2))
                        for k in range(KT):
                            nc.scalar.activation(sl(z16[:, 0, k]), zh[:, k], ACT.Copy)
                            nc.scalar.activation(sl(z16[:, 1, k]), zl[:, k], ACT.Copy).then_inc(a_ot, 1)
                        act.wait_ge(p_ab, blk + 1)
                        act.wait_ge(s_out[g], it * 32)
                        nc.scalar.activation(ab[:, g, :, 1:CX], bank[2][0:2 * NH, :].rearrange("p (c x) -> p c x", c=NC),
                                             ACT.Sigmoid, bias=bab[:, :], scale=1.0 / WS).then_inc(a_ab, 1)
                        act.wait_ge(a_ab, blk + 1)
                        act.dma_start(a_to[g][bass.ds(it, 1)].rearrange("o h c x -> (o h) c x"),
                                      ab[0:NH, g]).then_inc(s_out[g], 16)
                        act.wait_ge(d_g, NC * (blk + 1))
                        act.dma_start(g_to[g][bass.ds(it, 1)].rearrange("o h c x -> (o h) c x"),
                                      gx[:, g]).then_inc(s_out[g], 16)
                    else:
                        for n in range(2):
                            act.wait_ge(p_ot, 2 * blk + n + 1)
                            if n == 0:
                                act.wait_ge(s_out[g], it * 16)
                            nc.scalar.activation(tok[:, g, 2 * n:2 * n + 2].rearrange("p t c -> p (t c)"),
                                                 bank[n][:, :], ACT.Copy).then_inc(a_ot, 1)
                        act.wait_ge(a_ot, 2 * (blk + 1))
                        act.dma_start(y_tok[bass.ds(blk, 1)].rearrange("o p t c -> (o p) t c"),
                                      tok[:, g]).then_inc(s_out[g], 16)

        @block.tensor
        def _(pe):
            pe.wait_ge(s_const, 4)
            pe.wait_ge(s_wd, 1)
            with pe.Fori(0, B // 2) as it:
                for g in range(2):
                    blk = it * 2 + g
                    x = xb[:, g]
                    if first:
                        pe.wait_ge(s_x[g], 16 * (it + 1))
                        pe.wait_ge(d_z, 4 * blk)
                        for k in range(KT):
                            for t in range(4):
                                mm = pe.transpose(bank[k][:, t * P:(t + 1) * P], tok[:, g, t, k * P:(k + 1) * P],
                                                  ident[:, :])
                        mm.then_inc(p_tr, 1)
                    pe.wait_ge(a_x, KT * (blk + 1))
                    if not first:
                        pe.wait_ge(a_ot, 2 * blk)

                    def norm(i):
                        e = LN * blk + i
                        for k in range(KT):
                            mm = pe.matmul(bank[0][:, :], avg[:, :], x[:, k], start=(k == 0), stop=(k == KT - 1))
                        mm.then_inc(p_mean, 1)
                        pe.wait_ge(a_sq, 2 * (e + 1))
                        for k in range(KT):
                            mm = pe.matmul(bank[1][:, :], avg[:, :], sq[:, k], start=(k == 0), stop=(k == KT - 1))
                        mm.then_inc(p_var, 1)
                        pe.wait_ge(a_zh, e + 1)
                        pe.wait_ge(d_zl, 2 * (e + 1))

                    def down(m):
                        q = MT * blk + m
                        pe.wait_ge(g_hl, q + 1)
                        if m == 0:
                            pe.wait_ge(d_y, KT * blk)
                        for part, half in enumerate((hh, hl)):
                            for k in range(KT):
                                mm = pe.matmul(bank[6 + k][:, :], down16[:, m, k * P:(k + 1) * P], half[:, m % 2],
                                               start=(m == 0 and part == 0), stop=(m == MT - 1 and part == 1))
                        mm.then_inc(p_down, 1)

                    norm(0)
                    for m in range(MT):
                        q = MT * blk + m
                        for wt, b0, done in ((gate16, 2, p_gate), (up16, 4, p_up)):
                            if done is p_gate:
                                pe.wait_ge(a_sg, MT * blk + max(m - 1, 0))
                                if first and m == 0:
                                    pe.wait_ge(a_ab, blk)
                                if first and m == 1:
                                    pe.wait_ge(d_b, blk)
                            else:
                                pe.wait_ge(d_h, MT * blk + max(m - 1, 0))
                            n = 0
                            for k in range(KT):
                                for half in (zh, zl):
                                    mm = pe.matmul(bank[b0 + m % 2][:, :], wt[:, k, m * P:(m + 1) * P], half[:, k],
                                                   start=(n == 0), stop=(n == 2 * KT - 1))
                                    n += 1
                            mm.then_inc(done, 1)
                        if m:
                            down(m - 1)
                    down(MT - 1)
                    if first:
                        pe.wait_ge(d_y, KT * (blk + 1))
                        norm(1)
                        n = 0
                        for k in range(KT):
                            for wt, half in ((wabh, zh), (wabh, zl), (wabl, zh)):
                                mm = pe.matmul(bank[2][0:2 * NH, :], wt[:, k, :], half[:, k],
                                               start=(n == 0), stop=(n == 3 * KT - 1))
                                n += 1
                        mm.then_inc(p_ab, 1)
                        pe.wait_ge(a_ab, blk + 1)
                        for c in range(NC):
                            mm = pe.matmul(bank[3][:, c * 2 * NH:(c + 1) * 2 * NH], ab[:, g, c, 1:CX],
                                           ident[0:2 * NH, 0:2 * NH], start=True, stop=True)
                        mm.then_inc(p_abt, 1)
                    else:
                        pe.wait_ge(d_y, KT * (blk + 1))
                        pe.wait_ge(d_xc, KT * (blk + 1))
                        for n in range(2):
                            for t in range(2):
                                for k in range(KT):
                                    mm = pe.transpose(bank[n][:, (t * KT + k) * P:(t * KT + k + 1) * P],
                                                      x[:, k, (2 * n + t) * P:(2 * n + t + 1) * P], ident[:, :])
                            mm.then_inc(p_ot, 1)


def attention_phase(nc, stream, z16, scratch, w):
    with ExitStack() as ctx:
        def sb(name, shape, dt=F32):
            return ctx.enter_context(nc.sbuf_tensor("a_" + name, shape, dt))

        def sem(name):
            return ctx.enter_context(nc.semaphore("a_" + name))

        bank = [ctx.enter_context(nc.psum_tensor(f"a_bank{i}", [P, 512], F32)) for i in range(8)]
        PJ, GRAM, LEV, SOLVE, TURN, OUT, UPD = (0, 1), 2, 3, 4, 5, 6, 7

        def units(b):
            return bank[b][:, :].rearrange("p (u c) -> p u c", u=U)

        ident = sb("ident", [P, P]); ident16 = sb("ident16", [P, P], F16)
        blocks = sb("blocks", [P, P])
        mask0 = sb("mask0", [P, P])
        mask0t = sb("mask0t", [P, P])
        masks = sb("masks", [P, NL, P // 2])
        nhalf = sb("nhalf", [P, U])
        lnw = sb("lnw", [P, 1]); lnb = sb("lnb", [P, 1])
        qb = sb("qb", [P, 2, U, S]); kb = sb("kb", [P, 2, U, S]); vb = sb("vb", [P, 2, U, S])
        gb = sb("gb", [P, U, S])
        w_kqv = sb("w_kqv", [P, KT, 3, D]); w_go = sb("w_go", [P, 2 * KT * D])
        kqv16 = sb("kqv16", [P, 2, KT, 3, D], F16)
        gate16 = sb("gate16", [P, 2, KT * D], F16)
        wo16 = sb("wo16", [P, 2, 2, H], F16)
        prm = sb("prm", [P, 2, 3, TAPS + 1]); prs = sb("prs", [P, 2, 3, TAPS])
        bcol = sb("bcol", [P, 2, NC, U])
        decay = sb("decay", [P, 2, U * CX]); cum = sb("cum", [P, 2, U, CX])
        diag = sb("diag", [P, U, CX]); prod = sb("prod", [P, U * CX])
        at = sb("at", [P, 2, U, C]); mix = sb("mix", [P, 2, U, C]); kdec = sb("kdec", [P, 2, U, D])
        am16 = sb("am16", [P, U, C], F16); t16 = sb("t16", [P, U, C], F16)
        tt16 = sb("tt16", [P, 2, U, C], F16); y16 = sb("y16", [P, NL, U, C], F16)
        kg = sb("kg", [P, U, C]); qg = sb("qg", [P, U, C]); z = sb("z", [P, U, D]); zs = sb("zs", [P, U, D])
        vt = sb("vt", [P, U, D]); rhs = sb("rhs", [P, U, D]); rhs16 = sb("rhs16", [P, U, D], F16)
        wv = sb("wv", [P, U, D]); res16 = sb("res16", [P, U, D], F16)
        bn = sb("bn", [P, U, 6]); mv = sb("mv", [P, U, 2]); var = sb("var", [P, U])
        rstd = sb("rstd", [P, U]); shift = sb("shift", [P, U])
        on = sb("on", [P, U, D]); oa = sb("oa", [P, U, C])
        oh = sb("oh", [P, U, C], F16); ol = sb("ol", [P, U, C], F16)

        names = dict(
            dma="const kqv go prm0 prm1 bcol0 bcol1 decay0 decay1 cum0 cum1",
            pe="gram kt l0 y t vt kz w0 aw tr o z ot wo pj",
            dve="scan at mix kdec t0 y rhs res w z bn mv var shift out tap conv prs",
            act="vt rhs16 w0 t tt on oa oh acc silu gate w64 wh go64 goh",
            pool="const ready diag am tt kg qg zs z0 rhs rstd og ol wl gol",
        )
        sems = {f"{e}_{n}": sem(f"{e}_{n}") for e, v in names.items() for n in v.split()}

        class M:
            pass
        m = sems

        a_rows, g_rows, b_cols, _ = scratch
        z_in = z16
        xs = [stream[:, k].rearrange("p (j g s) -> p g j s", j=U, g=G) for k in range(KT)]

        def tile_done(n, c, j):
            if c == 0:
                return m["act_gate"], 4 * n + j + 1
            return m["dve_conv"], 12 * n + 12 + 4 * (c - 1) + j + 1

        def bank_free(n, c, j):
            if j >= 2:
                return tile_done(n, c, j - 2)
            if c > 0:
                return tile_done(n, c - 1, j + 2)
            return m["dve_conv"], 12 * n + 8 + j + 3

        block = ctx.enter_context(nc.Block())
        heads = {k: w[k].rearrange("(k p) (h d) -> h p k d", p=P, d=D) for k in ("Wq", "Wk", "Wv", "Wg")}
        wo_h = w["Wo"].rearrange("(h p) n -> h p n", p=P)
        cw_h = {k: w[k].rearrange("(h p) t -> h p t", p=P) for k in ("kcw", "qcw", "vcw")}
        cb_h = {k: w[k].rearrange("(h p o) -> h p o", p=P, o=1) for k in ("kcb", "qcb", "vcb")}

        def one(ap, h):
            if isinstance(h, int):
                return ap[h]
            return ap[bass.ds(h, 1)].rearrange("o p ... -> (o p) ...")

        def pick(ap, h):
            if isinstance(h, int):
                return ap[h]
            v = ap[bass.ds(h, 1)]
            return v.rearrange("o p k d -> (o p) k d") if len(v.shape) == 4 else v.rearrange("o p d -> (o p) d")

        def over_heads(body):
            body(0, True, False)
            return body

        @block.sync
        def _(sp):
            def load_kqv(h, n):
                need(sp, m["pool_wl"], n)
                for i, k in enumerate(("Wk", "Wq", "Wv")):
                    sp.dma_start(w_kqv[:, :, i], pick(heads[k], h)).then_inc(m["dma_kqv"], 16)

            def load_go(h, n):
                need(sp, m["pool_gol"], n)
                sp.dma_start(w_go[:, 0:KT * D].rearrange("p (k d) -> p k d", k=KT), pick(heads["Wg"], h))\
                    .then_inc(m["dma_go"], 16)
                sp.dma_start(w_go[:, KT * D:], pick(wo_h, h)).then_inc(m["dma_go"], 16)

            def load_prm(h, par, n):
                need(sp, m["act_silu"], 12 * (n - 1))
                for i, k in enumerate("kqv"):
                    sp.dma_start(prm[:, par, i, 0:TAPS], pick(cw_h[k + "cw"], h)).then_inc(m[f"dma_prm{par}"], 16)
                    sp.dma_start(prm[:, par, i, TAPS:], pick(cb_h[k + "cb"], h)).then_inc(m[f"dma_prm{par}"], 16)

            def load_bcol(h, par, n):
                need(sp, m["pool_diag"], 4 * (n - 1))
                if isinstance(h, int):
                    src = b_cols[:, (G * h + par) * NC * U:(G * h + par + 1) * NC * U]
                else:
                    src = b_cols.rearrange("p (h r) -> p h r", h=NH)[:, bass.ds(h, 1), par * NC * U:(par + 1) * NC * U]\
                        .rearrange("p o r -> p (o r)")
                sp.dma_start(bcol[:, par].rearrange("p c u -> p (c u)"), src).then_inc(m[f"dma_bcol{par}"], 16)

            def load_decay(t, par):
                need(sp, m["dve_scan"], t - 1)
                need(sp, m["pool_zs"], t - 1)
                need(sp, m["pool_kg"], t - 1)
                need(sp, m["pool_qg"], t - 1)
                rows = [r[t:t + 1] if isinstance(t, int) else r[bass.ds(t, 1)] for r in (a_rows, g_rows)]
                sp.dma_start(decay[:, par], rows[0].broadcast_to([P, U * CX])).then_inc(m[f"dma_decay{par}"], 16)
                sp.dma_start(cum[:, par].rearrange("p u x -> p (u x)"),
                             rows[1].broadcast_to([P, U * CX])).then_inc(m[f"dma_cum{par}"], 16)

            sp.dma_start(lnw[:, :], w["ln_w"].rearrange("(p o) -> p o", o=1)).then_inc(m["dma_const"], 16)
            sp.dma_start(lnb[:, :], w["ln_b"].rearrange("(p o) -> p o", o=1)).then_inc(m["dma_const"], 16)
            load_kqv(0, 0)
            load_prm(0, 0, 0)
            load_bcol(0, 0, 0)
            load_decay(0, 0)
            load_go(0, 0)
            load_prm(0, 1, 1)
            load_bcol(0, 1, 1)
            load_decay(1, 1)
            load_kqv(0, 1)
            load_go(0, 1)

            def body(h, last):
                for g in range(G):
                    n = G * h + g
                    for c in range(NC):
                        t = NC * n + c
                        if not (last and g == 1 and c >= NC - 2):
                            load_decay(t + 2, c % 2)
                        if last:
                            continue
                        if c == 1:
                            load_kqv(h + 1, n + 2)
                            load_prm(h + 1, g, n + 2)
                        if c == 2:
                            load_go(h + 1, n + 2)
                        if c == 3:
                            load_bcol(h + 1, g, n + 2)

            body(0, False)
            with sp.Fori(1, NH - 1) as h:
                body(h, False)
            body(NH - 1, True)

        @block.gpsimd
        def _(pool):
            nm = [0]

            def chain(ins):
                nm[0] += 1
                ins.then_inc(m["pool_const"], 1)
                pool.wait_ge(m["pool_const"], nm[0])

            def fill(out, value, test, base, pattern, mult):
                chain(nc.gpsimd.affine_select(out=out, in_=out, compare_op=test, fill=value, base=base,
                                              pattern=pattern, channel_multiplier=mult))

            chain(nc.gpsimd.memset(ident[:, :], 0.0))
            fill(ident[:, :], 1.0, ALU.not_equal, 0, [[-1, P]], 1)
            chain(nc.gpsimd.tensor_copy(ident16[:, :], ident[:, :]))
            chain(nc.gpsimd.memset(diag[:, :, :], 0.0))
            chain(nc.gpsimd.memset(y16[:, :, :, :], 0.0))
            for li, mb in enumerate([1] + LEVELS):
                nb = P // (2 * mb)
                blk = blocks[:, :].rearrange("p (b two m) -> p b two m", two=2, m=mb)[:, :, 0, :]
                chain(nc.gpsimd.memset(blocks[:, :], 0.0))
                chain(nc.gpsimd.memset(blk, -1.0))
                fill(blk, 0.0, ALU.is_ge, -mb, [[-2 * mb, nb], [0, mb]], 1)
                fill(blk, 0.0, ALU.is_ge, 2 * mb - 1, [[2 * mb, nb], [0, mb]], -1)
                fill(blocks[:, :], -1.0, ALU.not_equal, 0, [[-1, P]], 1)
                if li == 0:
                    chain(nc.gpsimd.tensor_copy(mask0[:, :], blocks[:, :]))
                    tb = mask0t[:, :].rearrange("p (b two) -> p b two", two=2)
                    chain(nc.gpsimd.memset(mask0t[:, :], 0.0))
                    chain(nc.gpsimd.memset(tb[:, :, 1], -1.0))
                    fill(tb[:, :, 1], 0.0, ALU.is_equal, 0, [[-2, nb]], 1)
                    fill(mask0t[:, :], -1.0, ALU.not_equal, 0, [[-1, P]], 1)
                else:
                    chain(nc.gpsimd.tensor_copy(masks[:, li - 1].rearrange("p (b m) -> p b m", m=mb), blk))
                    for u in range(U):
                        chain(nc.gpsimd.tensor_copy(halves(y16[:, li - 1, u], mb, 1), halves(ident[:, :], mb, 1)))

            nc.gpsimd.memset(nhalf[:, :], -0.5).then_inc(m["pool_ready"], 1)

            def bc(ap, n):
                return ap.rearrange("p (u o) -> p u o", o=1).broadcast_to([P, U, n])

            def all_units(ap):
                return ap.rearrange("p (o c) -> p o c", o=1).broadcast_to([P, U, C])

            def inv(t, h, g, c):
                pool.wait_ge(m[f"dma_bcol{g}"], 16 * (h + 1))
                need(pool, m["dve_scan"], t)
                nc.gpsimd.tensor_tensor(diag[:, :, 1:CX], all_units(ident[:, :]), bc(bcol[:, g, c], C),
                                        ALU.mult).then_inc(m["pool_diag"], 1)

            def inv2(t, par):
                pool.wait_ge(m["dve_at"], t + 1)
                need(pool, m["pe_y"], NL * t)
                need(pool, m["pool_tt"], t)
                nc.gpsimd.tensor_tensor(am16[:, :, :], at[:, par], all_units(ident[:, :]),
                                        ALU.subtract).then_inc(m["pool_am"], 1)
                pool.wait_ge(m["pool_am"], t + 1)
                need(pool, m["pe_tr"], t - 1)
                nc.gpsimd.tensor_tensor(tt16[:, par], am16[:, :, :], all_units(mask0t[:, :]),
                                        ALU.mult).then_inc(m["pool_tt"], 1)

            def seq1(s, par, g, c, n):
                pool.wait_ge(m[f"dma_cum{par}"], 16 * (2 * n + c // 2 + 1))
                pool.wait_ge(m["act_silu"], (s - c) * 3 + 8)
                need(pool, m["pe_kz"], s)
                if c == 0:
                    need(pool, m["dve_z"], s)
                    need(pool, m["pe_o"], s)
                cols = slice(c * C, (c + 1) * C)
                nc.gpsimd.tensor_tensor(kg[:, :, :], kb[:, g, :, cols], cum[:, par, :, 0:C],
                                        ALU.mult).then_inc(m["pool_kg"], 1)
                if c == 0:
                    nc.gpsimd.memset(z[:, :, :], 0.0).then_inc(m["pool_z0"], 1)
                    nc.gpsimd.memset(zs[:, :, :], 0.0).then_inc(m["pool_zs"], 1)
                else:
                    need(pool, m["dve_z"], s)
                    need(pool, m["pe_o"], s)
                    nc.gpsimd.tensor_tensor(zs[:, :, :], z[:, :, :], bc(cum[:, par, :, C], D),
                                            ALU.mult).then_inc(m["pool_zs"], 1)
                nc.gpsimd.tensor_tensor(qg[:, :, :], qb[:, g, :, cols], cum[:, par, :, 1:CX],
                                        ALU.mult).then_inc(m["pool_qg"], 1)

            def seq2(s):
                pool.wait_ge(m["act_w0"], s + 1)
                pool.wait_ge(m["act_rhs16"], s + 1)
                nc.gpsimd.tensor_tensor(rhs[:, :, :], rhs[:, :, :], wv[:, :, :],
                                        ALU.subtract).then_inc(m["pool_rhs"], 1)

            def seq3(s):
                pool.wait_ge(m["dve_var"], s + 1)
                need(pool, m["act_on"], s)
                nc.gpsimd.tensor_tensor(rstd[:, :], var[:, :], nhalf[:, :], ALU.pow).then_inc(m["pool_rstd"], 1)

            def out1(s, g, c):
                pool.wait_ge(m["act_oa"], s + 1)
                pool.wait_ge(m["act_gate"], (s - c) + 4)
                nc.gpsimd.tensor_tensor(oa[:, :, :], oa[:, :, :], gb[:, :, c * C:(c + 1) * C],
                                        ALU.mult).then_inc(m["pool_og"], 1)

            def out2(s):
                pool.wait_ge(m["act_oh"], s + 1)
                nc.gpsimd.tensor_tensor(ol[:, :, :], oa[:, :, :], oh[:, :, :],
                                        ALU.subtract).then_inc(m["pool_ol"], 1)

            def split_kqv(n):
                pool.wait_ge(m["act_wh"], n + 1)
                nc.gpsimd.tensor_tensor(kqv16[:, 1], w_kqv[:, :, :, :], kqv16[:, 0],
                                        ALU.subtract).then_inc(m["pool_wl"], 1)

            def split_go(n, par):
                pool.wait_ge(m["act_goh"], 2 * (n + 1))
                nc.gpsimd.tensor_tensor(gate16[:, 1], w_go[:, 0:KT * D], gate16[:, 0], ALU.subtract)
                nc.gpsimd.tensor_tensor(wo16[:, par, 1], w_go[:, KT * D:], wo16[:, par, 0],
                                        ALU.subtract).then_inc(m["pool_gol"], 1)

            split_kqv(0)
            split_go(0, 0)
            inv(0, 0, 0, 0)
            inv2(0, 0)

            def body(h, first, last):
                for g in range(G):
                    n = G * h + g
                    for c in range(NC):
                        s = NC * n + c
                        more = not (last and g == G - 1 and c == NC - 1)
                        nextg, nextc = (g, c + 1) if c < NC - 1 else (1 - g, 0)
                        prev = not (first and g == 0 and c == 0)
                        pg, pc = (g, c - 1) if c else (1 - g, NC - 1)
                        seq1(s, c % 2, g, c, n)
                        if more:
                            inv(s + 1, h + 1 if nextg < g else h, nextg, nextc)
                        if c == 0 and not (last and g == 1):
                            split_kqv(n + 1)
                        if more:
                            inv2(s + 1, (c + 1) % 2)
                        seq2(s)
                        if prev:
                            out1(s - 1, pg, pc)
                            out2(s - 1)
                        if c == 1 and not (last and g == 1):
                            split_go(n + 1, 1 - g)
                        seq3(s)

            body(0, True, False)
            with pool.Fori(1, NH - 1) as h:
                body(h, False, False)
            body(NH - 1, False, True)
            out1(STEPS - 1, G - 1, NC - 1)
            out2(STEPS - 1)

        @block.vector
        def _(dve):
            def inv1(t, par, n, c):
                dve.wait_ge(m["pool_diag"], t + 1)
                dve.wait_ge(m[f"dma_decay{par}"], 16 * (NC // 2 * n + c // 2 + 1))
                need(dve, m["dve_kdec"], t)
                nc.vector.tensor_tensor_scan(prod[:, :], decay[:, par], diag[:, :, :].rearrange("p u x -> p (u x)"),
                                             0.0, ALU.mult, ALU.add).then_inc(m["dve_scan"], 1)

            pr = prod[:, :].rearrange("p (u x) -> p u x", u=U)

            def inv2(t, par):
                dve.wait_ge(m["pe_gram"], 2 * t + 1)
                dve.wait_ge(m["dve_scan"], t + 1)
                need(dve, m["pe_aw"], t - 1)
                nc.vector.tensor_tensor(at[:, par], units(GRAM), pr[:, :, 0:C], ALU.mult).then_inc(m["dve_at"], 1)
                dve.wait_ge(m["pe_gram"], 2 * t + 2)
                need(dve, m["pe_o"], t - 1)
                nc.vector.tensor_tensor(mix[:, par], units(LEV), pr[:, :, 1:CX], ALU.mult).then_inc(m["dve_mix"], 1)

            def inv3(t, par):
                dve.wait_ge(m["pe_kt"], t + 1)
                need(dve, m["pe_z"], t - 1)
                nc.vector.tensor_tensor(kdec[:, par], units(GRAM), pr[:, :, C:CX].broadcast_to([P, U, D]),
                                        ALU.mult).then_inc(m["dve_kdec"], 1)

            def inv4(t):
                dve.wait_ge(m["pe_l0"], t + 1)
                nc.vector.tensor_tensor(t16[:, :, :], units(GRAM),
                                        mask0[:, :].rearrange("p (o c) -> p o c", o=1).broadcast_to([P, U, C]),
                                        ALU.mult).then_inc(m["dve_t0"], 1)

            def level(t, j):
                mb = LEVELS[j]
                nb = P // (2 * mb)
                dve.wait_ge(m["pe_y"], NL * t + j + 1)
                nc.vector.tensor_tensor(
                    even(y16[:, j], mb),
                    bank[GRAM][:, 0:U * C // 2].rearrange("p (u b m) -> p u b m", u=U, m=mb),
                    masks[:, j].rearrange("p (o b m) -> p o b m", o=1, m=mb).broadcast_to([P, U, nb, mb]),
                    ALU.mult).then_inc(m["dve_y"], 1)

            def seq1(s):
                dve.wait_ge(m["pe_kz"], s + 1)
                dve.wait_ge(m["act_vt"], s + 1)
                need(dve, m["act_rhs16"], s)
                need(dve, m["dve_res"], s)
                nc.vector.tensor_tensor(rhs[:, :, :], vt[:, :, :], units(SOLVE), ALU.subtract)\
                    .then_inc(m["dve_rhs"], 1)

            def seq2(s):
                dve.wait_ge(m["pool_rhs"], s + 1)
                dve.wait_ge(m["pe_aw"], s + 1)
                nc.vector.tensor_tensor(res16[:, :, :], rhs[:, :, :], units(SOLVE), ALU.subtract)\
                    .then_inc(m["dve_res"], 1)

            def seq3(s):
                dve.wait_ge(m["pe_tr"], s + 1)
                dve.wait_ge(m["pool_rhs"], s + 1)
                nc.vector.tensor_tensor(wv[:, :, :], wv[:, :, :], units(SOLVE), ALU.add).then_inc(m["dve_w"], 1)

            def seq4(s):
                dve.wait_ge(m["pe_o"], s + 1)
                need(dve, m["dve_mv"], U * s)
                for u in range(U):
                    nc.vector.bn_stats(bn[:, u], bank[OUT][:, u * D:(u + 1) * D]).then_inc(m["dve_bn"], 1)

            def seq5(s):
                dve.wait_ge(m["pe_z"], s + 1)
                dve.wait_ge(m["pool_zs"], s + 1)
                dve.wait_ge(m["dve_bn"], U * (s + 1))
                need(dve, m["dve_shift"], s)
                nc.vector.tensor_tensor(z[:, :, :], zs[:, :, :], units(UPD), ALU.add).then_inc(m["dve_z"], 1)

            def seq6(s):
                for u in range(U):
                    nc.vector.bn_aggr(mv[:, u], bn[:, u]).then_inc(m["dve_mv"], 1)
                dve.wait_ge(m["dve_mv"], U * (s + 1))
                need(dve, m["pool_rstd"], s)
                nc.vector.tensor_scalar(var[:, :], mv[:, :, 1], EPS / D, None, ALU.add).then_inc(m["dve_var"], 1)

            def seq7(s):
                dve.wait_ge(m["pool_rstd"], s + 1)
                need(dve, m["act_on"], s)
                nc.vector.scalar_tensor_tensor(out=shift[:, :], in0=mv[:, :, 0], scalar=-1.0, in1=rstd[:, :],
                                               op0=ALU.mult, op1=ALU.mult).then_inc(m["dve_shift"], 1)

            def out(s, g, c, k):
                dve.wait_ge(m["pe_wo"], 2 * s + k + 1)
                x = xs[k][:, g, :, c * C:(c + 1) * C]
                nc.vector.scalar_tensor_tensor(out=x, in0=units(UPD), scalar=1.0 / WS, in1=x,
                                               op0=ALU.mult, op1=ALU.add).then_inc(m["dve_out"], 1)

            def conv(q, slot, i, j, par):
                dst = (kb, qb, vb)[i][:, par, j]
                dve.wait_ge(m["act_acc"], q + 1)
                for d in range(1, TAPS):
                    if d > 1:
                        dve.wait_ge(m["dve_tap"], 2 * q + d - 1)
                    ins = nc.vector.scalar_tensor_tensor(
                        out=dst[:, d:S], in0=bank[PJ[slot]][:, 0:S - d], scalar=prs[:, par, i, TAPS - 1 - d:TAPS - d],
                        in1=dst[:, d:S], op0=ALU.mult, op1=ALU.add)
                    ins.then_inc(m["dve_tap"] if d < TAPS - 1 else m["dve_conv"], 1)

            def taps(n, par, h):
                dve.wait_ge(m[f"dma_prm{par}"], 96 * (h + 1))
                need(dve, m["dve_conv"], 12 * (n - 1))
                need(dve, m["act_acc"], 12 * (n - 1))
                nc.vector.tensor_scalar(prs[:, par], prm[:, par, :, 0:TAPS], 1.0 / WS, None, ALU.mult)\
                    .then_inc(m["dve_prs"], 1)

            dve.wait_ge(m["pool_ready"], 1)
            taps(0, 0, 0)
            dve.wait_ge(m["dve_prs"], 1)
            for i in range(3):
                for j in range(U):
                    conv(4 * i + j, j % 2, i, j, 0)
            inv1(0, 0, 0, 0)
            inv2(0, 0)
            inv3(0, 0)
            inv4(0)
            for j in range(NL):
                level(0, j)

            def body(h, first, last):
                for g in range(G):
                    n = G * h + g
                    for c in range(NC):
                        s = NC * n + c
                        more = not (last and g == G - 1 and c == NC - 1)
                        prev = not (first and g == 0 and c == 0)
                        proj = c > 0 and not (last and g == G - 1)
                        pg, pc = (g, c - 1) if c else (1 - g, NC - 1)
                        q0 = 12 * n + 12 + 4 * (c - 1)
                        if c == 0 and not (last and g == 1):
                            taps(n + 1, 1 - g, h + g)
                        if c == 1 and proj:
                            dve.wait_ge(m["dve_prs"], n + 2)
                        if more:
                            inv1(s + 1, (c + 1) % 2, n + (c == NC - 1), (c + 1) % NC)
                            inv2(s + 1, (c + 1) % 2)
                        seq1(s)
                        if more:
                            inv3(s + 1, (c + 1) % 2)
                        if proj:
                            conv(q0, 0, c - 1, 0, 1 - g)
                        if more:
                            inv4(s + 1)
                        seq2(s)
                        if more:
                            level(s + 1, 0)
                        if proj:
                            conv(q0 + 1, 1, c - 1, 1, 1 - g)
                        seq3(s)
                        if more:
                            level(s + 1, 1)
                        if prev:
                            out(s - 1, pg, pc, 0)
                        if more:
                            level(s + 1, 2)
                        seq4(s)
                        seq5(s)
                        seq6(s)
                        if proj:
                            conv(q0 + 2, 0, c - 1, 2, 1 - g)
                        if more:
                            level(s + 1, 3)
                        if prev:
                            out(s - 1, pg, pc, 1)
                        seq7(s)
                        if more:
                            level(s + 1, 4)
                        if proj:
                            conv(q0 + 3, 1, c - 1, 3, 1 - g)
                        if more:
                            level(s + 1, 5)

            body(0, True, False)
            with dve.Fori(1, NH - 1) as h:
                body(h, False, False)
            body(NH - 1, False, True)
            for k in range(KT):
                out(STEPS - 1, G - 1, NC - 1, k)
            dve.wait_ge(m["dve_out"], KT * STEPS)

        @block.scalar
        def _(act):
            act.wait_ge(m["dma_const"], 32)

            def split_kqv(n):
                act.wait_ge(m["dma_kqv"], 48 * (n + 1))
                nc.scalar.activation(w_kqv[:, :, :, :], w_kqv[:, :, :, :], ACT.Copy, scale=WS)\
                    .then_inc(m["act_w64"], 1)
                act.wait_ge(m["act_w64"], n + 1)
                need(act, m["pe_pj"], 16 * n + 12 - 4 if False else n_tiles(n))
                nc.scalar.activation(kqv16[:, 0], w_kqv[:, :, :, :], ACT.Copy).then_inc(m["act_wh"], 1)

            def n_tiles(n):
                return 16 * n - 4 if not isinstance(n, int) or n > 0 else 0

            def split_go(n, par):
                act.wait_ge(m["dma_go"], 32 * (n + 1))
                nc.scalar.activation(w_go[:, :], w_go[:, :], ACT.Copy, scale=WS).then_inc(m["act_go64"], 1)
                act.wait_ge(m["act_go64"], n + 1)
                if not isinstance(n, int) or n > 0:
                    act.wait_ge(m["pe_pj"], 16 * n)
                need(act, m["pe_wo"], 2 * NC * (n - 1))
                nc.scalar.activation(gate16[:, 0], w_go[:, 0:KT * D], ACT.Copy).then_inc(m["act_goh"], 1)
                nc.scalar.activation(wo16[:, par, 0], w_go[:, KT * D:], ACT.Copy).then_inc(m["act_goh"], 1)

            def acc(q, npj, slot, i, j, par, n):
                dst = (kb, qb, vb)[i][:, par, j]
                act.wait_ge(m["pe_pj"], npj + 1)
                if j == 0:
                    act.wait_ge(m["dve_prs"], n + 1)
                    used = (("pool_kg", "pe_kt", "pe_gram"), ("pool_qg",), ("pe_vt",))[i]
                    for name in used:
                        need(act, m[name], (2 if name == "pe_gram" else 1) * NC * (n - 1))
                    if i == 1:
                        need(act, m["pe_gram"], 2 * NC * (n - 1))
                nc.scalar.activation(dst, bank[PJ[slot]][:, :], ACT.Identity, bias=prm[:, par, i, TAPS:],
                                     scale=prs[:, par, i, TAPS - 1:TAPS]).then_inc(m["act_acc"], 1)

            def silu(q, i, j, par):
                dst = (kb, qb, vb)[i][:, par, j]
                act.wait_ge(m["dve_conv"], q + 1)
                nc.scalar.activation(dst, dst, ACT.Silu).then_inc(m["act_silu"], 1)

            def gate(s, j, npj):
                act.wait_ge(m["pe_pj"], npj + 1)
                if j == 0:
                    need(act, m["pool_og"], s)
                nc.scalar.activation(gb[:, j], bank[PJ[j % 2]][:, :], ACT.Sigmoid, scale=1.0 / WS)\
                    .then_inc(m["act_gate"], 1)

            def level(t, j, par):
                mb = LEVELS[j]
                act.wait_ge(m["pe_t"], NL * t + j + 1)
                half = U * C // 2
                if j < NL - 1:
                    nc.scalar.activation(even(t16[:, :, :], mb),
                                         bank[LEV][:, 0:half].rearrange("p (u b m) -> p u b m", u=U, m=mb),
                                         ACT.Copy).then_inc(m["act_t"], 1)
                nc.scalar.activation(odd(tt16[:, par], mb),
                                     bank[LEV][:, half:].rearrange("p (u b m) -> p u b m", u=U, m=mb),
                                     ACT.Copy).then_inc(m["act_tt"], 1)

            def seq1(s):
                act.wait_ge(m["pe_vt"], s + 1)
                need(act, m["dve_rhs"], s)
                nc.scalar.activation(vt[:, :, :], units(TURN), ACT.Copy).then_inc(m["act_vt"], 1)

            def seq2(s):
                act.wait_ge(m["dve_rhs"], s + 1)
                need(act, m["pe_w0"], s)
                nc.scalar.activation(rhs16[:, :, :], rhs[:, :, :], ACT.Copy).then_inc(m["act_rhs16"], 1)

            def seq3(s):
                act.wait_ge(m["pe_w0"], s + 1)
                need(act, m["pe_z"], s)
                nc.scalar.activation(wv[:, :, :], units(SOLVE), ACT.Copy).then_inc(m["act_w0"], 1)

            def out1(s):
                act.wait_ge(m["dve_shift"], s + 1)
                need(act, m["pe_ot"], s)
                for u in range(U):
                    ins = nc.scalar.activation(on[:, u], bank[OUT][:, u * D:(u + 1) * D], ACT.Identity,
                                               bias=shift[:, u:u + 1], scale=rstd[:, u:u + 1])
                ins.then_inc(m["act_on"], 1)

            def out2(s):
                act.wait_ge(m["pe_ot"], s + 1)
                need(act, m["pool_ol"], s)
                nc.scalar.activation(oa[:, :, :], units(TURN), ACT.Identity, bias=lnb[:, :], scale=lnw[:, :])\
                    .then_inc(m["act_oa"], 1)

            def out3(s):
                act.wait_ge(m["pool_og"], s + 1)
                need(act, m["pe_wo"], 2 * s)
                nc.scalar.activation(oh[:, :, :], oa[:, :, :], ACT.Copy).then_inc(m["act_oh"], 1)

            split_kqv(0)
            for i in range(3):
                for j in range(U):
                    q = 4 * i + j
                    acc(q, q, j % 2, i, j, 0, 0)
                    silu(q, i, j, 0)
            split_go(0, 0)
            for j in range(NL):
                level(0, j, 0)

            def body(h, first, last):
                for g in range(G):
                    n = G * h + g
                    for c in range(NC):
                        s = NC * n + c
                        more = not (last and g == G - 1 and c == NC - 1)
                        prev = not (first and g == 0 and c == 0)
                        nxt = not (last and g == G - 1)
                        proj = c > 0 and nxt
                        q0 = 12 * n + 12 + 4 * (c - 1)
                        npj = 4 * s + 12
                        par = (c + 1) % 2

                        def tile(j):
                            if proj:
                                acc(q0 + j, npj + j, j % 2, c - 1, j, 1 - g, n + 1)
                            elif c == 0:
                                gate(s, j, npj + j)

                        def fin(j):
                            if proj:
                                silu(q0 + j, c - 1, j, 1 - g)

                        if prev:
                            out1(s - 1)
                        seq1(s)
                        seq2(s)
                        if c == 0 and nxt:
                            split_kqv(n + 1)
                        if c:
                            tile(0)
                        seq3(s)
                        if prev:
                            out2(s - 1)
                        fin(0)
                        if prev:
                            out3(s - 1)
                        if c == 0:
                            tile(0)
                        if more:
                            level(s + 1, 0, par)
                        tile(1)
                        if c == 1 and nxt:
                            split_go(n + 1, 1 - g)
                        if more:
                            level(s + 1, 1, par)
                        fin(1)
                        if more:
                            level(s + 1, 2, par)
                        tile(2)
                        if more:
                            level(s + 1, 3, par)
                        fin(2)
                        if more:
                            level(s + 1, 4, par)
                        tile(3)
                        if more:
                            level(s + 1, 5, par)
                        fin(3)

            body(0, True, False)
            with act.Fori(1, NH - 1) as h:
                body(h, False, False)
            body(NH - 1, False, True)
            out1(STEPS - 1)
            out2(STEPS - 1)
            out3(STEPS - 1)

        @block.tensor
        def _(pe):
            def gram(t, g, c, par):
                pe.wait_ge(m["act_silu"], (t - c) * 3 + 8)
                need(pe, m["dve_y"], NL * t)
                need(pe, m["act_tt"], NL * t)
                cols = slice(c * C, (c + 1) * C)
                for dst, rhs_ in ((GRAM, kb), (LEV, qb)):
                    for u in range(U):
                        mm = pe.matmul(units(dst)[:, u], kb[:, g, u, cols], rhs_[:, g, u, cols], start=True, stop=True)
                    mm.then_inc(m["pe_gram"], 1)

            def k_turn(t, g, c):
                pe.wait_ge(m["dve_at"], t + 1)
                for u in range(U):
                    mm = pe.transpose(units(GRAM)[:, u], kb[:, g, u, c * C:(c + 1) * C], ident[:, :])
                mm.then_inc(m["pe_kt"], 1)

            def level0(t):
                pe.wait_ge(m["pool_am"], t + 1)
                pe.wait_ge(m["dve_kdec"], t + 1)
                for u in range(U):
                    mm = pe.matmul(units(GRAM)[:, u], am16[:, u], ident16[:, :], start=True, stop=True)
                mm.then_inc(m["pe_l0"], 1)

            half = U * C // 2

            def at_half(b, o, u):
                return bank[b][:, o + u * C // 2:o + (u + 1) * C // 2]

            def level_a(t, j):
                mb = LEVELS[j]
                if j == 0:
                    pe.wait_ge(m["dve_t0"], t + 1)
                else:
                    pe.wait_ge(m["act_t"], (NL - 1) * t + j)
                for u in range(U):
                    mm = pe.matmul(at_half(GRAM, 0, u), am16[:, u], halves(t16[:, u], mb, 0), start=True, stop=True)
                mm.then_inc(m["pe_y"], 1)

            def level_b(t, j, par):
                mb = LEVELS[j]
                pe.wait_ge(m["dve_y"], NL * t + j + 1)
                if j == 0:
                    pe.wait_ge(m["pool_tt"], t + 1)
                    pe.wait_ge(m["dve_mix"], t + 1)
                else:
                    pe.wait_ge(m["act_tt"], NL * t + j)
                for u in range(U):
                    if j < NL - 1:
                        pe.matmul(at_half(LEV, 0, u), tt16[:, par, u], halves(y16[:, j, u], mb, 0), start=True, stop=True)
                    mm = pe.matmul(at_half(LEV, half, u), y16[:, j, u], halves(tt16[:, par, u], mb, 1),
                                   start=True, stop=True)
                mm.then_inc(m["pe_t"], 1)

            def seq1(s, g, c):
                pe.wait_ge(m["act_silu"], (s - c) * 3 + 12)
                need(pe, m["act_oa"], s - 1)
                for u in range(U):
                    mm = pe.transpose(units(TURN)[:, u], vb[:, g, u, c * C:(c + 1) * C], ident[:, :])
                mm.then_inc(m["pe_vt"], 1)
                pe.wait_ge(m["pool_kg"], s + 1)
                if c == 0:
                    pe.wait_ge(m["pool_z0"], (s - c) / 4 + 1 if False else zero_count(s, c))
                else:
                    pe.wait_ge(m["dve_z"], s)
                need(pe, m["dve_w"], s)
                for u in range(U):
                    mm = pe.matmul(units(SOLVE)[:, u], kg[:, u], z[:, u], start=True, stop=True)
                mm.then_inc(m["pe_kz"], 1)

            def seq2(s, par):
                pe.wait_ge(m["act_rhs16"], s + 1)
                pe.wait_ge(m["act_tt"], NL * (s + 1))
                for u in range(U):
                    mm = pe.matmul(units(SOLVE)[:, u], tt16[:, par, u], rhs16[:, u], start=True, stop=True)
                mm.then_inc(m["pe_w0"], 1)

            def seq3(s, par):
                pe.wait_ge(m["act_w0"], s + 1)
                for u in range(U):
                    mm = pe.matmul(units(SOLVE)[:, u], at[:, par, u], wv[:, u], start=True, stop=True)
                mm.then_inc(m["pe_aw"], 1)

            def seq4(s, par):
                pe.wait_ge(m["dve_res"], s + 1)
                for u in range(U):
                    mm = pe.matmul(units(SOLVE)[:, u], tt16[:, par, u], res16[:, u], start=True, stop=True)
                mm.then_inc(m["pe_tr"], 1)

            def seq5(s, par):
                pe.wait_ge(m["dve_w"], s + 1)
                pe.wait_ge(m["pool_qg"], s + 1)
                need(pe, m["act_on"], s)
                need(pe, m["dve_bn"], U * s)
                for u in range(U):
                    pe.matmul(units(OUT)[:, u], qg[:, u], z[:, u], start=True, stop=False)
                    mm = pe.matmul(units(OUT)[:, u], mix[:, par, u], wv[:, u], start=False, stop=True)
                mm.then_inc(m["pe_o"], 1)
                need(pe, m["dve_out"], 2 * s - 1)
                for u in range(U):
                    mm = pe.matmul(units(UPD)[:, u], kdec[:, par, u], wv[:, u], start=True, stop=True)
                mm.then_inc(m["pe_z"], 1)

            def out1(s):
                pe.wait_ge(m["act_on"], s + 1)
                need(pe, m["act_vt"], min_step(s + 2))
                for u in range(U):
                    mm = pe.transpose(units(TURN)[:, u], on[:, u], ident[:, :])
                mm.then_inc(m["pe_ot"], 1)

            def min_step(v):
                return v if not isinstance(v, int) else min(v, STEPS)

            def out2(s, par, k):
                pe.wait_ge(m["pool_ol"], s + 1)
                if k == 0:
                    need(pe, m["dve_out"], 2 * s)
                else:
                    need(pe, m["dve_z"], min_step(s + 2))
                    need(pe, m["dve_out"], 2 * s + 1)
                ch = slice(k * P, (k + 1) * P)
                for i, (wh, o) in enumerate(((0, oh), (0, ol), (1, oh))):
                    mm = pe.matmul(bank[UPD][:, :], wo16[:, par, wh, ch], o[:, :, :].rearrange("p u c -> p (u c)"),
                                   start=(i == 0), stop=(i == 2))
                mm.then_inc(m["pe_wo"], 1)

            def zero_count(s, c):
                if isinstance(s, int):
                    return s // NC + 1
                return zeros_at[0]

            zeros_at = [None]

            def project(i, g, j, slot, part):
                cols = slice((G * j + g) * S, (G * j + g + 1) * S)
                terms = [(wh, k, zh) for (wh, zh) in ((0, 0), (0, 1), (1, 0)) for k in range(KT)]
                for x in range(2 * part, 2 * part + 2):
                    wh, k, zh = terms[x]
                    wt = gate16[:, wh, k * D:(k + 1) * D] if i == 3 else kqv16[:, wh, k, i]
                    mm = pe.matmul(bank[PJ[slot]][:, :], wt, z_in[:, zh, k, cols], start=(x == 0), stop=(x == 5))
                if part == 2:
                    mm.then_inc(m["pe_pj"], 1)

            pe.wait_ge(m["pool_ready"], 1)
            pe.wait_ge(m["pool_wl"], 1)
            for i in range(3):
                for j in range(U):
                    need(pe, m["dve_conv"], 4 * i + j - 1)
                    for part in range(3):
                        project(i, 0, j, j % 2, part)
            gram(0, 0, 0, 0)
            k_turn(0, 0, 0)
            level0(0)
            for j in range(NL):
                level_a(0, j)
                level_b(0, j, 0)

            def body(h, first, last):
                for g in range(G):
                    n = G * h + g
                    for c in range(NC):
                        s = NC * n + c
                        zeros_at[0] = n + 1
                        more = not (last and g == G - 1 and c == NC - 1)
                        prev = not (first and g == 0 and c == 0)
                        nxt = not (last and g == G - 1)
                        ng, ncn = (g, c + 1) if c < NC - 1 else (1 - g, 0)
                        pg = g if c else 1 - g
                        par = c % 2
                        pieces = [(j, part) for j in range(U) for part in range(3)]
                        if c == 0:
                            pe.wait_ge(m["pool_gol"], n + 1)
                        elif c == 1 and nxt:
                            pe.wait_ge(m["pool_wl"], n + 2)

                        def fill(count):
                            if c > 0 and not nxt:
                                return
                            for _ in range(count):
                                if not pieces:
                                    return
                                j, part = pieces.pop(0)
                                if part == 0:
                                    pe.wait_ge(*bank_free(n, c, j))
                                if c == 0:
                                    project(3, g, j, j % 2, part)
                                else:
                                    project(c - 1, 1 - g, j, j % 2, part)

                        if more:
                            gram(s + 1, ng, ncn, 1 - par)
                        seq1(s, g, c)
                        fill(1)
                        if more:
                            k_turn(s + 1, ng, ncn)
                        fill(1)
                        seq2(s, par)
                        fill(1)
                        if more:
                            level0(s + 1)
                        if prev:
                            out1(s - 1)
                        seq3(s, par)
                        if more:
                            level_a(s + 1, 0)
                        fill(1)
                        if more:
                            level_b(s + 1, 0, 1 - par)
                        seq4(s, par)
                        fill(1)
                        if more:
                            level_a(s + 1, 1)
                        fill(1)
                        if prev:
                            out2(s - 1, pg, 0)
                        if more:
                            level_b(s + 1, 1, 1 - par)
                        fill(1)
                        if more:
                            level_a(s + 1, 2)
                        seq5(s, par)
                        if more:
                            level_b(s + 1, 2, 1 - par)
                        fill(1)
                        if more:
                            level_a(s + 1, 3)
                        fill(1)
                        if more:
                            level_b(s + 1, 3, 1 - par)
                        if prev:
                            out2(s - 1, pg, 1)
                        if more:
                            level_a(s + 1, 4)
                        fill(1)
                        if more:
                            level_b(s + 1, 4, 1 - par)
                        fill(2)
                        if more:
                            level_a(s + 1, 5)
                            level_b(s + 1, 5, 1 - par)

            body(0, True, False)
            with pe.Fori(1, NH - 1) as h:
                body(h, False, False)
            body(NH - 1, False, True)
            out1(STEPS - 1)
            for k in range(KT):
                out2(STEPS - 1, G - 1, k)


def macaron(nc, names, aps, out):
    w = {k.removeprefix("L0_attn_").removeprefix("L0_ffn_"): v for k, v in zip(names, aps)}
    a_rows = nc.dram_tensor("decay_rows", (STEPS, U * CX), F32, kind="Internal").ap()
    g_rows = nc.dram_tensor("cumulative_rows", (STEPS, U * CX), F32, kind="Internal").ap()
    b_cols = nc.dram_tensor("strength_columns", (P, STEPS * U), F32, kind="Internal").ap()
    w_saved = nc.dram_tensor("quantised_weights", (P, 3 * KT * FF), F16, kind="Internal").ap()
    scratch = (a_rows, g_rows, b_cols, w_saved)
    with ExitStack() as ctx:
        stream = ctx.enter_context(nc.sbuf_tensor("stream", [P, KT, B * S], F32))
        with ExitStack() as inner:
            z16 = inner.enter_context(nc.sbuf_tensor("z16", [P, 2, KT, B * S], F16))
            ffn_phase(nc, True, w["x"], None, stream, z16, scratch, w)
            attention_phase(nc, stream, z16, scratch, w)
        ffn_phase(nc, False, None, out, stream, None, scratch, w)


_INS = ["L0_attn_x", "L0_attn_Wq", "L0_attn_Wk", "L0_attn_Wv", "L0_attn_Wa", "L0_attn_ba", "L0_attn_Wb",
        "L0_attn_bb", "L0_attn_Wg", "L0_attn_Wo", "L0_attn_qcw", "L0_attn_qcb", "L0_attn_kcw", "L0_attn_kcb",
        "L0_attn_vcw", "L0_attn_vcb", "L0_attn_ln_w", "L0_attn_ln_b", "L0_ffn_gate_w", "L0_ffn_up_w",
        "L0_ffn_down_w", "L0_ffn_gate_scale", "L0_ffn_up_scale", "L0_ffn_down_scale"]


def kernel(**inputs):
    import concourse.bacc as bacc
    from concourse.bass_utils import run_bass_kernel_spmd

    nc = bacc.Bacc("TRN2", target_bir_lowering=False, num_devices=1)
    arrays, aps = {}, []
    for name in _INS:
        a = np.ascontiguousarray(inputs[name])
        arrays[f"in_{name}"] = a
        aps.append(nc.dram_tensor(f"in_{name}", a.shape, mybir.dt.from_np(a.dtype), kind="ExternalInput").ap())
    out = nc.dram_tensor("out", (B, S, H), F32, kind="ExternalOutput").ap()
    macaron(nc, _INS, aps, out)
    r = run_bass_kernel_spmd(nc, [arrays], core_ids=[0])
    return r.results[0]["out"]
```

```python
from contextlib import ExitStack

import numpy as np

import concourse.bass as bass
from concourse import mybir

F32 = mybir.dt.float32
F16 = mybir.dt.float16
I32 = mybir.dt.int32
ALU = mybir.AluOpType
ACT = mybir.ActivationFunctionType

B, S, H = 8, 512, 256
NH, D, TAPS = 16, 128, 4
FF = 768
P = 128
KT = H // P
MT = FF // P
TT = S // P
HB = 3
C = 128
NC = S // C
G = 2
U = B // G
STEPS = NH * G * NC
SPH = G * NC
WS = 64.0
LEVELS = [2, 4, 8, 16, 32, 64]
NL = len(LEVELS)
EPS = 1e-5
CX = C + 1


def need(eng, sem, value):
    if isinstance(value, int) and value <= 0:
        return
    eng.wait_ge(sem, value)


def even(ap, m):
    return ap.rearrange("p u (b two m) -> p u b two m", two=2, m=m)[:, :, :, 0, :]


def odd(ap, m):
    return ap.rearrange("p u (b two m) -> p u b two m", two=2, m=m)[:, :, :, 1, :]


def halves(ap, m, which):
    return ap.rearrange("p (b two m) -> p b two m", two=2, m=m)[:, :, which, :]


def ffn_phase(nc, first, x_in, y_out, stream, z16, scratch, w):
    with ExitStack() as ctx:
        tag = "f1_" if first else "f3_"

        def sb(name, shape, dt=F32):
            return ctx.enter_context(nc.sbuf_tensor(tag + name, shape, dt))

        def sem(name):
            return ctx.enter_context(nc.semaphore(tag + name))

        bank = [ctx.enter_context(nc.psum_tensor(f"{tag}bank{i}", [P, 512], F32)) for i in range(8)]
        gate_b, up_b, down_b, turn_b = bank[0:2], bank[2:4], bank[4:6], bank[6:8]
        ident = sb("ident", [P, P])
        gs = sb("gs", [P, MT]); us = sb("us", [P, MT]); ds_ = sb("ds", [P, KT]); hds = sb("hds", [P, KT])
        wq16 = sb("wq16", [P, 3 * KT * FF], F16)
        gate16 = wq16[:, 0:KT * FF].rearrange("p (k n) -> p k n", k=KT)
        up16 = wq16[:, KT * FF:2 * KT * FF].rearrange("p (k n) -> p k n", k=KT)
        down16 = wq16[:, 2 * KT * FF:].rearrange("p (m n) -> p m n", m=MT)
        tok = sb("tok", [P, 2, TT, H])
        xin = sb("xin", [P, KT, S])
        res = sb("res", [P, KT, S])
        nhalf = sb("nhalf", [P, TT])
        bn = sb("bn", [P, 2, TT, 6]); mv = sb("mv", [P, 2, TT, 2])
        var = sb("var", [P, 2, TT]); rstd = sb("rstd", [P, 2, TT])
        ztok = sb("ztok", [P, 2, TT, H])
        zh = sb("zh", [P, 2, KT, S], F16); zl = sb("zl", [P, 2, KT, S], F16)
        sg = sb("sg", [P, 2, S]); hid = sb("hid", [P, HB, S])
        hh = sb("hh", [P, HB, S], F16); hl = sb("hl", [P, HB, S], F16)
        if first:
            wraw = sb("wraw", [P, 3 * KT * FF]); wexp = sb("wexp", [P, KT * FF])
            wab = sb("wab", [P, KT, 2 * NH]); wab64 = sb("wab64", [P, KT, 2 * NH])
            wabh = sb("wabh", [P, KT, 2 * NH], F16); wabl = sb("wabl", [P, KT, 2 * NH], F16)
            bab = sb("bab", [2 * NH, 1])
            ab = sb("ab", [2 * NH, 2, NC, CX]); gx = sb("gx", [NH, 2, NC, CX])
            zero = sb("zero", [NH, C])
            bcol = sb("bcol", [P, NH, G, NC, U])

        def for_first(*names):
            return [sem(n) if first else None for n in names]

        def of_norms(name):
            return [sem(name + "0")] + for_first(name + "1")

        s_w = [sem(f"dma_weights{i}") for i in range(3)]; s_small = sem("dma_small")
        s_x = for_first("dma_tokens0", "dma_tokens1"); s_out = [sem("dma_out0"), sem("dma_out1")]
        s_save, s_wd = for_first("dma_saved", "weights_ready")
        s_const = sem("constants"); s_q = sem("quantise_step")
        p_x = sem("pe_x_turned"); p_res = sem("pe_res_turned"); p_z = of_norms("pe_z")
        p_gate = sem("pe_gate"); p_up = sem("pe_up"); p_down = sem("pe_down")
        p_ab, p_abt, a_ab = for_first("pe_ab", "pe_abt", "act_ab")
        a_x = sem("act_x"); a_zh = of_norms("act_zh"); a_ot = sem("act_out")
        a_sg = sem("act_silu"); a_hh = sem("act_hh")
        d_bn = of_norms("dve_stats"); d_mv = of_norms("dve_mean"); d_var = of_norms("dve_var")
        d_z = of_norms("dve_z"); d_zl = of_norms("dve_zl")
        d_h = sem("dve_hidden"); d_y = sem("dve_y"); d_g, d_b = for_first("dve_g", "dve_bcol")
        g_rs = of_norms("pool_rstd"); g_hl = sem("pool_hl")
        n_out = 32 if first else 16

        x_tok = None if x_in is None else x_in.rearrange("b (t p) c -> b p t c", p=P)
        y_tok = None if y_out is None else y_out.rearrange("b (t p) c -> b p t c", p=P)
        a_rows, g_rows, b_cols, w_saved = scratch
        a_to = a_rows.rearrange("(h g c) (j x) -> g j h c x", h=NH, g=G, x=CX)
        g_to = g_rows.rearrange("(h g c) (j x) -> g j h c x", h=NH, g=G, x=CX)

        def block_of(ap, b):
            if isinstance(b, int):
                return ap[:, b * S:(b + 1) * S]
            return ap.rearrange("p (b s) -> p b s", b=B)[:, bass.ds(b, 1), :].rearrange("p o s -> p (o s)")

        def item(ap, b):
            return ap[b:b + 1] if isinstance(b, int) else ap[bass.ds(b, 1)]

        def turns(eng, turn):
            for g in range(G):
                turn(0, g)
            with eng.Fori(1, U - 1) as it:
                for g in range(G):
                    turn(it, g)
            for g in range(G):
                turn(U - 1, g)
            turn(U, 0)

        def around(it, g):
            b = G * it + g
            has_next = not (isinstance(b, int) and b + 1 >= B)
            has_last = not (isinstance(b, int) and b == 0)
            return (b, ((it, 1) if g == 0 else (it + 1, 0)) if has_next else None,
                    ((it - 1, 1) if g == 0 else (it, 0)) if has_last else None,
                    not (isinstance(b, int) and b >= B))

        block = ctx.enter_context(nc.Block())

        @block.sync
        def _(sp):
            def load_tok(pair, g):
                sp.dma_start(tok[:, g], item(x_tok, G * pair + g).rearrange("o p t c -> (o p) t c"))\
                    .then_inc(s_x[g], 16)

            if first:
                load_tok(0, 0)
                for i, (name, rows) in enumerate((("gate_w", KT), ("up_w", KT), ("down_w", MT))):
                    sp.dma_start(wraw[:, i * KT * FF:(i + 1) * KT * FF].rearrange("p (k n) -> p k n", k=rows),
                                 w[name].rearrange("(k p) n -> p k n", p=P)).then_inc(s_w[i], 16)
                    if i == 0:
                        load_tok(0, 1)
                sp.dma_start(wab[:, :, 0:NH], w["Wa"].rearrange("(k p) n -> p k n", p=P)).then_inc(s_small, 16)
                sp.dma_start(wab[:, :, NH:], w["Wb"].rearrange("(k p) n -> p k n", p=P)).then_inc(s_small, 16)
                sp.dma_start(bab[0:NH, :], w["ba"].rearrange("(p o) -> p o", o=1)).then_inc(s_small, 16)
                sp.dma_start(bab[NH:, :], w["bb"].rearrange("(p o) -> p o", o=1)).then_inc(s_small, 16)
            else:
                for i in range(3):
                    cols = slice(i * KT * FF, (i + 1) * KT * FF)
                    sp.dma_start(wq16[:, cols], w_saved[:, cols]).then_inc(s_w[i], 16)
            for dst, name in ((gs, "gate_scale"), (us, "up_scale"), (ds_, "down_scale")):
                sp.dma_start(dst[:, :], w[name].rearrange("(m p) -> p m", p=P),
                             allow_slow_non_contiguous=True).then_inc(s_small, 16)

            def turn(it, g):
                b, nxt, last, cur = around(it, g)
                if first and not (isinstance(b, int) and b + G >= B):
                    sp.wait_ge(p_x, b + 1)
                    sp.wait_ge(d_z[0], b + 1)
                    load_tok(it + 1, g)
                if first and last:
                    sp.wait_ge(a_ab, b)
                    sp.dma_start(item(a_to[last[1]], last[0]).rearrange("o h c x -> (o h) c x"),
                                 ab[0:NH, last[1]]).then_inc(s_out[last[1]], 16)
                    sp.wait_ge(d_g, NC * b)
                    sp.dma_start(item(g_to[last[1]], last[0]).rearrange("o h c x -> (o h) c x"),
                                 gx[:, last[1]]).then_inc(s_out[last[1]], 16)
                if not first and last:
                    sp.wait_ge(a_ot, KT * b)
                    sp.dma_start(item(y_tok, G * last[0] + last[1]).rearrange("o p t c -> (o p) t c"),
                                 tok[:, last[1]]).then_inc(s_out[last[1]], 16)

            turns(sp, turn)
            if first:
                sp.wait_ge(d_b, B)
                sp.dma_start(b_cols, bcol[:, :, :, :, :].rearrange("p h g c j -> p (h g c j)")).then_inc(s_save, 16)
                sp.wait_ge(s_wd, 4)
                sp.dma_start(w_saved, wq16[:, :]).then_inc(s_save, 16)
                sp.wait_ge(s_save, 32)
            for g in range(2):
                sp.wait_ge(s_out[g], n_out * U)

        @block.gpsimd
        def _(pool):
            nc.gpsimd.memset(ident[:, :], 0.0).then_inc(s_const, 1)
            nc.gpsimd.memset(nhalf[:, :], -0.5).then_inc(s_const, 1)
            if first:
                nc.gpsimd.memset(zero[:, :], 0.0)
                nc.gpsimd.memset(ab[:, :, :, :], 0.0)
                nc.gpsimd.memset(gx[:, :, :, :], 1.0).then_inc(s_const, 1)
            else:
                nc.gpsimd.memset(rstd[:, :, :], 0.0).then_inc(s_const, 1)
            pool.wait_ge(s_const, 2)
            nc.gpsimd.affine_select(out=ident[:, :], in_=ident[:, :], compare_op=ALU.not_equal, fill=1.0,
                                    base=0, pattern=[[-1, P]], channel_multiplier=1).then_inc(s_const, 1)

            def root(n, e):
                pool.wait_ge(d_var[n], e + 1)
                need(pool, d_z[n], e)
                nc.gpsimd.tensor_tensor(rstd[:, n], var[:, n], nhalf[:, :], ALU.pow).then_inc(g_rs[n], 1)

            def low(b, m):
                q = MT * b + m
                pool.wait_ge(a_hh, q + 1)
                need(pool, p_down, q - HB + 1)
                nc.gpsimd.tensor_tensor(hl[:, m % HB], hid[:, m % HB], hh[:, m % HB],
                                        ALU.subtract).then_inc(g_hl, 1)

            def turn(it, g):
                b, nxt, last, cur = around(it, g)
                for m in range(MT):
                    if m == 1 and nxt:
                        root(0, b + 1)
                    if m == 3 and first and last:
                        root(1, b - 1)
                    if cur:
                        low(b, m)

            root(0, 0)
            turns(pool, turn)

        @block.vector
        def _(dve):
            qn = [0]

            def chain(ins):
                qn[0] += 1
                ins.then_inc(s_q, 1)
                dve.wait_ge(s_q, qn[0])

            def stats(n, e, g):
                if n == 0 and first:
                    pair = (e - g) // G if isinstance(e, int) else None
                    src = [tok[:, g, t] for t in range(TT)]
                else:
                    dve.wait_ge(p_res if n else p_x, e + 1)
                    src = [turn_b[t // 2][:, t % 2 * H:(t % 2 + 1) * H] for t in range(TT)]
                need(dve, d_mv[n], TT * e)
                for t in range(TT):
                    nc.vector.bn_stats(bn[:, n, t], src[t]).then_inc(d_bn[n], 1)

            def variance(n, e):
                for t in range(TT):
                    nc.vector.bn_aggr(mv[:, n, t], bn[:, n, t]).then_inc(d_mv[n], 1)
                dve.wait_ge(d_mv[n], TT * (e + 1))
                need(dve, g_rs[n], e)
                nc.vector.tensor_scalar(var[:, n], mv[:, n, :, 1], EPS, None, ALU.add).then_inc(d_var[n], 1)

            def normed(n, e, g):
                dve.wait_ge(g_rs[n], e + 1)
                need(dve, p_z[n], e)
                for t in range(TT):
                    if n == 0 and first:
                        src = tok[:, g, t]
                    else:
                        src = turn_b[t // 2][:, t % 2 * H:(t % 2 + 1) * H]
                    ins = nc.vector.tensor_scalar(ztok[:, n, t], src, mv[:, n, t, 0:1], rstd[:, n, t:t + 1],
                                                  ALU.subtract, ALU.mult)
                ins.then_inc(d_z[n], 1)

            def low(n, e, g):
                dve.wait_ge(a_zh[n], KT * (e + 1))
                for k in range(KT):
                    if n == 0:
                        hi, lo = zh[:, g, k], zl[:, g, k]
                    else:
                        hi, lo = block_of(z16[:, 0, k], e), block_of(z16[:, 1, k], e)
                    nc.vector.tensor_tensor(lo, turn_b[k][:, :], hi, ALU.subtract).then_inc(d_zl[n], 1)

            def hidden(b, m):
                q = MT * b + m
                dve.wait_ge(p_up, q + 1)
                dve.wait_ge(a_sg, q + 1)
                need(dve, g_hl, q - HB + 1)
                nc.vector.scalar_tensor_tensor(out=hid[:, m % HB], in0=up_b[m % 2][:, :],
                                               scalar=us[:, m:m + 1], in1=sg[:, m % 2],
                                               op0=ALU.mult, op1=ALU.mult).then_inc(d_h, 1)

            def added(e):
                dve.wait_ge(p_down, MT * (e + 1))
                need(dve, p_res, e)
                if first:
                    need(dve, a_ot, KT * e)
                for k in range(KT):
                    nc.vector.scalar_tensor_tensor(out=res[:, k], in0=down_b[k][:, :],
                                                   scalar=hds[:, k:k + 1], in1=block_of(stream[:, k], e),
                                                   op0=ALU.mult, op1=ALU.add).then_inc(d_y, 1)

            def cumulative(e, pair, g):
                dve.wait_ge(a_ab, e + 1)
                need(dve, s_out[g], n_out * pair)
                for c in range(NC):
                    nc.vector.tensor_tensor_scan(gx[:, g, c, 1:CX], ab[0:NH, g, c, 1:CX], zero[:, :],
                                                 1.0, ALU.mult, ALU.add).then_inc(d_g, 1)

            def strengths(e, pair, g):
                dve.wait_ge(p_abt, e + 1)
                dst = bcol[:, :, g, :, pair:pair + 1] if isinstance(pair, int) else bcol[:, :, g, :, bass.ds(pair, 1)]
                nc.vector.tensor_scalar(dst.rearrange("p h c o -> p h (c o)"),
                                        turn_b[1][:, 0:NC * 2 * NH].rearrange("p (c r) -> p r c", c=NC)[:, NH:, :],
                                        1.0 / D, None, ALU.mult).then_inc(d_b, 1)

            def turn(it, g):
                b, nxt, last, cur = around(it, g)

                def hid_tile(m):
                    if cur:
                        hidden(b, m)

                hid_tile(0)
                if nxt:
                    if first:
                        dve.wait_ge(s_x[nxt[1]], 16 * (nxt[0] + 1))
                    stats(0, b + 1, nxt[1])
                    dve.wait_ge(d_bn[0], TT * (b + 2))
                    need(dve, d_z[0], b + 1)
                hid_tile(1)
                if nxt:
                    variance(0, b + 1)
                if last:
                    added(b - 1)
                if nxt:
                    normed(0, b + 1, nxt[1])
                hid_tile(2)
                if nxt:
                    dve.wait_ge(p_z[0], b + 2)
                    low(0, b + 1, nxt[1])
                if first and last:
                    stats(1, b - 1, last[1])
                    dve.wait_ge(d_bn[1], TT * b)
                    need(dve, d_z[1], b - 1)
                hid_tile(3)
                if first and last:
                    variance(1, b - 1)
                    normed(1, b - 1, last[1])
                hid_tile(4)
                if first and last:
                    low(1, b - 1, last[1])
                hid_tile(5)
                if first and last:
                    cumulative(b - 1, *last)
                    strengths(b - 1, *last)

            dve.wait_ge(s_const, 4)
            if first:
                dve.wait_ge(s_x[0], 16)
            stats(0, 0, 0)
            dve.wait_ge(d_bn[0], TT)
            variance(0, 0)
            dve.wait_ge(s_small, 16 * (7 if first else 3))
            chain(nc.vector.tensor_scalar(hds[:, :], ds_[:, :], 0.5, None, ALU.mult))
            normed(0, 0, 0)
            low(0, 0, 0)
            if first:
                for i in range(3):
                    r, q = wraw[:, i * KT * FF:(i + 1) * KT * FF], wq16[:, i * KT * FF:(i + 1) * KT * FF]
                    e = wexp[:, :]
                    dve.wait_ge(s_w[i], 16)
                    chain(nc.vector.tensor_scalar(e.bitcast(I32), r.bitcast(I32), 0x7F800000, None, ALU.bitwise_and))
                    chain(nc.vector.tensor_scalar(e, e, 2.0 ** -6, 1.5 * 2.0 ** 20, ALU.max, ALU.mult))
                    chain(nc.vector.tensor_tensor(r, r, e, ALU.add))
                    chain(nc.vector.tensor_tensor(r, r, e, ALU.subtract))
                    chain(nc.vector.tensor_scalar(e, r, 1.125 * 2.0 ** 119, 0.0, ALU.mult, ALU.mult))
                    nc.vector.tensor_tensor(q, r, e, ALU.add).then_inc(s_wd, 1)
                    dve.wait_ge(s_wd, i + 1)
                chain(nc.vector.tensor_scalar(wab64[:, :, :], wab[:, :, :], WS, None, ALU.mult))
                chain(nc.vector.tensor_copy(wabh[:, :, :], wab64[:, :, :]))
                nc.vector.tensor_tensor(wabl[:, :, :], wab64[:, :, :], wabh[:, :, :], ALU.subtract)\
                    .then_inc(s_wd, 1)
            turns(dve, turn)

        @block.scalar
        def _(act):
            def stream_in(e):
                if first:
                    act.wait_ge(p_x, e + 1)
                else:
                    need(act, p_x, e)
                for k in range(KT):
                    if first:
                        nc.scalar.activation(block_of(stream[:, k], e), turn_b[k][:, :], ACT.Copy).then_inc(a_x, 1)
                    else:
                        nc.scalar.activation(xin[:, k], block_of(stream[:, k], e), ACT.Copy).then_inc(a_x, 1)

            def high(n, e, g):
                act.wait_ge(p_z[n], e + 1)
                if n == 0:
                    need(act, p_up, MT * (e - 1))
                for k in range(KT):
                    dst = block_of(z16[:, 0, k], e) if n else zh[:, g, k]
                    nc.scalar.activation(dst, turn_b[k][:, :], ACT.Copy).then_inc(a_zh[n], 1)

            def silu(b, m):
                q = MT * b + m
                act.wait_ge(p_gate, q + 1)
                need(act, d_h, q - 1)
                nc.scalar.activation(sg[:, m % 2], gate_b[m % 2][:, :], ACT.Silu,
                                     scale=gs[:, m:m + 1]).then_inc(a_sg, 1)

            def hidden_high(b, m):
                q = MT * b + m
                act.wait_ge(d_h, q + 1)
                need(act, p_down, q - HB + 1)
                nc.scalar.activation(hh[:, m % HB], hid[:, m % HB], ACT.Copy).then_inc(a_hh, 1)

            def stream_out(e):
                act.wait_ge(d_y, KT * (e + 1))
                for k in range(KT):
                    nc.scalar.activation(block_of(stream[:, k], e), res[:, k], ACT.Copy).then_inc(a_ot, 1)

            def decays(e, pair, g):
                act.wait_ge(p_ab, e + 1)
                need(act, p_abt, e - 1)
                need(act, s_out[g], n_out * pair)
                nc.scalar.activation(ab[:, g, :, 1:CX], turn_b[0][0:2 * NH, :].rearrange("p (c x) -> p c x", c=NC),
                                     ACT.Sigmoid, bias=bab[:, :], scale=1.0 / WS).then_inc(a_ab, 1)

            def result(e, pair, g):
                act.wait_ge(p_res, e + 1)
                need(act, s_out[g], n_out * pair)
                for n in range(KT):
                    nc.scalar.activation(tok[:, g, 2 * n:2 * n + 2].rearrange("p t c -> p (t c)"),
                                         turn_b[n][:, :], ACT.Copy).then_inc(a_ot, 1)

            def turn(it, g):
                b, nxt, last, cur = around(it, g)

                def hid_tile(m):
                    if cur:
                        silu(b, m)
                        hidden_high(b, m)

                if first and nxt:
                    stream_in(b + 1)
                hid_tile(0)
                hid_tile(1)
                if cur:
                    silu(b, 2)
                if nxt:
                    high(0, b + 1, nxt[1])
                if cur:
                    hidden_high(b, 2)
                if first and last:
                    stream_out(b - 1)
                hid_tile(3)
                if not first and nxt and not (isinstance(b, int) and b + 2 >= B):
                    stream_in(b + 2)
                hid_tile(4)
                if last:
                    high(1, b - 1, last[1]) if first else result(b - 1, *last)
                hid_tile(5)
                if first and last:
                    decays(b - 1, *last)

            act.wait_ge(s_small, 16 * (7 if first else 3))
            stream_in(0)
            if not first:
                stream_in(1)
            high(0, 0, 0)
            turns(act, turn)

        @block.tensor
        def _(pe):
            def x_turned(e, pair, g):
                if first:
                    pe.wait_ge(s_x[g], 16 * (pair + 1))
                    need(pe, d_b, e - 2)
                    need(pe, a_ab, e - 2)
                else:
                    pe.wait_ge(a_x, KT * (e + 1))
                    need(pe, a_ot, KT * (e - 2))
                for t in range(TT):
                    for k in range(KT):
                        if first:
                            dst, src = turn_b[k][:, t * P:(t + 1) * P], tok[:, g, t, k * P:(k + 1) * P]
                        else:
                            o = (t % 2 * KT + k) * P
                            dst, src = turn_b[t // 2][:, o:o + P], xin[:, k, t * P:(t + 1) * P]
                        mm = pe.transpose(dst, src, ident[:, :])
                mm.then_inc(p_x, 1)

            def z_turned(n, e):
                pe.wait_ge(d_z[n], e + 1)
                if first and n == 0:
                    pe.wait_ge(a_x, KT * (e + 1))
                for k in range(KT):
                    for t in range(TT):
                        mm = pe.transpose(turn_b[k][:, t * P:(t + 1) * P], ztok[:, n, t, k * P:(k + 1) * P],
                                          ident[:, :])
                mm.then_inc(p_z[n], 1)

            def res_turned(e, nxt):
                pe.wait_ge(d_y, KT * (e + 1))
                if nxt:
                    pe.wait_ge(a_zh[0], KT * (e + 3))
                    pe.wait_ge(d_zl[0], KT * (e + 3))
                for t in range(TT):
                    for k in range(KT):
                        o = (t % 2 * KT + k) * P
                        mm = pe.transpose(turn_b[t // 2][:, o:o + P], res[:, k, t * P:(t + 1) * P], ident[:, :])
                mm.then_inc(p_res, 1)

            def gate(b, m, g):
                q = MT * b + m
                if m == 0:
                    pe.wait_ge(a_zh[0], KT * (b + 1))
                    pe.wait_ge(d_zl[0], KT * (b + 1))
                need(pe, a_sg, q - 1)
                products(gate_b[m % 2], gate16, m, g, p_gate)

            def up(b, m, g):
                need(pe, d_h, MT * b + m - 1)
                products(up_b[m % 2], up16, m, g, p_up)

            def products(dst, wt, m, g, done):
                n = 0
                for half in (zh, zl):
                    for k in range(KT):
                        mm = pe.matmul(dst[:, :], wt[:, k, m * P:(m + 1) * P], half[:, g, k],
                                       start=(n == 0), stop=(n == 2 * KT - 1))
                        n += 1
                mm.then_inc(done, 1)

            def down(b, m):
                q = MT * b + m
                pe.wait_ge(g_hl, q + 1)
                if m == 0:
                    need(pe, d_y, KT * b)
                for part, half in enumerate((hh, hl)):
                    for k in range(KT):
                        mm = pe.matmul(down_b[k][:, :], down16[:, m, k * P:(k + 1) * P], half[:, m % HB],
                                       start=(m == 0 and part == 0), stop=(m == MT - 1 and part == 1))
                mm.then_inc(p_down, 1)

            def decay_products(e):
                pe.wait_ge(a_zh[1], KT * (e + 1))
                pe.wait_ge(d_zl[1], KT * (e + 1))
                n = 0
                for k in range(KT):
                    for wt, half in ((wabh, 0), (wabh, 1), (wabl, 0)):
                        mm = pe.matmul(turn_b[0][0:2 * NH, :], wt[:, k, :], block_of(z16[:, half, k], e),
                                       start=(n == 0), stop=(n == 3 * KT - 1))
                        n += 1
                mm.then_inc(p_ab, 1)

            def strengths_turned(e, g):
                pe.wait_ge(a_ab, e + 1)
                for c in range(NC):
                    mm = pe.matmul(turn_b[1][:, c * 2 * NH:(c + 1) * 2 * NH], ab[:, g, c, 1:CX],
                                   ident[0:2 * NH, 0:2 * NH], start=True, stop=True)
                mm.then_inc(p_abt, 1)

            def turn(it, g):
                b, nxt, last, cur = around(it, g)
                start = isinstance(b, int) and b == 0
                for m in range(MT):
                    if cur:
                        if start and m == 0:
                            pe.wait_ge(*((s_wd, 1) if first else (s_w[0], 16)))
                        gate(b, m, g)
                    if m == 0 and nxt:
                        x_turned(b + 1, *nxt)
                    if m == 2 and nxt:
                        z_turned(0, b + 1)
                    if cur:
                        if start and m == 0:
                            pe.wait_ge(*((s_wd, 2) if first else (s_w[1], 16)))
                        up(b, m, g)
                    if first and m == 5 and last:
                        decay_products(b - 1)
                    if m < 2 and last:
                        down(b - 1, m + MT - 2)
                    if m >= 2 and cur:
                        if start and m == 2:
                            pe.wait_ge(*((s_wd, 4) if first else (s_w[2], 16)))
                        down(b, m - 2)
                    if last:
                        if m == 2:
                            res_turned(b - 1, nxt)
                        if m == 4 and first:
                            z_turned(1, b - 1)
                        if m == 5 and first:
                            strengths_turned(b - 1, last[1])

            pe.wait_ge(s_const, 4)
            x_turned(0, 0, 0)
            z_turned(0, 0)
            turns(pe, turn)


def attention_phase(nc, stream, z16, scratch, w):
    with ExitStack() as ctx:
        def sb(name, shape, dt=F32):
            return ctx.enter_context(nc.sbuf_tensor("a_" + name, shape, dt))

        def sem(name):
            return ctx.enter_context(nc.semaphore("a_" + name))

        bank = [ctx.enter_context(nc.psum_tensor(f"a_bank{i}", [P, 512], F32)) for i in range(8)]
        PJ, GRAM, LEV, SOLVE, TURN, OUT, UPD = (0, 1), 2, 3, 4, 5, 6, 7

        def units(b):
            return bank[b][:, :].rearrange("p (u c) -> p u c", u=U)

        ident = sb("ident", [P, P]); ident16 = sb("ident16", [P, P], F16)
        blocks = sb("blocks", [P, P])
        mask0 = sb("mask0", [P, P])
        mask0t = sb("mask0t", [P, P])
        masks = sb("masks", [P, NL, P // 2])
        nhalf = sb("nhalf", [P, U])
        lnw = sb("lnw", [P, 1]); lnb = sb("lnb", [P, 1])
        qb = sb("qb", [P, 2, U, S]); kb = sb("kb", [P, 2, U, S]); vb = sb("vb", [P, 2, U, S])
        gb = sb("gb", [P, 2, U, S])
        w_kqv = sb("w_kqv", [P, KT, 3, D]); w_go = sb("w_go", [P, 2 * KT * D])
        kqv16 = sb("kqv16", [P, 2, KT, 3, D], F16)
        gate16 = sb("gate16", [P, 2, KT * D], F16)
        wo16 = sb("wo16", [P, 2, 2, H], F16)
        prm = sb("prm", [P, 2, 3, TAPS + 1]); prs = sb("prs", [P, 2, 3, TAPS])
        bcol = sb("bcol", [P, 2, NC, U])
        decay = sb("decay", [P, 2, U * CX]); cum = sb("cum", [P, 2, U, CX])
        diag = sb("diag", [P, U, CX]); prod = sb("prod", [P, U * CX])
        at = sb("at", [P, 2, U, C]); mix = sb("mix", [P, 2, U, C]); kdec = sb("kdec", [P, 2, U, D])
        am16 = sb("am16", [P, U, C], F16); t16 = sb("t16", [P, U, C], F16)
        tt16 = sb("tt16", [P, 2, U, C], F16); y16 = sb("y16", [P, NL, U, C], F16)
        kg = sb("kg", [P, U, C]); qg = sb("qg", [P, U, C]); z = sb("z", [P, U, D]); zs = sb("zs", [P, U, D])
        vt = sb("vt", [P, U, D]); rhs = sb("rhs", [P, U, D]); rhs16 = sb("rhs16", [P, U, D], F16)
        wv = sb("wv", [P, U, D]); res16 = sb("res16", [P, U, D], F16)
        bn = sb("bn", [P, U, 6]); mv = sb("mv", [P, U, 2]); var = sb("var", [P, U])
        rstd = sb("rstd", [P, U]); shift = sb("shift", [P, U])
        on = sb("on", [P, U, D]); oa = sb("oa", [P, U, C])
        oh = sb("oh", [P, U, C], F16); ol = sb("ol", [P, U, C], F16)

        names = dict(
            dma="const kqv go prm0 prm1 bcol0 bcol1 decay0 decay1 cum0 cum1",
            pe="gram kt l0 y t vt kz w0 aw tr o z ot wo pj",
            dve="scan at mix y rhs res w z bn mv var shift out tap conv prs",
            act="vt rhs16 w0 kdec t0 t tt on oa oh acc silu gate w64 wh go64 goh",
            pool="const ready diag am tt atp kg qg zs rstd og ol wl gol",
        )
        m = {f"{e}_{n}": sem(f"{e}_{n}") for e, v in names.items() for n in v.split()}

        a_rows, g_rows, b_cols, _ = scratch
        z_in = z16
        xs = [stream[:, k].rearrange("p (j g s) -> p g j s", j=U, g=G) for k in range(KT)]

        def nz(n, c):
            return (NC - 1) * n + max(c - 1, 0)

        def later(n, c, k):
            return n + (c + k) // NC, (c + k) % NC

        def tile_done(n, c, j):
            if c == NC - 1:
                return m["act_gate"], U * (n + 1) + j + 1
            return m["dve_conv"], 3 * U * (n + 1) + U * c + j + 1

        def bank_free(n, c, j):
            if j >= 2:
                return tile_done(n, c, j - 2)
            return tile_done(n, c - 1, j + 2) if c else tile_done(n - 1, NC - 1, j + 2)

        block = ctx.enter_context(nc.Block())
        heads = {k: w[k].rearrange("(k p) (h d) -> h p k d", p=P, d=D) for k in ("Wq", "Wk", "Wv", "Wg")}
        wo_h = w["Wo"].rearrange("(h p) n -> h p n", p=P)
        cw_h = {k: w[k].rearrange("(h p) t -> h p t", p=P) for k in ("kcw", "qcw", "vcw")}
        cb_h = {k: w[k].rearrange("(h p o) -> h p o", p=P, o=1) for k in ("kcb", "qcb", "vcb")}

        def pick(ap, h):
            if isinstance(h, int):
                return ap[h]
            v = ap[bass.ds(h, 1)]
            return v.rearrange("o p k d -> (o p) k d") if len(v.shape) == 4 else v.rearrange("o p d -> (o p) d")

        @block.sync
        def _(sp):
            def load_kqv(h, n):
                need(sp, m["pool_wl"], n)
                for i, k in enumerate(("Wk", "Wq", "Wv")):
                    sp.dma_start(w_kqv[:, :, i], pick(heads[k], h)).then_inc(m["dma_kqv"], 16)

            def load_go(h, n):
                need(sp, m["pool_gol"], n)
                sp.dma_start(w_go[:, 0:KT * D].rearrange("p (k d) -> p k d", k=KT), pick(heads["Wg"], h))\
                    .then_inc(m["dma_go"], 16)
                sp.dma_start(w_go[:, KT * D:], pick(wo_h, h)).then_inc(m["dma_go"], 16)

            def load_prm(h, g, n):
                need(sp, m["act_silu"], 3 * U * (n - 1))
                for i, k in enumerate("kqv"):
                    sp.dma_start(prm[:, g, i, 0:TAPS], pick(cw_h[k + "cw"], h)).then_inc(m[f"dma_prm{g}"], 16)
                    sp.dma_start(prm[:, g, i, TAPS:], pick(cb_h[k + "cb"], h)).then_inc(m[f"dma_prm{g}"], 16)

            def load_bcol(h, g, n):
                need(sp, m["pool_diag"], NC * (n - 1))
                if isinstance(h, int):
                    src = b_cols[:, (G * h + g) * NC * U:(G * h + g + 1) * NC * U]
                else:
                    src = b_cols.rearrange("p (h r) -> p h r", h=NH)[:, bass.ds(h, 1), g * NC * U:(g + 1) * NC * U]\
                        .rearrange("p o r -> p (o r)")
                sp.dma_start(bcol[:, g].rearrange("p c u -> p (c u)"), src).then_inc(m[f"dma_bcol{g}"], 16)

            def load_decay(n, c):
                t, par = NC * n + c, c % 2
                rows = [r[t:t + 1] if isinstance(t, int) else r[bass.ds(t, 1)] for r in (a_rows, g_rows)]
                need(sp, m["dve_scan"], t - 1)
                need(sp, m["dve_z"], t - 1)
                sp.dma_start(decay[:, par], rows[0].broadcast_to([P, U * CX])).then_inc(m[f"dma_decay{par}"], 16)
                sp.dma_start(cum[:, par].rearrange("p u x -> p (u x)"),
                             rows[1].broadcast_to([P, U * CX])).then_inc(m[f"dma_cum{par}"], 16)

            sp.dma_start(lnw[:, :], w["ln_w"].rearrange("(p o) -> p o", o=1)).then_inc(m["dma_const"], 16)
            sp.dma_start(lnb[:, :], w["ln_b"].rearrange("(p o) -> p o", o=1)).then_inc(m["dma_const"], 16)
            load_kqv(0, 0)
            load_prm(0, 0, 0)
            load_go(0, 0)
            load_bcol(0, 0, 0)
            load_decay(0, 0)
            load_prm(0, 1, 1)
            load_bcol(0, 1, 1)
            load_decay(0, 1)
            load_kqv(0, 1)
            load_go(0, 1)

            def body(h, last):
                for g in range(G):
                    n = G * h + g
                    for c in range(NC):
                        if not (last and g == G - 1 and c >= NC - 2):
                            load_decay(*later(n, c, 2))
                        if last:
                            continue
                        if c == 0:
                            load_kqv(h + 1, n + 2)
                        if c == 1:
                            load_prm(h + 1, g, n + 2)
                        if c == 2:
                            load_go(h + 1, n + 2)
                            load_bcol(h + 1, g, n + 2)

            body(0, False)
            with sp.Fori(1, NH - 1) as h:
                body(h, False)
            body(NH - 1, True)

        @block.gpsimd
        def _(pool):
            made = [0]

            def chain(ins):
                made[0] += 1
                ins.then_inc(m["pool_const"], 1)
                pool.wait_ge(m["pool_const"], made[0])

            def fill(out, value, test, base, pattern, mult):
                chain(nc.gpsimd.affine_select(out=out, in_=out, compare_op=test, fill=value, base=base,
                                              pattern=pattern, channel_multiplier=mult))

            chain(nc.gpsimd.memset(ident[:, :], 0.0))
            fill(ident[:, :], 1.0, ALU.not_equal, 0, [[-1, P]], 1)
            chain(nc.gpsimd.tensor_copy(ident16[:, :], ident[:, :]))
            chain(nc.gpsimd.memset(diag[:, :, :], 0.0))
            chain(nc.gpsimd.memset(y16[:, :, :, :], 0.0))
            tb = mask0t[:, :].rearrange("p (b two) -> p b two", two=2)
            chain(nc.gpsimd.memset(mask0t[:, :], 0.0))
            chain(nc.gpsimd.memset(tb[:, :, 1], -1.0))
            fill(tb[:, :, 1], 0.0, ALU.is_equal, 0, [[-2, P // 2]], 1)
            fill(mask0t[:, :], -1.0, ALU.not_equal, 0, [[-1, P]], 1)
            for li, mb in enumerate(LEVELS):
                nb = P // (2 * mb)
                blk = blocks[:, :].rearrange("p (b two m) -> p b two m", two=2, m=mb)[:, :, 0, :]
                chain(nc.gpsimd.memset(blocks[:, :], 0.0))
                chain(nc.gpsimd.memset(blk, -1.0))
                fill(blk, 0.0, ALU.is_ge, -mb, [[-2 * mb, nb], [0, mb]], 1)
                fill(blk, 0.0, ALU.is_ge, 2 * mb - 1, [[2 * mb, nb], [0, mb]], -1)
                fill(blocks[:, :], -1.0, ALU.not_equal, 0, [[-1, P]], 1)
                chain(nc.gpsimd.tensor_copy(masks[:, li].rearrange("p (b m) -> p b m", m=mb), blk))
                for u in range(U):
                    chain(nc.gpsimd.tensor_copy(halves(y16[:, li, u], mb, 1), halves(ident[:, :], mb, 1)))
            nc.gpsimd.memset(nhalf[:, :], -0.5).then_inc(m["pool_ready"], 1)

            def bc(ap, n):
                return ap.rearrange("p (u o) -> p u o", o=1).broadcast_to([P, U, n])

            def all_units(ap):
                return ap.rearrange("p (o c) -> p o c", o=1).broadcast_to([P, U, C])

            def strengths(n, c, h):
                t, g = NC * n + c, h[1]
                pool.wait_ge(m[f"dma_bcol{g}"], 16 * (h[0] + 1))
                need(pool, m["dve_scan"], t)
                nc.gpsimd.tensor_tensor(diag[:, :, 1:CX], all_units(ident[:, :]), bc(bcol[:, g, c], C),
                                        ALU.mult).then_inc(m["pool_diag"], 1)

            def system(n, c):
                t, par = NC * n + c, c % 2
                pool.wait_ge(m["dve_at"], t + 1)
                need(pool, m["pe_y"], NL * t)
                need(pool, m["pool_tt"], t)
                nc.gpsimd.tensor_tensor(am16[:, :, :], at[:, par], all_units(ident[:, :]),
                                        ALU.subtract).then_inc(m["pool_am"], 1)
                pool.wait_ge(m["pool_am"], t + 1)
                need(pool, m["pe_tr"], t - 1)
                nc.gpsimd.tensor_tensor(tt16[:, par], am16[:, :, :], all_units(mask0t[:, :]),
                                        ALU.mult).then_inc(m["pool_tt"], 1)

            def system2(n, c):
                t, par = NC * n + c, c % 2
                nc.gpsimd.tensor_tensor(at[:, par], at[:, par], all_units(ident[:, :]),
                                        ALU.add).then_inc(m["pool_atp"], 1)

            def scaled(n, c, g):
                par, cols, k = c % 2, slice(c * C, (c + 1) * C), nz(n, c)
                pool.wait_ge(m[f"dma_cum{par}"], 16 * (NC // 2 * n + c // 2 + 1))
                pool.wait_ge(m["act_silu"], 3 * U * n + 2 * U)
                need(pool, m["pe_kz"], k)
                nc.gpsimd.tensor_tensor(kg[:, :, :], kb[:, g, :, cols], cum[:, par, :, 0:C],
                                        ALU.mult).then_inc(m["pool_kg"], 1)
                need(pool, m["pe_o"], NC * n + c)
                nc.gpsimd.tensor_tensor(qg[:, :, :], qb[:, g, :, cols], cum[:, par, :, 1:CX],
                                        ALU.mult).then_inc(m["pool_qg"], 1)

            def state(n, c):
                s, par = NC * n + c, c % 2
                pool.wait_ge(m[f"dma_cum{par}"], 16 * (NC // 2 * n + c // 2 + 1))
                pool.wait_ge(m["dve_z"], s)
                nc.gpsimd.tensor_tensor(zs[:, :, :], z[:, :, :], bc(cum[:, par, :, C], D),
                                        ALU.mult).then_inc(m["pool_zs"], 1)

            def root(n, c):
                s = NC * n + c
                pool.wait_ge(m["dve_var"], s + 1)
                need(pool, m["act_on"], s)
                nc.gpsimd.tensor_tensor(rstd[:, :], var[:, :], nhalf[:, :], ALU.pow).then_inc(m["pool_rstd"], 1)

            def gated(n, c, g):
                s = NC * n + c
                pool.wait_ge(m["act_oa"], s + 1)
                pool.wait_ge(m["act_gate"], U * (n + 1))
                nc.gpsimd.tensor_tensor(oa[:, :, :], oa[:, :, :], gb[:, g, :, c * C:(c + 1) * C],
                                        ALU.mult).then_inc(m["pool_og"], 1)

            def low(n, c):
                pool.wait_ge(m["act_oh"], NC * n + c + 1)
                nc.gpsimd.tensor_tensor(ol[:, :, :], oa[:, :, :], oh[:, :, :],
                                        ALU.subtract).then_inc(m["pool_ol"], 1)

            def split_kqv(n):
                pool.wait_ge(m["act_wh"], n + 1)
                nc.gpsimd.tensor_tensor(kqv16[:, 1], w_kqv[:, :, :, :], kqv16[:, 0],
                                        ALU.subtract).then_inc(m["pool_wl"], 1)

            def split_go(n, g):
                pool.wait_ge(m["act_goh"], 2 * (n + 1))
                nc.gpsimd.tensor_tensor(gate16[:, 1], w_go[:, 0:KT * D], gate16[:, 0], ALU.subtract)
                nc.gpsimd.tensor_tensor(wo16[:, g, 1], w_go[:, KT * D:], wo16[:, g, 0],
                                        ALU.subtract).then_inc(m["pool_gol"], 1)

            split_kqv(0)
            split_go(0, 0)
            strengths(0, 0, (0, 0))
            system(0, 0)
            system2(0, 0)
            split_kqv(1)
            strengths(0, 1, (0, 0))

            def body(h, first, last):
                for g in range(G):
                    n = G * h + g
                    for c in range(NC):
                        end = last and g == G - 1
                        more = not (end and c == NC - 1)
                        prev = not (first and g == 0 and c == 0)
                        n1, c1 = later(n, c, 1)
                        g1 = g if c1 else 1 - g
                        if c:
                            state(n, c)
                        if more:
                            system(n1, c1)
                        if prev:
                            gated(*((n, c - 1, g) if c else (n - 1, NC - 1, 1 - g)))
                        if more:
                            system2(n1, c1)
                        if prev:
                            low(*((n, c - 1) if c else (n - 1, NC - 1)))
                        root(n, c)
                        if c == 1 and not end:
                            split_go(n + 1, 1 - g)
                        if c == NC - 1 and not last:
                            split_kqv(n + 2)
                        if c1 and more:
                            scaled(n1, c1, g1)
                        if not (end and c >= NC - 2):
                            n2, c2 = later(n, c, 2)
                            hg = (h, g) if c2 > 1 else ((h, 1) if g == 0 else (h + 1, 0))
                            strengths(n2, c2, hg)

            body(0, True, False)
            with pool.Fori(1, NH - 1) as h:
                body(h, False, False)
            body(NH - 1, False, True)
            gated(G * NH - 1, NC - 1, G - 1)
            low(G * NH - 1, NC - 1)

        @block.vector
        def _(dve):
            pr = prod[:, :].rearrange("p (u x) -> p u x", u=U)

            def decays(n, c):
                t, par = NC * n + c, c % 2
                dve.wait_ge(m["pool_diag"], t + 1)
                dve.wait_ge(m[f"dma_decay{par}"], 16 * (NC // 2 * n + c // 2 + 1))
                need(dve, m["act_kdec"], t)
                need(dve, m["dve_mix"], t)
                nc.vector.tensor_tensor_scan(prod[:, :], decay[:, par], diag[:, :, :].rearrange("p u x -> p (u x)"),
                                             0.0, ALU.mult, ALU.add).then_inc(m["dve_scan"], 1)

            def system(n, c):
                t, par = NC * n + c, c % 2
                dve.wait_ge(m["pe_gram"], 2 * t + 1)
                dve.wait_ge(m["dve_scan"], t + 1)
                need(dve, m["pe_aw"], t - 1)
                nc.vector.tensor_tensor(at[:, par], units(GRAM), pr[:, :, 0:C], ALU.mult).then_inc(m["dve_at"], 1)

            def mixing(n, c):
                t, par = NC * n + c, c % 2
                dve.wait_ge(m["pe_gram"], 2 * t + 2)
                need(dve, m["pe_o"], t - 1)
                nc.vector.tensor_tensor(mix[:, par], units(LEV), pr[:, :, 1:CX], ALU.mult).then_inc(m["dve_mix"], 1)

            def level(n, c, j):
                t = NC * n + c
                mb = LEVELS[j]
                nb = P // (2 * mb)
                dve.wait_ge(m["pe_y"], NL * t + j + 1)
                nc.vector.tensor_tensor(
                    even(y16[:, j], mb),
                    bank[GRAM][:, 0:U * C // 2].rearrange("p (u b m) -> p u b m", u=U, m=mb),
                    masks[:, j].rearrange("p (o b m) -> p o b m", o=1, m=mb).broadcast_to([P, U, nb, mb]),
                    ALU.mult).then_inc(m["dve_y"], 1)

            def right_side(n, c):
                s = NC * n + c
                dve.wait_ge(m["pe_kz"], nz(n, c) + 1)
                dve.wait_ge(m["act_vt"], s + 1)
                need(dve, m["act_rhs16"], s)
                need(dve, m["dve_res"], s)
                nc.vector.tensor_tensor(rhs[:, :, :], vt[:, :, :], units(SOLVE), ALU.subtract)\
                    .then_inc(m["dve_rhs"], 1)

            def residual(n, c):
                s = NC * n + c
                dve.wait_ge(m["pe_aw"], s + 1)
                dve.wait_ge(m["act_rhs16"], s + 1)
                nc.vector.tensor_tensor(res16[:, :, :], (rhs if c else vt)[:, :, :], units(SOLVE), ALU.subtract)\
                    .then_inc(m["dve_res"], 1)

            def corrected(n, c):
                s = NC * n + c
                dve.wait_ge(m["pe_tr"], s + 1)
                nc.vector.tensor_tensor(wv[:, :, :], wv[:, :, :], units(SOLVE), ALU.add).then_inc(m["dve_w"], 1)

            def new_state(n, c):
                s = NC * n + c
                dve.wait_ge(m["pe_z"], s + 1)
                if c:
                    dve.wait_ge(m["pool_zs"], nz(n, c) + 1)
                    need(dve, m["pe_kz"], nz(n, c) + 1)
                    dve.wait_ge(m["pe_o"], s + 1)
                    nc.vector.tensor_tensor(z[:, :, :], zs[:, :, :], units(UPD), ALU.add).then_inc(m["dve_z"], 1)
                else:
                    need(dve, m["pe_o"], s)
                    nc.vector.tensor_copy(z[:, :, :], units(UPD)).then_inc(m["dve_z"], 1)

            def statistics(n, c):
                s = NC * n + c
                dve.wait_ge(m["pe_o"], s + 1)
                need(dve, m["dve_mv"], U * s)
                for u in range(U):
                    nc.vector.bn_stats(bn[:, u], bank[OUT][:, u * D:(u + 1) * D]).then_inc(m["dve_bn"], 1)

            def aggregated(n, c):
                s = NC * n + c
                for u in range(U):
                    nc.vector.bn_aggr(mv[:, u], bn[:, u]).then_inc(m["dve_mv"], 1)
                dve.wait_ge(m["dve_mv"], U * (s + 1))
                need(dve, m["pool_rstd"], s)
                nc.vector.tensor_scalar(var[:, :], mv[:, :, 1], EPS / D, None, ALU.add).then_inc(m["dve_var"], 1)

            def shifts(n, c):
                s = NC * n + c
                dve.wait_ge(m["pool_rstd"], s + 1)
                need(dve, m["act_on"], s)
                nc.vector.scalar_tensor_tensor(out=shift[:, :], in0=mv[:, :, 0], scalar=-1.0, in1=rstd[:, :],
                                               op0=ALU.mult, op1=ALU.mult).then_inc(m["dve_shift"], 1)

            def output(n, c, g, k):
                dve.wait_ge(m["pe_wo"], KT * (NC * n + c) + k + 1)
                x = xs[k][:, g, :, c * C:(c + 1) * C]
                nc.vector.scalar_tensor_tensor(out=x, in0=units(UPD), scalar=1.0 / WS, in1=x,
                                               op0=ALU.mult, op1=ALU.add).then_inc(m["dve_out"], 1)

            def tap(q, i, j, par, d):
                dst = (kb, qb, vb)[i][:, par, j]
                if d == 1:
                    dve.wait_ge(m["act_acc"], q + 1)
                else:
                    dve.wait_ge(m["dve_tap"], 2 * q + d - 1)
                nc.vector.scalar_tensor_tensor(
                    out=dst[:, d:S], in0=bank[PJ[j % 2]][:, 0:S - d], scalar=prs[:, par, i, TAPS - 1 - d:TAPS - d],
                    in1=dst[:, d:S], op0=ALU.mult, op1=ALU.add)\
                    .then_inc(m["dve_tap"] if d < TAPS - 1 else m["dve_conv"], 1)

            def taps(n, g, h):
                dve.wait_ge(m[f"dma_prm{g}"], 96 * (h + 1))
                need(dve, m["dve_conv"], 3 * U * (n - 1))
                need(dve, m["act_acc"], 3 * U * (n - 1))
                nc.vector.tensor_scalar(prs[:, g], prm[:, g, :, 0:TAPS], 1.0 / WS, None, ALU.mult)\
                    .then_inc(m["dve_prs"], 1)

            dve.wait_ge(m["pool_ready"], 1)
            taps(0, 0, 0)
            dve.wait_ge(m["dve_prs"], 1)
            for i in range(3):
                for j in range(U):
                    for d in range(1, TAPS):
                        tap(U * i + j, i, j, 0, d)
            decays(0, 0)
            system(0, 0)
            mixing(0, 0)
            taps(1, 1, 0)
            for j in range(NL):
                level(0, 0, j)

            def body(h, first, last):
                for g in range(G):
                    n = G * h + g
                    for c in range(NC):
                        end = last and g == G - 1
                        more = not (end and c == NC - 1)
                        prev = not (first and g == 0 and c == 0)
                        n1, c1 = later(n, c, 1)
                        before = (n, c - 1, g) if c else (n - 1, NC - 1, 1 - g)
                        q0 = 3 * U * (n + 1) + U * c

                        def mine(j, d):
                            if c < NC - 1 and not end:
                                tap(q0 + j, c, j, 1 - g, d)

                        def carried(d):
                            if c and not end:
                                tap(q0 - 1, c - 1, U - 1, 1 - g, d)

                        def lev(j):
                            if more:
                                level(n1, c1, j)

                        if c == 0 and not end:
                            dve.wait_ge(m["dve_prs"], n + 2)
                        if more:
                            decays(n1, c1)
                        carried(1)
                        if c:
                            right_side(n, c)
                        if more:
                            system(n1, c1)
                        carried(2)
                        if more:
                            mixing(n1, c1)
                        carried(3)
                        residual(n, c)
                        corrected(n, c)
                        lev(0)
                        mine(0, 1)
                        mine(0, 2)
                        lev(1)
                        mine(0, 3)
                        statistics(n, c)
                        new_state(n, c)
                        lev(2)
                        mine(1, 1)
                        if prev:
                            output(*before, 0)
                        mine(1, 2)
                        need(dve, m["dve_bn"], U * (NC * n + c + 1))
                        need(dve, m["dve_shift"], NC * n + c)
                        lev(3)
                        mine(1, 3)
                        aggregated(n, c)
                        lev(4)
                        mine(2, 1)
                        shifts(n, c)
                        mine(2, 2)
                        lev(5)
                        if prev:
                            output(*before, 1)
                        mine(2, 3)
                        if c == NC - 1 and not last:
                            taps(n + 2, g, h + 1)

            body(0, True, False)
            with dve.Fori(1, NH - 1) as h:
                body(h, False, False)
            body(NH - 1, False, True)
            for k in range(KT):
                output(G * NH - 1, NC - 1, G - 1, k)
            dve.wait_ge(m["dve_out"], KT * STEPS)

        @block.scalar
        def _(act):
            act.wait_ge(m["dma_const"], 32)

            def split_kqv(n):
                act.wait_ge(m["dma_kqv"], 48 * (n + 1))
                nc.scalar.activation(w_kqv[:, :, :, :], w_kqv[:, :, :, :], ACT.Copy, scale=WS)\
                    .then_inc(m["act_w64"], 1)
                act.wait_ge(m["act_w64"], n + 1)
                need(act, m["pe_pj"], 16 * (n - 1) + 12 if not isinstance(n, int) or n else 0)
                nc.scalar.activation(kqv16[:, 0], w_kqv[:, :, :, :], ACT.Copy).then_inc(m["act_wh"], 1)

            def split_go(n, g):
                act.wait_ge(m["dma_go"], 32 * (n + 1))
                nc.scalar.activation(w_go[:, :], w_go[:, :], ACT.Copy, scale=WS).then_inc(m["act_go64"], 1)
                act.wait_ge(m["act_go64"], n + 1)
                need(act, m["pe_pj"], 16 * n)
                need(act, m["pe_wo"], KT * NC * (n - 1))
                nc.scalar.activation(gate16[:, 0], w_go[:, 0:KT * D], ACT.Copy).then_inc(m["act_goh"], 1)
                nc.scalar.activation(wo16[:, g, 0], w_go[:, KT * D:], ACT.Copy).then_inc(m["act_goh"], 1)

            def acc(q, npj, i, j, par, n):
                act.wait_ge(m["pe_pj"], npj + 1)
                if j == 0:
                    act.wait_ge(m["dve_prs"], n + 1)
                    need(act, m["pe_gram"], 2 * NC * (n - 1))
                    need(act, m[("pool_kg", "pool_qg", "pe_vt")[i]], (NC - 1 if i < 2 else NC) * (n - 1))
                    need(act, m["pe_kt"], NC * (n - 1))
                nc.scalar.activation((kb, qb, vb)[i][:, par, j], bank[PJ[j % 2]][:, :], ACT.Identity,
                                     bias=prm[:, par, i, TAPS:], scale=prs[:, par, i, TAPS - 1:TAPS])\
                    .then_inc(m["act_acc"], 1)

            def silu(q, i, j, par):
                dst = (kb, qb, vb)[i][:, par, j]
                act.wait_ge(m["dve_conv"], q + 1)
                nc.scalar.activation(dst, dst, ACT.Silu).then_inc(m["act_silu"], 1)

            def gate(n, g, j):
                act.wait_ge(m["pe_pj"], 16 * n + 12 + j + 1)
                if j == 0:
                    need(act, m["pool_og"], NC * (n - 1))
                nc.scalar.activation(gb[:, g, j], bank[PJ[j % 2]][:, :], ACT.Sigmoid, scale=1.0 / WS)\
                    .then_inc(m["act_gate"], 1)

            def kdecayed(n, c):
                t, par = NC * n + c, c % 2
                act.wait_ge(m["pe_kt"], t + 1)
                need(act, m["pe_z"], t - 1)
                for u in range(U):
                    ins = nc.scalar.activation(kdec[:, par, u], bank[GRAM][:, u * D:(u + 1) * D], ACT.Copy,
                                               scale=prod[:, (u + 1) * CX - 1:(u + 1) * CX])
                ins.then_inc(m["act_kdec"], 1)

            def first_inverse(n, c):
                t = NC * n + c
                act.wait_ge(m["pe_l0"], t + 1)
                need(act, m["pe_y"], NL * t)
                nc.scalar.activation(t16[:, :, :], units(GRAM), ACT.Copy).then_inc(m["act_t0"], 1)

            def level(n, c, j):
                t, par = NC * n + c, c % 2
                mb = LEVELS[j]
                act.wait_ge(m["pe_t"], NL * t + j + 1)
                half = U * C // 2
                if j < NL - 1:
                    nc.scalar.activation(even(t16[:, :, :], mb),
                                         bank[LEV][:, 0:half].rearrange("p (u b m) -> p u b m", u=U, m=mb),
                                         ACT.Copy).then_inc(m["act_t"], 1)
                nc.scalar.activation(odd(tt16[:, par], mb),
                                     bank[LEV][:, half:].rearrange("p (u b m) -> p u b m", u=U, m=mb),
                                     ACT.Copy).then_inc(m["act_tt"], 1)

            def values(n, c):
                s = NC * n + c
                act.wait_ge(m["pe_vt"], s + 1)
                need(act, m["dve_res"], s)
                need(act, m["act_rhs16"], s)
                nc.scalar.activation(vt[:, :, :], units(TURN), ACT.Copy).then_inc(m["act_vt"], 1)

            def right_side(n, c):
                s = NC * n + c
                if c:
                    act.wait_ge(m["dve_rhs"], nz(n, c) + 1)
                else:
                    act.wait_ge(m["act_vt"], s + 1)
                need(act, m["pe_w0"], s)
                nc.scalar.activation(rhs16[:, :, :], (rhs if c else vt)[:, :, :], ACT.Copy)\
                    .then_inc(m["act_rhs16"], 1)

            def first_solution(n, c):
                s = NC * n + c
                act.wait_ge(m["pe_w0"], s + 1)
                need(act, m["pe_o"], s)
                need(act, m["pe_z"], s)
                nc.scalar.activation(wv[:, :, :], units(SOLVE), ACT.Copy).then_inc(m["act_w0"], 1)

            def normed(n, c):
                s = NC * n + c
                act.wait_ge(m["dve_shift"], s + 1)
                need(act, m["pe_ot"], s)
                for u in range(U):
                    ins = nc.scalar.activation(on[:, u], bank[OUT][:, u * D:(u + 1) * D], ACT.Identity,
                                               bias=shift[:, u:u + 1], scale=rstd[:, u:u + 1])
                ins.then_inc(m["act_on"], 1)

            def affine(n, c):
                s = NC * n + c
                act.wait_ge(m["pe_ot"], s + 1)
                need(act, m["pool_ol"], s)
                nc.scalar.activation(oa[:, :, :], units(TURN), ACT.Identity, bias=lnb[:, :], scale=lnw[:, :])\
                    .then_inc(m["act_oa"], 1)

            def high(n, c):
                s = NC * n + c
                act.wait_ge(m["pool_og"], s + 1)
                need(act, m["pe_wo"], KT * s)
                nc.scalar.activation(oh[:, :, :], oa[:, :, :], ACT.Copy).then_inc(m["act_oh"], 1)

            split_kqv(0)
            for i in range(3):
                for j in range(U):
                    q = U * i + j
                    acc(q, q, i, j, 0, 0)
                    silu(q, i, j, 0)
            split_go(0, 0)
            for j in range(U):
                gate(0, 0, j)
            kdecayed(0, 0)
            first_inverse(0, 0)
            for j in range(NL):
                level(0, 0, j)
            values(0, 0)
            split_kqv(1)

            def body(h, first, last):
                for g in range(G):
                    n = G * h + g
                    for c in range(NC):
                        end = last and g == G - 1
                        more = not (end and c == NC - 1)
                        prev = not (first and g == 0 and c == 0)
                        before = (n, c - 1) if c else (n - 1, NC - 1)
                        n1, c1 = later(n, c, 1)
                        q0 = 3 * U * (n + 1) + U * c
                        pj0 = 4 * U * (n + 1) + U * c

                        def tile(j):
                            if end:
                                return
                            if c < NC - 1:
                                acc(q0 + j, pj0 + j, c, j, 1 - g, n + 1)
                            else:
                                gate(n + 1, 1 - g, j)

                        def act_on(j):
                            if end:
                                return
                            if j < 2 and c < NC - 1:
                                silu(q0 + j, c, j, 1 - g)
                            if j >= 2 and c:
                                silu(q0 - U + j, c - 1, j, 1 - g)

                        def lev(j):
                            if more:
                                level(n1, c1, j)

                        if prev:
                            normed(*before)
                        right_side(n, c)
                        act_on(2)
                        first_solution(n, c)
                        if prev:
                            affine(*before)
                        if more:
                            kdecayed(n1, c1)
                        act_on(3)
                        tile(0)
                        if more:
                            first_inverse(n1, c1)
                        if prev:
                            high(*before)
                        lev(0)
                        lev(1)
                        tile(1)
                        act_on(0)
                        lev(2)
                        if c == 1 and not end:
                            split_go(n + 1, 1 - g)
                        lev(3)
                        tile(2)
                        act_on(1)
                        lev(4)
                        if c == NC - 1 and not last:
                            split_kqv(n + 2)
                        lev(5)
                        if more:
                            values(n1, c1)
                        tile(3)

            body(0, True, False)
            with act.Fori(1, NH - 1) as h:
                body(h, False, False)
            body(NH - 1, False, True)
            normed(G * NH - 1, NC - 1)
            affine(G * NH - 1, NC - 1)
            high(G * NH - 1, NC - 1)

        @block.tensor
        def _(pe):
            half = U * C // 2

            def at_half(b, o, u):
                return bank[b][:, o + u * C // 2:o + (u + 1) * C // 2]

            def gram(n, c, g):
                t = NC * n + c
                pe.wait_ge(m["act_silu"], 3 * U * n + 2 * U)
                need(pe, m["dve_y"], NL * t)
                need(pe, m["act_tt"], NL * t)
                cols = slice(c * C, (c + 1) * C)
                for dst, right in ((GRAM, kb), (LEV, qb)):
                    for u in range(U):
                        mm = pe.matmul(units(dst)[:, u], kb[:, g, u, cols], right[:, g, u, cols], start=True, stop=True)
                    mm.then_inc(m["pe_gram"], 1)

            def k_turned(n, c, g):
                pe.wait_ge(m["dve_at"], NC * n + c + 1)
                for u in range(U):
                    mm = pe.transpose(units(GRAM)[:, u], kb[:, g, u, c * C:(c + 1) * C], ident[:, :])
                mm.then_inc(m["pe_kt"], 1)

            def first_inverse(n, c):
                t, par = NC * n + c, c % 2
                pe.wait_ge(m["pool_tt"], t + 1)
                pe.wait_ge(m["act_kdec"], t + 1)
                for u in range(U):
                    mm = pe.matmul(units(GRAM)[:, u], tt16[:, par, u], ident16[:, :], start=True, stop=True)
                mm.then_inc(m["pe_l0"], 1)

            def level_a(n, c, j):
                t, mb = NC * n + c, LEVELS[j]
                if j == 0:
                    pe.wait_ge(m["act_t0"], t + 1)
                else:
                    pe.wait_ge(m["act_t"], (NL - 1) * t + j)
                for u in range(U):
                    mm = pe.matmul(at_half(GRAM, 0, u), am16[:, u], halves(t16[:, u], mb, 0), start=True, stop=True)
                mm.then_inc(m["pe_y"], 1)

            def level_b(n, c, j):
                t, par, mb = NC * n + c, c % 2, LEVELS[j]
                pe.wait_ge(m["dve_y"], NL * t + j + 1)
                if j == 0:
                    pe.wait_ge(m["dve_mix"], t + 1)
                else:
                    pe.wait_ge(m["act_tt"], NL * t + j)
                for u in range(U):
                    if j < NL - 1:
                        pe.matmul(at_half(LEV, 0, u), tt16[:, par, u], halves(y16[:, j, u], mb, 0), start=True, stop=True)
                    mm = pe.matmul(at_half(LEV, half, u), y16[:, j, u], halves(tt16[:, par, u], mb, 1),
                                   start=True, stop=True)
                mm.then_inc(m["pe_t"], 1)

            def v_turned(n, c, g):
                s = NC * n + c
                pe.wait_ge(m["act_silu"], 3 * U * n + 3 * U)
                need(pe, m["act_oa"], s - 1)
                for u in range(U):
                    mm = pe.transpose(units(TURN)[:, u], vb[:, g, u, c * C:(c + 1) * C], ident[:, :])
                mm.then_inc(m["pe_vt"], 1)

            def state_k(n, c):
                s, k = NC * n + c, nz(n, c)
                pe.wait_ge(m["pool_kg"], k + 1)
                pe.wait_ge(m["dve_z"], s)
                pe.wait_ge(m["dve_w"], s)
                for u in range(U):
                    mm = pe.matmul(units(SOLVE)[:, u], kg[:, u], z[:, u], start=True, stop=True)
                mm.then_inc(m["pe_kz"], 1)

            def first_solution(n, c):
                s, par = NC * n + c, c % 2
                pe.wait_ge(m["act_rhs16"], s + 1)
                pe.wait_ge(m["act_tt"], NL * (s + 1))
                need(pe, m["dve_w"], s)
                for u in range(U):
                    mm = pe.matmul(units(SOLVE)[:, u], tt16[:, par, u], rhs16[:, u], start=True, stop=True)
                mm.then_inc(m["pe_w0"], 1)

            def check_solution(n, c):
                s, par = NC * n + c, c % 2
                pe.wait_ge(m["act_w0"], s + 1)
                pe.wait_ge(m["pool_atp"], s + 1)
                for u in range(U):
                    mm = pe.matmul(units(SOLVE)[:, u], at[:, par, u], wv[:, u], start=True, stop=True)
                mm.then_inc(m["pe_aw"], 1)

            def correction(n, c):
                s, par = NC * n + c, c % 2
                pe.wait_ge(m["dve_res"], s + 1)
                for u in range(U):
                    mm = pe.matmul(units(SOLVE)[:, u], tt16[:, par, u], res16[:, u], start=True, stop=True)
                mm.then_inc(m["pe_tr"], 1)

            def update(n, c):
                s, par = NC * n + c, c % 2
                pe.wait_ge(m["dve_w"], s + 1)
                need(pe, m["dve_out"], KT * (s - 1))
                for u in range(U):
                    mm = pe.matmul(units(UPD)[:, u], kdec[:, par, u], wv[:, u], start=True, stop=True)
                mm.then_inc(m["pe_z"], 1)

            def read(n, c, u0, u1):
                s, par = NC * n + c, c % 2
                if u0 == 0:
                    need(pe, m["act_on"], s)
                    if c:
                        pe.wait_ge(m["pool_qg"], nz(n, c) + 1)
                for u in range(u0, u1):
                    if c:
                        pe.matmul(units(OUT)[:, u], qg[:, u], z[:, u], start=True, stop=False)
                    mm = pe.matmul(units(OUT)[:, u], mix[:, par, u], wv[:, u], start=not c, stop=True)
                if u1 == U:
                    mm.then_inc(m["pe_o"], 1)

            def out_turned(n, c, final=False):
                s = NC * n + c
                pe.wait_ge(m["act_on"], s + 1)
                if not final:
                    need(pe, m["act_vt"], s + 2)
                for u in range(U):
                    mm = pe.transpose(units(TURN)[:, u], on[:, u], ident[:, :])
                mm.then_inc(m["pe_ot"], 1)

            def output(n, c, g, k, final=False):
                s = NC * n + c
                pe.wait_ge(m["pool_ol"], s + 1)
                if not final:
                    pe.wait_ge(m["dve_z"], s + 2)
                need(pe, m["dve_out"], KT * s + k)
                ch = slice(k * P, (k + 1) * P)
                for i, (wh, o) in enumerate(((0, oh), (0, ol), (1, oh))):
                    mm = pe.matmul(bank[UPD][:, :], wo16[:, g, wh, ch], o[:, :, :].rearrange("p u c -> p (u c)"),
                                   start=(i == 0), stop=(i == 2))
                mm.then_inc(m["pe_wo"], 1)

            def project(i, g, j, part):
                cols = slice((G * j + g) * S, (G * j + g + 1) * S)
                terms = [(wh, k, zh) for (wh, zh) in ((0, 0), (0, 1), (1, 0)) for k in range(KT)]
                for x in range(2 * part, 2 * part + 2):
                    wh, k, zh = terms[x]
                    wt = gate16[:, wh, k * D:(k + 1) * D] if i == 3 else kqv16[:, wh, k, i]
                    mm = pe.matmul(bank[PJ[j % 2]][:, :], wt, z_in[:, zh, k, cols], start=(x == 0), stop=(x == 5))
                if part == 2:
                    mm.then_inc(m["pe_pj"], 1)

            pe.wait_ge(m["pool_ready"], 1)
            pe.wait_ge(m["pool_wl"], 1)
            for i in range(4):
                if i == 3:
                    pe.wait_ge(m["pool_gol"], 1)
                for j in range(U):
                    q = U * i + j - 2
                    if q >= 0:
                        pe.wait_ge(*((m["dve_conv"], q + 1) if q < 3 * U else (m["act_gate"], q + 1 - 3 * U)))
                    for part in range(3):
                        project(i, 0, j, part)
            gram(0, 0, 0)
            k_turned(0, 0, 0)
            first_inverse(0, 0)
            for j in range(NL):
                level_a(0, 0, j)
                level_b(0, 0, j)
            v_turned(0, 0, 0)

            def body(h, first, last):
                for g in range(G):
                    n = G * h + g
                    for c in range(NC):
                        end = last and g == G - 1
                        more = not (end and c == NC - 1)
                        prev = not (first and g == 0 and c == 0)
                        before = (n, c - 1, g) if c else (n - 1, NC - 1, 1 - g)
                        n1, c1 = later(n, c, 1)
                        g1 = g if c1 else 1 - g
                        pieces = [] if end else [(j, part) for j in range(U) for part in range(3)]

                        def fill(count):
                            for _ in range(min(count, len(pieces))):
                                j, part = pieces.pop(0)
                                if part == 0:
                                    pe.wait_ge(*bank_free(n, c, j))
                                project(c, 1 - g, j, part)

                        def lev_a(j):
                            if more:
                                level_a(n1, c1, j)

                        def lev_b(j):
                            if more:
                                level_b(n1, c1, j)

                        if c:
                            state_k(n, c)
                        if more:
                            gram(n1, c1, g1)
                        if not end:
                            if c == 0:
                                pe.wait_ge(m["pool_wl"], n + 2)
                            if c == NC - 1:
                                pe.wait_ge(m["pool_gol"], n + 2)
                        fill(1)
                        first_solution(n, c)
                        if prev:
                            out_turned(*before[:2])
                        if more:
                            k_turned(n1, c1, g1)
                        fill(1)
                        check_solution(n, c)
                        fill(1)
                        correction(n, c)
                        if more:
                            first_inverse(n1, c1)
                        fill(1)
                        lev_a(0)
                        update(n, c)
                        lev_b(0)
                        read(n, c, 0, U // 2)
                        lev_a(1)
                        read(n, c, U // 2, U)
                        lev_b(1)
                        fill(2)
                        lev_a(2)
                        fill(1)
                        lev_b(2)
                        if prev:
                            output(*before, 0)
                        lev_a(3)
                        fill(1)
                        lev_b(3)
                        fill(1)
                        lev_a(4)
                        fill(1)
                        lev_b(4)
                        if prev:
                            output(*before, 1)
                        lev_a(5)
                        fill(2)
                        lev_b(5)
                        if more:
                            v_turned(n1, c1, g1)

            body(0, True, False)
            with pe.Fori(1, NH - 1) as h:
                body(h, False, False)
            body(NH - 1, False, True)
            out_turned(G * NH - 1, NC - 1, final=True)
            for k in range(KT):
                output(G * NH - 1, NC - 1, G - 1, k, final=True)


def macaron(nc, names, aps, out):
    w = {k.removeprefix("L0_attn_").removeprefix("L0_ffn_"): v for k, v in zip(names, aps)}
    a_rows = nc.dram_tensor("decay_rows", (STEPS, U * CX), F32, kind="Internal").ap()
    g_rows = nc.dram_tensor("cumulative_rows", (STEPS, U * CX), F32, kind="Internal").ap()
    b_cols = nc.dram_tensor("strength_columns", (P, STEPS * U), F32, kind="Internal").ap()
    w_saved = nc.dram_tensor("quantised_weights", (P, 3 * KT * FF), F16, kind="Internal").ap()
    scratch = (a_rows, g_rows, b_cols, w_saved)
    with ExitStack() as ctx:
        stream = ctx.enter_context(nc.sbuf_tensor("stream", [P, KT, B * S], F32))
        with ExitStack() as inner:
            z16 = inner.enter_context(nc.sbuf_tensor("z16", [P, 2, KT, B * S], F16))
            ffn_phase(nc, True, w["x"], None, stream, z16, scratch, w)
            attention_phase(nc, stream, z16, scratch, w)
        ffn_phase(nc, False, None, out, stream, None, scratch, w)


_INS = ["L0_attn_x", "L0_attn_Wq", "L0_attn_Wk", "L0_attn_Wv", "L0_attn_Wa", "L0_attn_ba", "L0_attn_Wb",
        "L0_attn_bb", "L0_attn_Wg", "L0_attn_Wo", "L0_attn_qcw", "L0_attn_qcb", "L0_attn_kcw", "L0_attn_kcb",
        "L0_attn_vcw", "L0_attn_vcb", "L0_attn_ln_w", "L0_attn_ln_b", "L0_ffn_gate_w", "L0_ffn_up_w",
        "L0_ffn_down_w", "L0_ffn_gate_scale", "L0_ffn_up_scale", "L0_ffn_down_scale"]


def kernel(**inputs):
    import concourse.bacc as bacc
    from concourse.bass_utils import run_bass_kernel_spmd

    nc = bacc.Bacc("TRN2", target_bir_lowering=False, num_devices=1)
    arrays, aps = {}, []
    for name in _INS:
        a = np.ascontiguousarray(inputs[name])
        arrays[f"in_{name}"] = a
        aps.append(nc.dram_tensor(f"in_{name}", a.shape, mybir.dt.from_np(a.dtype), kind="ExternalInput").ap())
    out = nc.dram_tensor("out", (B, S, H), F32, kind="ExternalOutput").ap()
    macaron(nc, _INS, aps, out)
    r = run_bass_kernel_spmd(nc, [arrays], core_ids=[0])
    return r.results[0]["out"]
```

```python
from contextlib import ExitStack

import numpy as np

import concourse.bass as bass
from concourse import mybir

F32 = mybir.dt.float32
F16 = mybir.dt.float16
I32 = mybir.dt.int32
ALU = mybir.AluOpType
ACT = mybir.ActivationFunctionType

B, S, H = 8, 512, 256
NH, D, TAPS = 16, 128, 4
FF = 768
P = 128
KT = H // P
MT = FF // P
TT = S // P
HB = 3
C = 128
NC = S // C
G = 2
U = B // G
STEPS = NH * G * NC
SPH = G * NC
WS = 64.0
LEVELS = [2, 4, 8, 16, 32, 64]
NL = len(LEVELS)
EPS = 1e-5
CX = C + 1


def need(eng, sem, value):
    if isinstance(value, int) and value <= 0:
        return
    eng.wait_ge(sem, value)


def even(ap, m):
    return ap.rearrange("p u (b two m) -> p u b two m", two=2, m=m)[:, :, :, 0, :]


def odd(ap, m):
    return ap.rearrange("p u (b two m) -> p u b two m", two=2, m=m)[:, :, :, 1, :]


def halves(ap, m, which):
    return ap.rearrange("p (b two m) -> p b two m", two=2, m=m)[:, :, which, :]


def ffn_phase(nc, first, x_in, y_out, stream, z16, scratch, w):
    with ExitStack() as ctx:
        tag = "f1_" if first else "f3_"

        def sb(name, shape, dt=F32):
            return ctx.enter_context(nc.sbuf_tensor(tag + name, shape, dt))

        def sem(name):
            return ctx.enter_context(nc.semaphore(tag + name))

        bank = [ctx.enter_context(nc.psum_tensor(f"{tag}bank{i}", [P, 512], F32)) for i in range(8)]
        down_b, turn_b, decay_b = bank[3:5], bank[5:7], bank[7]

        def gate_b(m):
            return bank[2 * m % 3]

        def up_b(m):
            return bank[(2 * m + 1) % 3]

        ident = sb("ident", [P, P])
        gs = sb("gs", [P, MT]); us = sb("us", [P, MT]); ds_ = sb("ds", [P, KT]); hds = sb("hds", [P, KT])
        wq16 = sb("wq16", [P, 3 * KT * FF], F16)
        gate16 = wq16[:, 0:KT * FF].rearrange("p (k n) -> p k n", k=KT)
        up16 = wq16[:, KT * FF:2 * KT * FF].rearrange("p (k n) -> p k n", k=KT)
        down16 = wq16[:, 2 * KT * FF:].rearrange("p (m n) -> p m n", m=MT)
        tok = sb("tok", [P, 2, TT, H])
        xin = None if first else sb("xin", [P, KT, S])
        res = sb("res", [P, KT, S])
        nhalf = sb("nhalf", [P, TT])
        bn = sb("bn", [P, 2, TT, 6]); mv = sb("mv", [P, 2, TT, 2])
        var = sb("var", [P, 2, TT]); rstd = sb("rstd", [P, 2, TT])
        ztok = sb("ztok", [P, 2, TT, H])
        zh = sb("zh", [P, 2, KT, S], F16); zl = sb("zl", [P, 2, KT, S], F16)
        sg = sb("sg", [P, 2, S]); hid = sb("hid", [P, HB, S])
        hh = sb("hh", [P, HB, S], F16); hl = sb("hl", [P, HB, S], F16)
        if first:
            wraw = sb("wraw", [P, 3 * KT * FF]); wexp = sb("wexp", [P, KT * FF])
            wab = sb("wab", [P, KT, 2 * NH]); wab64 = sb("wab64", [P, KT, 2 * NH])
            wabh = sb("wabh", [P, KT, 2 * NH], F16); wabl = sb("wabl", [P, KT, 2 * NH], F16)
            bab = sb("bab", [2 * NH, 1])
            ab = sb("ab", [2 * NH, 2, NC, CX]); gx = sb("gx", [NH, 2, NC, CX])
            zero = sb("zero", [NH, C])
            bcol = sb("bcol", [P, NH, G, NC, U])

        def for_first(*names):
            return [sem(n) if first else None for n in names]

        def of_norms(name):
            return [sem(name + "0")] + for_first(name + "1")

        s_w = [sem(f"dma_weights{i}") for i in range(3)]; s_small = sem("dma_small")
        s_x = for_first("dma_tokens0", "dma_tokens1"); s_out = [sem("dma_out0"), sem("dma_out1")]
        s_save, s_wd = for_first("dma_saved", "weights_ready")
        s_const = sem("constants"); s_q = sem("quantise_step")
        p_x = sem("pe_x_turned"); p_res = sem("pe_res_turned"); p_z = of_norms("pe_z")
        p_gate = sem("pe_gate"); p_up = sem("pe_up"); p_down = sem("pe_down")
        p_ab, p_abt, a_ab = for_first("pe_ab", "pe_abt", "act_ab")
        a_x = sem("act_x"); a_zh = of_norms("act_zh"); a_ot = sem("act_out")
        a_sg = sem("act_silu"); a_hh = sem("act_hh")
        d_bn = of_norms("dve_stats"); d_mv = of_norms("dve_mean"); d_var = of_norms("dve_var")
        d_z = of_norms("dve_z"); d_zl = of_norms("dve_zl")
        d_h = sem("dve_hidden"); d_y = sem("dve_y"); d_g, d_b = for_first("dve_g", "dve_bcol")
        g_rs = of_norms("pool_rstd"); g_hl = sem("pool_hl")

        def stored(pairs):
            return 16 + (32 if first else 16) * pairs

        x_tok = None if x_in is None else x_in.rearrange("b (t p) c -> b p t c", p=P)
        y_tok = None if y_out is None else y_out.rearrange("b (t p) c -> b p t c", p=P)
        a_rows, g_rows, b_cols, w_saved = scratch
        a_to = a_rows.rearrange("(h g c) (j x) -> g j h c x", h=NH, g=G, x=CX)
        g_to = g_rows.rearrange("(h g c) (j x) -> g j h c x", h=NH, g=G, x=CX)

        def block_of(ap, b):
            if isinstance(b, int):
                return ap[:, b * S:(b + 1) * S]
            return ap.rearrange("p (b s) -> p b s", b=B)[:, bass.ds(b, 1), :].rearrange("p o s -> p (o s)")

        def item(ap, b):
            return ap[b:b + 1] if isinstance(b, int) else ap[bass.ds(b, 1)]

        def turns(eng, turn):
            for g in range(G):
                turn(0, g)
            with eng.Fori(1, U - 1) as it:
                for g in range(G):
                    turn(it, g)
            for g in range(G):
                turn(U - 1, g)
            for g in range(G):
                turn(U, g)

        def around(it, g):
            b = G * it + g

            def there(other):
                return not isinstance(b, int) or 0 <= other < B

            return (b, ((it, 1) if g == 0 else (it + 1, 0)) if there(b + 1) else None,
                    ((it - 1, 1) if g == 0 else (it, 0)) if there(b - 1) else None,
                    (it - 1, g) if first and there(b - 2) else None, there(b))

        block = ctx.enter_context(nc.Block())

        @block.sync
        def _(sp):
            def load_tok(pair, g):
                sp.dma_start(tok[:, g], item(x_tok, G * pair + g).rearrange("o p t c -> (o p) t c"))\
                    .then_inc(s_x[g], 16)

            if first:
                load_tok(0, 0)
                for i, (name, rows) in enumerate((("gate_w", KT), ("up_w", KT), ("down_w", MT))):
                    sp.dma_start(wraw[:, i * KT * FF:(i + 1) * KT * FF].rearrange("p (k n) -> p k n", k=rows),
                                 w[name].rearrange("(k p) n -> p k n", p=P)).then_inc(s_w[i], 16)
                    if i == 0:
                        load_tok(0, 1)
                sp.dma_start(wab[:, :, 0:NH], w["Wa"].rearrange("(k p) n -> p k n", p=P)).then_inc(s_small, 16)
                sp.dma_start(wab[:, :, NH:], w["Wb"].rearrange("(k p) n -> p k n", p=P)).then_inc(s_small, 16)
                sp.dma_start(bab[0:NH, :], w["ba"].rearrange("(p o) -> p o", o=1)).then_inc(s_small, 16)
                sp.dma_start(bab[NH:, :], w["bb"].rearrange("(p o) -> p o", o=1)).then_inc(s_small, 16)
            else:
                for i in range(3):
                    cols = slice(i * KT * FF, (i + 1) * KT * FF)
                    sp.dma_start(wq16[:, cols], w_saved[:, cols]).then_inc(s_w[i], 16)
            for dst, name, done in ((gs, "gate_scale", s_out[0]), (us, "up_scale", s_out[1]),
                                    (ds_, "down_scale", s_small)):
                sp.dma_start(dst[:, :], w[name].rearrange("(m p) -> p m", p=P),
                             allow_slow_non_contiguous=True).then_inc(done, 16)

            def turn(it, g):
                b, nxt, last, old, cur = around(it, g)
                if first and isinstance(b, int) and b == 1:
                    sp.wait_ge(s_wd, 4)
                    sp.dma_start(w_saved, wq16[:, :]).then_inc(s_save, 16)
                if first and not (isinstance(b, int) and b + G >= B):
                    sp.wait_ge(p_x, b + 1)
                    sp.wait_ge(d_z[0], b + 1)
                    load_tok(it + 1, g)
                if old:
                    sp.wait_ge(a_ab, b - 1)
                    sp.dma_start(item(a_to[g], old[0]).rearrange("o h c x -> (o h) c x"),
                                 ab[0:NH, g]).then_inc(s_out[g], 16)
                    sp.wait_ge(d_g, NC * (b - 1))
                    sp.dma_start(item(g_to[g], old[0]).rearrange("o h c x -> (o h) c x"),
                                 gx[:, g]).then_inc(s_out[g], 16)
                if not first and last:
                    sp.wait_ge(a_ot, KT * b)
                    sp.dma_start(item(y_tok, G * last[0] + last[1]).rearrange("o p t c -> (o p) t c"),
                                 tok[:, last[1]]).then_inc(s_out[last[1]], 16)

            turns(sp, turn)
            if first:
                sp.wait_ge(d_b, B)
                sp.dma_start(b_cols, bcol[:, :, :, :, :].rearrange("p h g c j -> p (h g c j)")).then_inc(s_save, 16)
                sp.wait_ge(s_save, 32)
            for g in range(2):
                sp.wait_ge(s_out[g], stored(U))

        @block.gpsimd
        def _(pool):
            nc.gpsimd.memset(ident[:, :], 0.0).then_inc(s_const, 1)
            nc.gpsimd.memset(nhalf[:, :], -0.5).then_inc(s_const, 1)
            if first:
                nc.gpsimd.memset(zero[:, :], 0.0)
                nc.gpsimd.memset(ab[:, :, :, :], 0.0)
                nc.gpsimd.memset(gx[:, :, :, :], 1.0).then_inc(s_const, 1)
            else:
                nc.gpsimd.memset(rstd[:, :, :], 0.0).then_inc(s_const, 1)
            pool.wait_ge(s_const, 2)
            nc.gpsimd.affine_select(out=ident[:, :], in_=ident[:, :], compare_op=ALU.not_equal, fill=1.0,
                                    base=0, pattern=[[-1, P]], channel_multiplier=1).then_inc(s_const, 1)

            def root(n, e):
                pool.wait_ge(d_var[n], e + 1)
                need(pool, d_z[n], e)
                nc.gpsimd.tensor_tensor(rstd[:, n], var[:, n], nhalf[:, :], ALU.pow).then_inc(g_rs[n], 1)

            def low(b, m):
                q = MT * b + m
                pool.wait_ge(a_hh, q + 1)
                need(pool, p_down, q - HB + 1)
                nc.gpsimd.tensor_tensor(hl[:, m % HB], hid[:, m % HB], hh[:, m % HB],
                                        ALU.subtract).then_inc(g_hl, 1)

            def turn(it, g):
                b, nxt, last, old, cur = around(it, g)
                if first:
                    if nxt:
                        root(0, b + 1)
                    if cur:
                        low(b, 0)
                    if last:
                        root(1, b - 1)
                    if cur:
                        low(b, 1)
                        low(b, 2)
                        low(b, 3)
                        low(b, 4)
                        low(b, 5)
                else:
                    if nxt:
                        root(0, b + 1)
                    if cur:
                        low(b, 0)
                        low(b, 1)
                        low(b, 2)
                        low(b, 3)
                        low(b, 4)
                        low(b, 5)

            root(0, 0)
            turns(pool, turn)

        @block.vector
        def _(dve):
            qn = [0]

            def chain(ins):
                qn[0] += 1
                ins.then_inc(s_q, 1)
                dve.wait_ge(s_q, qn[0])

            def stats(n, e, g):
                if n == 0 and first:
                    src = [tok[:, g, t] for t in range(TT)]
                else:
                    dve.wait_ge(p_res if n else p_x, e + 1)
                    src = [turn_b[t // 2][:, t % 2 * H:(t % 2 + 1) * H] for t in range(TT)]
                need(dve, d_mv[n], TT * e)
                for t in range(TT):
                    nc.vector.bn_stats(bn[:, n, t], src[t]).then_inc(d_bn[n], 1)

            def variance(n, e):
                for t in range(TT):
                    nc.vector.bn_aggr(mv[:, n, t], bn[:, n, t]).then_inc(d_mv[n], 1)
                dve.wait_ge(d_mv[n], TT * (e + 1))
                need(dve, g_rs[n], e)
                nc.vector.tensor_scalar(var[:, n], mv[:, n, :, 1], EPS, None, ALU.add).then_inc(d_var[n], 1)

            def normed(n, e, g):
                dve.wait_ge(g_rs[n], e + 1)
                need(dve, p_z[n], e)
                for t in range(TT):
                    if n == 0 and first:
                        src = tok[:, g, t]
                    else:
                        src = turn_b[t // 2][:, t % 2 * H:(t % 2 + 1) * H]
                    ins = nc.vector.tensor_scalar(ztok[:, n, t], src, mv[:, n, t, 0:1], rstd[:, n, t:t + 1],
                                                  ALU.subtract, ALU.mult)
                ins.then_inc(d_z[n], 1)

            def low(n, e, g):
                dve.wait_ge(p_z[n], e + 1)
                dve.wait_ge(a_zh[n], KT * (e + 1))
                for k in range(KT):
                    if n == 0:
                        hi, lo = zh[:, g, k], zl[:, g, k]
                    else:
                        hi, lo = block_of(z16[:, 0, k], e), block_of(z16[:, 1, k], e)
                    nc.vector.tensor_tensor(lo, turn_b[k][:, :], hi, ALU.subtract).then_inc(d_zl[n], 1)

            def hidden(b, m):
                q = MT * b + m
                dve.wait_ge(p_up, q + 1)
                dve.wait_ge(a_sg, q + 1)
                need(dve, g_hl, q - HB + 1)
                nc.vector.scalar_tensor_tensor(out=hid[:, m % HB], in0=up_b(m)[:, :],
                                               scalar=us[:, m:m + 1], in1=sg[:, m % 2],
                                               op0=ALU.mult, op1=ALU.mult).then_inc(d_h, 1)

            def added(e):
                dve.wait_ge(p_down, MT * (e + 1))
                need(dve, p_res, e)
                if first:
                    need(dve, a_ot, KT * e)
                for k in range(KT):
                    nc.vector.scalar_tensor_tensor(out=res[:, k], in0=down_b[k][:, :],
                                                   scalar=hds[:, k:k + 1], in1=block_of(stream[:, k], e),
                                                   op0=ALU.mult, op1=ALU.add).then_inc(d_y, 1)

            def cumulative(e, pair, g):
                dve.wait_ge(a_ab, e + 1)
                dve.wait_ge(s_out[g], stored(pair))
                for c in range(NC):
                    nc.vector.tensor_tensor_scan(gx[:, g, c, 1:CX], ab[0:NH, g, c, 1:CX], zero[:, :],
                                                 1.0, ALU.mult, ALU.add).then_inc(d_g, 1)

            def strengths(e, pair, g):
                dve.wait_ge(p_abt, e + 1)
                dst = bcol[:, :, g, :, pair:pair + 1] if isinstance(pair, int) else bcol[:, :, g, :, bass.ds(pair, 1)]
                nc.vector.tensor_scalar(dst.rearrange("p h c o -> p h (c o)"),
                                        decay_b[:, 0:NC * 2 * NH].rearrange("p (c r) -> p r c", c=NC)[:, NH:, :],
                                        1.0 / D, None, ALU.mult).then_inc(d_b, 1)

            def turn(it, g):
                b, nxt, last, old, cur = around(it, g)
                if first:
                    if nxt:
                        dve.wait_ge(s_x[nxt[1]], 16 * (nxt[0] + 1))
                        stats(0, b + 1, nxt[1])
                        dve.wait_ge(d_bn[0], TT * (b + 2))
                        need(dve, d_z[0], b + 1)
                    if cur:
                        hidden(b, 0)
                    if nxt:
                        variance(0, b + 1)
                        normed(0, b + 1, nxt[1])
                    if last:
                        added(b - 1)
                    if cur:
                        hidden(b, 1)
                    if nxt:
                        low(0, b + 1, nxt[1])
                    if cur:
                        hidden(b, 2)
                    if last:
                        stats(1, b - 1, last[1])
                        dve.wait_ge(d_bn[1], TT * b)
                        need(dve, d_z[1], b - 1)
                    if old:
                        strengths(b - 2, *old)
                    if last:
                        variance(1, b - 1)
                    if cur:
                        hidden(b, 3)
                    if last:
                        normed(1, b - 1, last[1])
                    if cur:
                        hidden(b, 4)
                    if last:
                        low(1, b - 1, last[1])
                    if cur:
                        hidden(b, 5)
                    if old:
                        cumulative(b - 2, *old)
                else:
                    if nxt:
                        stats(0, b + 1, nxt[1])
                        dve.wait_ge(d_bn[0], TT * (b + 2))
                        need(dve, d_z[0], b + 1)
                    if cur:
                        hidden(b, 0)
                    if nxt:
                        variance(0, b + 1)
                    if cur:
                        hidden(b, 1)
                    if last:
                        added(b - 1)
                    if cur:
                        hidden(b, 2)
                    if nxt:
                        normed(0, b + 1, nxt[1])
                    if cur:
                        hidden(b, 3)
                    if nxt:
                        low(0, b + 1, nxt[1])
                    if cur:
                        hidden(b, 4)
                        hidden(b, 5)

            dve.wait_ge(s_const, 4)
            if first:
                dve.wait_ge(s_x[0], 16)
            stats(0, 0, 0)
            dve.wait_ge(d_bn[0], TT)
            variance(0, 0)
            normed(0, 0, 0)
            if not first:
                low(0, 0, 0)
            if first:
                for i in range(3):
                    r, q = wraw[:, i * KT * FF:(i + 1) * KT * FF], wq16[:, i * KT * FF:(i + 1) * KT * FF]
                    e = wexp[:, :]
                    dve.wait_ge(s_w[i], 16)
                    chain(nc.vector.tensor_scalar(e.bitcast(I32), r.bitcast(I32), 0x7F800000, None, ALU.bitwise_and))
                    chain(nc.vector.tensor_scalar(e, e, 2.0 ** -6, 1.5 * 2.0 ** 20, ALU.max, ALU.mult))
                    chain(nc.vector.tensor_tensor(r, r, e, ALU.add))
                    chain(nc.vector.tensor_tensor(r, r, e, ALU.subtract))
                    chain(nc.vector.tensor_scalar(e, r, 1.125 * 2.0 ** 119, 0.0, ALU.mult, ALU.mult))
                    nc.vector.tensor_tensor(q, r, e, ALU.add).then_inc(s_wd, 1)
                    dve.wait_ge(s_wd, i + 1)
                    if i == 0:
                        low(0, 0, 0)
                dve.wait_ge(s_small, 16 * 5)
                chain(nc.vector.tensor_scalar(wab64[:, :, :], wab[:, :, :], WS, None, ALU.mult))
                chain(nc.vector.tensor_copy(wabh[:, :, :], wab64[:, :, :]))
                nc.vector.tensor_tensor(wabl[:, :, :], wab64[:, :, :], wabh[:, :, :], ALU.subtract)\
                    .then_inc(s_wd, 1)
            dve.wait_ge(s_small, 16 * (5 if first else 1))
            dve.wait_ge(s_out[1], stored(0))
            chain(nc.vector.tensor_scalar(hds[:, :], ds_[:, :], 0.5, None, ALU.mult))
            turns(dve, turn)

        @block.scalar
        def _(act):
            def stream_in(e):
                if first:
                    act.wait_ge(p_x, e + 1)
                else:
                    need(act, p_x, e)
                for k in range(KT):
                    if first:
                        nc.scalar.activation(block_of(stream[:, k], e), turn_b[k][:, :], ACT.Copy).then_inc(a_x, 1)
                    else:
                        nc.scalar.activation(xin[:, k], block_of(stream[:, k], e), ACT.Copy).then_inc(a_x, 1)

            def high(n, e, g):
                act.wait_ge(p_z[n], e + 1)
                if n == 0:
                    need(act, p_up, MT * (e - 1))
                for k in range(KT):
                    dst = block_of(z16[:, 0, k], e) if n else zh[:, g, k]
                    nc.scalar.activation(dst, turn_b[k][:, :], ACT.Copy).then_inc(a_zh[n], 1)

            def silu(b, m):
                q = MT * b + m
                act.wait_ge(p_gate, q + 1)
                need(act, d_h, q - 1)
                nc.scalar.activation(sg[:, m % 2], gate_b(m)[:, :], ACT.Silu,
                                     scale=gs[:, m:m + 1]).then_inc(a_sg, 1)

            def hidden_high(b, m):
                q = MT * b + m
                act.wait_ge(d_h, q + 1)
                need(act, p_down, q - HB + 1)
                nc.scalar.activation(hh[:, m % HB], hid[:, m % HB], ACT.Copy).then_inc(a_hh, 1)

            def stream_out(e):
                act.wait_ge(d_y, KT * (e + 1))
                for k in range(KT):
                    nc.scalar.activation(block_of(stream[:, k], e), res[:, k], ACT.Copy).then_inc(a_ot, 1)

            def decays(e, pair, g):
                act.wait_ge(p_ab, e + 1)
                act.wait_ge(s_out[g], stored(pair))
                nc.scalar.activation(ab[:, g, :, 1:CX], decay_b[0:2 * NH, :].rearrange("p (c x) -> p c x", c=NC),
                                     ACT.Sigmoid, bias=bab[:, :], scale=1.0 / WS).then_inc(a_ab, 1)

            def result(e, pair, g):
                act.wait_ge(p_res, e + 1)
                act.wait_ge(s_out[g], stored(pair))
                for n in range(KT):
                    nc.scalar.activation(tok[:, g, 2 * n:2 * n + 2].rearrange("p t c -> p (t c)"),
                                         turn_b[n][:, :], ACT.Copy).then_inc(a_ot, 1)

            def turn(it, g):
                b, nxt, last, old, cur = around(it, g)
                if first:
                    if cur:
                        silu(b, 0)
                    if old:
                        decays(b - 2, *old)
                    if nxt:
                        stream_in(b + 1)
                    if cur:
                        hidden_high(b, 0)
                        silu(b, 1)
                    if nxt:
                        high(0, b + 1, nxt[1])
                    if cur:
                        silu(b, 2)
                        hidden_high(b, 1)
                        hidden_high(b, 2)
                        silu(b, 3)
                    if last:
                        stream_out(b - 1)
                    if cur:
                        hidden_high(b, 3)
                        silu(b, 4)
                    if last:
                        high(1, b - 1, last[1])
                    if cur:
                        silu(b, 5)
                        hidden_high(b, 4)
                        hidden_high(b, 5)
                else:
                    if cur:
                        silu(b, 0)
                        silu(b, 1)
                        hidden_high(b, 0)
                    if nxt and not (isinstance(b, int) and b + 2 >= B):
                        stream_in(b + 2)
                    if cur:
                        hidden_high(b, 1)
                        silu(b, 2)
                        silu(b, 3)
                        hidden_high(b, 2)
                        hidden_high(b, 3)
                    if nxt:
                        high(0, b + 1, nxt[1])
                    if cur:
                        silu(b, 4)
                        silu(b, 5)
                        hidden_high(b, 4)
                    if last:
                        result(b - 1, *last)
                    if cur:
                        hidden_high(b, 5)

            stream_in(0)
            if not first:
                stream_in(1)
            high(0, 0, 0)
            act.wait_ge(s_small, 16 * (5 if first else 1))
            act.wait_ge(s_out[0], stored(0))
            turns(act, turn)

        @block.tensor
        def _(pe):
            def x_turned(e, pair, g):
                if first:
                    pe.wait_ge(s_x[g], 16 * (pair + 1))
                    need(pe, a_zh[1], KT * (e - 2))
                    need(pe, d_zl[1], KT * (e - 2))
                else:
                    pe.wait_ge(a_x, KT * (e + 1))
                    need(pe, a_ot, KT * (e - 2))
                for t in range(TT):
                    for k in range(KT):
                        if first:
                            dst, src = turn_b[k][:, t * P:(t + 1) * P], tok[:, g, t, k * P:(k + 1) * P]
                        else:
                            o = (t % 2 * KT + k) * P
                            dst, src = turn_b[t // 2][:, o:o + P], xin[:, k, t * P:(t + 1) * P]
                        mm = pe.transpose(dst, src, ident[:, :])
                mm.then_inc(p_x, 1)

            def z_turned(n, e):
                pe.wait_ge(d_z[n], e + 1)
                if first and n == 0:
                    pe.wait_ge(a_x, KT * (e + 1))
                for k in range(KT):
                    for t in range(TT):
                        mm = pe.transpose(turn_b[k][:, t * P:(t + 1) * P], ztok[:, n, t, k * P:(k + 1) * P],
                                          ident[:, :])
                mm.then_inc(p_z[n], 1)

            def res_turned(e, nxt):
                pe.wait_ge(d_y, KT * (e + 1))
                if nxt:
                    pe.wait_ge(a_zh[0], KT * (e + 3))
                    pe.wait_ge(d_zl[0], KT * (e + 3))
                for t in range(TT):
                    for k in range(KT):
                        o = (t % 2 * KT + k) * P
                        mm = pe.transpose(turn_b[t // 2][:, o:o + P], res[:, k, t * P:(t + 1) * P], ident[:, :])
                mm.then_inc(p_res, 1)

            def weights_there(b, i):
                if isinstance(b, int) and b == 0:
                    if first:
                        pe.wait_ge(s_wd, (1, 2, 4)[i])
                    else:
                        pe.wait_ge(s_w[i], 16)

            def gate(b, m, g):
                q = MT * b + m
                if m == 0:
                    weights_there(b, 0)
                    pe.wait_ge(a_zh[0], KT * (b + 1))
                    pe.wait_ge(d_zl[0], KT * (b + 1))
                need(pe, d_h, q - 1)
                products(gate_b(m), gate16, m, g, p_gate)

            def up(b, m, g):
                if m == 0:
                    weights_there(b, 1)
                need(pe, a_sg, MT * b + m)
                products(up_b(m), up16, m, g, p_up)

            def products(dst, wt, m, g, done):
                n = 0
                for half in (zh, zl):
                    for k in range(KT):
                        mm = pe.matmul(dst[:, :], wt[:, k, m * P:(m + 1) * P], half[:, g, k],
                                       start=(n == 0), stop=(n == 2 * KT - 1))
                        n += 1
                mm.then_inc(done, 1)

            def down(b, m):
                q = MT * b + m
                pe.wait_ge(g_hl, q + 1)
                if m == 0:
                    weights_there(b, 2)
                    need(pe, d_y, KT * b)
                for part, half in enumerate((hh, hl)):
                    for k in range(KT):
                        mm = pe.matmul(down_b[k][:, :], down16[:, m, k * P:(k + 1) * P], half[:, m % HB],
                                       start=(m == 0 and part == 0), stop=(m == MT - 1 and part == 1))
                mm.then_inc(p_down, 1)

            def decay_products(e):
                pe.wait_ge(a_zh[1], KT * (e + 1))
                pe.wait_ge(d_zl[1], KT * (e + 1))
                need(pe, d_b, e)
                n = 0
                for k in range(KT):
                    for wt, half in ((wabh, 0), (wabh, 1), (wabl, 0)):
                        mm = pe.matmul(decay_b[0:2 * NH, :], wt[:, k, :], block_of(z16[:, half, k], e),
                                       start=(n == 0), stop=(n == 3 * KT - 1))
                        n += 1
                mm.then_inc(p_ab, 1)

            def strengths_turned(e, g):
                pe.wait_ge(a_ab, e + 1)
                for c in range(NC):
                    mm = pe.matmul(decay_b[:, c * 2 * NH:(c + 1) * 2 * NH], ab[:, g, c, 1:CX],
                                   ident[0:2 * NH, 0:2 * NH], start=True, stop=True)
                mm.then_inc(p_abt, 1)

            def turn(it, g):
                b, nxt, last, old, cur = around(it, g)
                if first:
                    if cur:
                        gate(b, 0, g)
                        up(b, 0, g)
                    if last:
                        down(b - 1, 4)
                    if nxt:
                        x_turned(b + 1, *nxt)
                    if last:
                        down(b - 1, 5)
                    if cur:
                        gate(b, 1, g)
                    if old:
                        strengths_turned(b - 2, old[1])
                    if cur:
                        up(b, 1, g)
                    if nxt:
                        z_turned(0, b + 1)
                    if cur:
                        gate(b, 2, g)
                        up(b, 2, g)
                        gate(b, 3, g)
                    if last:
                        res_turned(b - 1, nxt)
                    if cur:
                        up(b, 3, g)
                        down(b, 0)
                        gate(b, 4, g)
                        up(b, 4, g)
                        gate(b, 5, g)
                        down(b, 1)
                    if last:
                        z_turned(1, b - 1)
                    if cur:
                        up(b, 5, g)
                        down(b, 2)
                        down(b, 3)
                    if last:
                        decay_products(b - 1)
                else:
                    if cur:
                        gate(b, 0, g)
                    if nxt:
                        x_turned(b + 1, *nxt)
                    if cur:
                        up(b, 0, g)
                    if last:
                        down(b - 1, 4)
                    if cur:
                        gate(b, 1, g)
                        up(b, 1, g)
                    if last:
                        down(b - 1, 5)
                    if cur:
                        gate(b, 2, g)
                        up(b, 2, g)
                        down(b, 0)
                        gate(b, 3, g)
                        down(b, 1)
                        up(b, 3, g)
                    if nxt:
                        z_turned(0, b + 1)
                    if cur:
                        gate(b, 4, g)
                        down(b, 2)
                        up(b, 4, g)
                        down(b, 3)
                        gate(b, 5, g)
                    if last:
                        res_turned(b - 1, nxt)
                    if cur:
                        up(b, 5, g)

            pe.wait_ge(s_const, 4)
            x_turned(0, 0, 0)
            z_turned(0, 0)
            turns(pe, turn)


def attention_phase(nc, stream, z16, scratch, w):
    with ExitStack() as ctx:
        def sb(name, shape, dt=F32):
            return ctx.enter_context(nc.sbuf_tensor("a_" + name, shape, dt))

        def sem(name):
            return ctx.enter_context(nc.semaphore("a_" + name))

        bank = [ctx.enter_context(nc.psum_tensor(f"a_bank{i}", [P, 512], F32)) for i in range(8)]
        PJ, DIFF, LEV, SOLVE, TURN, OUT, UPD = (0, 1), 2, 3, 4, 5, 6, 7

        def units(b):
            return bank[b][:, :].rearrange("p (u c) -> p u c", u=U)

        ident = sb("ident", [P, P]); ident16 = sb("ident16", [P, P], F16)
        blocks = sb("blocks", [P, P])
        mask0t = sb("mask0t", [P, P])
        masks = sb("masks", [P, NL, P // 2])
        nhalf = sb("nhalf", [P, U])
        lnw = sb("lnw", [P, 1]); lnb = sb("lnb", [P, 1])
        qb = sb("qb", [P, 2, U, S]); kb = sb("kb", [P, 2, U, S]); vb = sb("vb", [P, 2, U, S])
        gb = sb("gb", [P, 2, U, S])
        w_kqv = sb("w_kqv", [P, KT, 3, D]); w_go = sb("w_go", [P, 2 * KT * D])
        kqv16 = sb("kqv16", [P, 2, KT, 3, D], F16)
        gate16 = sb("gate16", [P, 2, KT * D], F16)
        wo16 = sb("wo16", [P, 2, 2, H], F16)
        prm = sb("prm", [P, 2, 3, TAPS + 1]); prs = sb("prs", [P, 2, 3, TAPS])
        bcol = sb("bcol", [P, 2, NC, U])
        decay = sb("decay", [P, 2, U * CX]); cum = sb("cum", [P, 2, U, CX])
        diag = sb("diag", [P, U, CX]); prod = sb("prod", [P, U * CX])
        at = sb("at", [P, 2, U, C]); mix = sb("mix", [P, 2, U, C]); kdec = sb("kdec", [P, 2, U, D])
        am16 = sb("am16", [P, 2, U, C], F16); t16 = sb("t16", [P, U, C], F16)
        tt16 = sb("tt16", [P, 2, U, C], F16); y16 = sb("y16", [P, NL, U, C], F16)
        kg = sb("kg", [P, U, C]); qg = sb("qg", [P, U, C]); z = sb("z", [P, U, D]); zs = sb("zs", [P, U, D])
        vt = sb("vt", [P, U, D]); rhs = sb("rhs", [P, U, D]); rhs16 = sb("rhs16", [P, U, D], F16)
        wv = sb("wv", [P, U, D]); res16 = sb("res16", [P, U, D], F16)
        bn = sb("bn", [P, U, 6]); mv = sb("mv", [P, U, 2]); var = sb("var", [P, U])
        rstd = sb("rstd", [P, U]); shift = sb("shift", [P, U])
        on = sb("on", [P, U, D]); oa = sb("oa", [P, U, C])
        oh = sb("oh", [P, U, C], F16); ol = sb("ol", [P, U, C], F16)

        names = dict(
            dma="const kqv go prm0 prm1 bcol0 bcol1 decay0 decay1 cum0 cum1",
            pe="gram kt l0 y t vt kz w0 aw tr o z ot wo pj",
            dve="scan at mix y rhs res w z bn mv var shift out tap conv prs",
            act="vt rhs16 w0 kdec t0 t tt on oa oh acc silu gate w64 wh go64 goh",
            pool="const ready diag am tt atp kg qg zs rstd og ol wl gol",
        )
        m = {f"{e}_{n}": sem(f"{e}_{n}") for e, v in names.items() for n in v.split()}

        a_rows, g_rows, b_cols, _ = scratch
        z_in = z16
        xs = [stream[:, k].rearrange("p (j g s) -> p g j s", j=U, g=G) for k in range(KT)]

        def nz(n, c):
            return (NC - 1) * n + max(c - 1, 0)

        def later(n, c, k):
            return n + (c + k) // NC, (c + k) % NC

        def tile_done(n, c, j):
            if c == NC - 1:
                return m["act_gate"], U * (n + 1) + j + 1
            return m["dve_conv"], 3 * U * (n + 1) + U * c + j + 1

        def bank_free(n, c, j):
            if j >= 2:
                return tile_done(n, c, j - 2)
            return tile_done(n, c - 1, j + 2) if c else tile_done(n - 1, NC - 1, j + 2)

        block = ctx.enter_context(nc.Block())
        heads = {k: w[k].rearrange("(k p) (h d) -> h p k d", p=P, d=D) for k in ("Wq", "Wk", "Wv", "Wg")}
        wo_h = w["Wo"].rearrange("(h p) n -> h p n", p=P)
        cw_h = {k: w[k].rearrange("(h p) t -> h p t", p=P) for k in ("kcw", "qcw", "vcw")}
        cb_h = {k: w[k].rearrange("(h p o) -> h p o", p=P, o=1) for k in ("kcb", "qcb", "vcb")}

        def pick(ap, h):
            if isinstance(h, int):
                return ap[h]
            v = ap[bass.ds(h, 1)]
            return v.rearrange("o p k d -> (o p) k d") if len(v.shape) == 4 else v.rearrange("o p d -> (o p) d")

        @block.sync
        def _(sp):
            def load_kqv(h, n):
                need(sp, m["pool_wl"], n)
                for i, k in enumerate(("Wk", "Wq", "Wv")):
                    sp.dma_start(w_kqv[:, :, i], pick(heads[k], h)).then_inc(m["dma_kqv"], 16)

            def load_go(h, n):
                need(sp, m["pool_gol"], n)
                sp.dma_start(w_go[:, 0:KT * D].rearrange("p (k d) -> p k d", k=KT), pick(heads["Wg"], h))\
                    .then_inc(m["dma_go"], 16)
                sp.dma_start(w_go[:, KT * D:], pick(wo_h, h)).then_inc(m["dma_go"], 16)

            def load_prm(h, g, n):
                need(sp, m["act_silu"], 3 * U * (n - 1))
                for i, k in enumerate("kqv"):
                    sp.dma_start(prm[:, g, i, 0:TAPS], pick(cw_h[k + "cw"], h)).then_inc(m[f"dma_prm{g}"], 16)
                    sp.dma_start(prm[:, g, i, TAPS:], pick(cb_h[k + "cb"], h)).then_inc(m[f"dma_prm{g}"], 16)

            def load_bcol(h, g, n):
                need(sp, m["pool_diag"], NC * (n - 1))
                if isinstance(h, int):
                    src = b_cols[:, (G * h + g) * NC * U:(G * h + g + 1) * NC * U]
                else:
                    src = b_cols.rearrange("p (h r) -> p h r", h=NH)[:, bass.ds(h, 1), g * NC * U:(g + 1) * NC * U]\
                        .rearrange("p o r -> p (o r)")
                sp.dma_start(bcol[:, g].rearrange("p c u -> p (c u)"), src).then_inc(m[f"dma_bcol{g}"], 16)

            def row(ap, t):
                return (ap[t:t + 1] if isinstance(t, int) else ap[bass.ds(t, 1)]).broadcast_to([P, U * CX])

            def load_decay(n, c):
                t, par = NC * n + c, c % 2
                need(sp, m["dve_scan"], t - 1)
                sp.dma_start(decay[:, par], row(a_rows, t)).then_inc(m[f"dma_decay{par}"], 16)

            def load_cum(n, c):
                t, par = NC * n + c, c % 2
                need(sp, m["dve_z"], t - 1)
                sp.dma_start(cum[:, par].rearrange("p u x -> p (u x)"),
                             row(g_rows, t)).then_inc(m[f"dma_cum{par}"], 16)

            load_kqv(0, 0)
            load_prm(0, 0, 0)
            load_go(0, 0)
            load_bcol(0, 0, 0)
            load_decay(0, 0)
            load_cum(0, 0)
            load_prm(0, 1, 1)
            load_bcol(0, 1, 1)
            load_decay(0, 1)
            load_cum(0, 1)
            sp.dma_start(lnw[:, :], w["ln_w"].rearrange("(p o) -> p o", o=1)).then_inc(m["dma_const"], 16)
            sp.dma_start(lnb[:, :], w["ln_b"].rearrange("(p o) -> p o", o=1)).then_inc(m["dma_const"], 16)
            load_kqv(0, 1)
            load_go(0, 1)
            load_decay(0, 2)

            def body(h, last):
                for g in range(G):
                    n = G * h + g
                    for c in range(NC):
                        if not (last and g == G - 1 and c >= NC - 3):
                            load_decay(*later(n, c, 3))
                        if not (last and g == G - 1 and c >= NC - 2):
                            load_cum(*later(n, c, 2))
                        if last:
                            continue
                        if c == 0:
                            load_kqv(h + 1, n + 2)
                        if c == 1:
                            load_prm(h + 1, g, n + 2)
                        if c == 2:
                            load_go(h + 1, n + 2)
                            load_bcol(h + 1, g, n + 2)

            body(0, False)
            with sp.Fori(1, NH - 1) as h:
                body(h, False)
            body(NH - 1, True)

        @block.gpsimd
        def _(pool):
            def bc(ap, n):
                return ap.rearrange("p (u o) -> p u o", o=1).broadcast_to([P, U, n])

            def all_units(ap):
                return ap.rearrange("p (o c) -> p o c", o=1).broadcast_to([P, U, C])

            def strengths(n, c, h):
                t, g = NC * n + c, h[1]
                pool.wait_ge(m[f"dma_bcol{g}"], 16 * (h[0] + 1))
                need(pool, m["dve_scan"], t)
                nc.gpsimd.tensor_tensor(diag[:, :, 1:CX], all_units(ident[:, :]), bc(bcol[:, g, c], C),
                                        ALU.mult).then_inc(m["pool_diag"], 1)

            def system16(n, c):
                t, par = NC * n + c, c % 2
                pool.wait_ge(m["dve_at"], t + 1)
                need(pool, m["pe_y"], NL * (t - 1))
                need(pool, m["pool_tt"], t - 1)
                nc.gpsimd.tensor_tensor(am16[:, par], at[:, par], all_units(ident[:, :]),
                                        ALU.subtract).then_inc(m["pool_am"], 1)

            def first_inverse(n, c):
                t, par = NC * n + c, c % 2
                pool.wait_ge(m["pool_am"], t + 1)
                need(pool, m["pe_tr"], t - 1)
                nc.gpsimd.tensor_tensor(tt16[:, par], am16[:, par], all_units(mask0t[:, :]),
                                        ALU.mult).then_inc(m["pool_tt"], 1)

            def system(n, c):
                t, par = NC * n + c, c % 2
                pool.wait_ge(m["pool_am"], t + 1)
                nc.gpsimd.tensor_tensor(at[:, par], at[:, par], all_units(ident[:, :]),
                                        ALU.add).then_inc(m["pool_atp"], 1)

            def scaled_k(n, c, g):
                par, cols = c % 2, slice(c * C, (c + 1) * C)
                pool.wait_ge(m[f"dma_cum{par}"], 16 * (NC // 2 * n + c // 2 + 1))
                pool.wait_ge(m["act_silu"], 3 * U * n + 2 * U)
                need(pool, m["pe_kz"], nz(n, c))
                nc.gpsimd.tensor_tensor(kg[:, :, :], kb[:, g, :, cols], cum[:, par, :, 0:C],
                                        ALU.mult).then_inc(m["pool_kg"], 1)

            def scaled_q(n, c, g):
                par, cols = c % 2, slice(c * C, (c + 1) * C)
                pool.wait_ge(m[f"dma_cum{par}"], 16 * (NC // 2 * n + c // 2 + 1))
                pool.wait_ge(m["act_silu"], 3 * U * n + 2 * U)
                need(pool, m["pe_o"], NC * n + c)
                nc.gpsimd.tensor_tensor(qg[:, :, :], qb[:, g, :, cols], cum[:, par, :, 1:CX],
                                        ALU.mult).then_inc(m["pool_qg"], 1)

            def state(n, c):
                s, par = NC * n + c, c % 2
                pool.wait_ge(m[f"dma_cum{par}"], 16 * (NC // 2 * n + c // 2 + 1))
                pool.wait_ge(m["dve_z"], s)
                nc.gpsimd.tensor_tensor(zs[:, :, :], z[:, :, :], bc(cum[:, par, :, C], D),
                                        ALU.mult).then_inc(m["pool_zs"], 1)

            def root(n, c):
                s = NC * n + c
                pool.wait_ge(m["dve_var"], s + 1)
                need(pool, m["act_on"], s)
                nc.gpsimd.tensor_tensor(rstd[:, :], var[:, :], nhalf[:, :], ALU.pow).then_inc(m["pool_rstd"], 1)

            def gated(n, c, g):
                s = NC * n + c
                pool.wait_ge(m["act_oa"], s + 1)
                pool.wait_ge(m["act_gate"], U * (n + 1))
                nc.gpsimd.tensor_tensor(oa[:, :, :], oa[:, :, :], gb[:, g, :, c * C:(c + 1) * C],
                                        ALU.mult).then_inc(m["pool_og"], 1)

            def low(n, c):
                pool.wait_ge(m["act_oh"], NC * n + c + 1)
                nc.gpsimd.tensor_tensor(ol[:, :, :], oa[:, :, :], oh[:, :, :],
                                        ALU.subtract).then_inc(m["pool_ol"], 1)

            def split_kqv(n):
                pool.wait_ge(m["act_wh"], n + 1)
                nc.gpsimd.tensor_tensor(kqv16[:, 1], w_kqv[:, :, :, :], kqv16[:, 0],
                                        ALU.subtract).then_inc(m["pool_wl"], 1)

            def split_go(n, g):
                pool.wait_ge(m["act_goh"], 2 * (n + 1))
                nc.gpsimd.tensor_tensor(gate16[:, 1], w_go[:, 0:KT * D], gate16[:, 0], ALU.subtract)
                nc.gpsimd.tensor_tensor(wo16[:, g, 1], w_go[:, KT * D:], wo16[:, g, 0],
                                        ALU.subtract).then_inc(m["pool_gol"], 1)

            split_kqv(0)
            made = [0]

            def chain(ins):
                made[0] += 1
                ins.then_inc(m["pool_const"], 1)
                pool.wait_ge(m["pool_const"], made[0])

            def fill(out, value, test, base, pattern, mult):
                chain(nc.gpsimd.affine_select(out=out, in_=out, compare_op=test, fill=value, base=base,
                                              pattern=pattern, channel_multiplier=mult))

            chain(nc.gpsimd.memset(ident[:, :], 0.0))
            fill(ident[:, :], 1.0, ALU.not_equal, 0, [[-1, P]], 1)
            chain(nc.gpsimd.tensor_copy(ident16[:, :], ident[:, :]))
            chain(nc.gpsimd.memset(diag[:, :, :], 0.0))
            chain(nc.gpsimd.memset(y16[:, :, :, :], 0.0))
            tb = mask0t[:, :].rearrange("p (b two) -> p b two", two=2)
            chain(nc.gpsimd.memset(mask0t[:, :], 0.0))
            chain(nc.gpsimd.memset(tb[:, :, 1], -1.0))
            fill(tb[:, :, 1], 0.0, ALU.is_equal, 0, [[-2, P // 2]], 1)
            fill(mask0t[:, :], -1.0, ALU.not_equal, 0, [[-1, P]], 1)
            for li, mb in enumerate(LEVELS):
                nb = P // (2 * mb)
                blk = blocks[:, :].rearrange("p (b two m) -> p b two m", two=2, m=mb)[:, :, 0, :]
                chain(nc.gpsimd.memset(blocks[:, :], 0.0))
                chain(nc.gpsimd.memset(blk, -1.0))
                fill(blk, 0.0, ALU.is_ge, -mb, [[-2 * mb, nb], [0, mb]], 1)
                fill(blk, 0.0, ALU.is_ge, 2 * mb - 1, [[2 * mb, nb], [0, mb]], -1)
                fill(blocks[:, :], -1.0, ALU.not_equal, 0, [[-1, P]], 1)
                chain(nc.gpsimd.tensor_copy(masks[:, li].rearrange("p (b m) -> p b m", m=mb), blk))
                for u in range(U):
                    chain(nc.gpsimd.tensor_copy(halves(y16[:, li, u], mb, 1), halves(ident[:, :], mb, 1)))
            nc.gpsimd.memset(nhalf[:, :], -0.5).then_inc(m["pool_ready"], 1)

            strengths(0, 0, (0, 0))
            split_go(0, 0)
            system16(0, 0)
            first_inverse(0, 0)
            system(0, 0)
            strengths(0, 1, (0, 0))
            system16(0, 1)
            first_inverse(0, 1)
            system(0, 1)
            strengths(0, 2, (0, 0))
            split_kqv(1)

            def body(h, first, last):
                for g in range(G):
                    n = G * h + g
                    for c in range(NC):
                        end = last and g == G - 1
                        more = not (end and c == NC - 1)
                        prev = not (first and g == 0 and c == 0)
                        n1, c1 = later(n, c, 1)
                        n2, c2 = later(n, c, 2)
                        more2 = not (end and c >= NC - 2)
                        g1 = g if c1 else 1 - g
                        g2 = g if c < NC - 2 else 1 - g
                        before = (n, c - 1, g) if c else (n - 1, NC - 1, 1 - g)
                        if c:
                            state(n, c)
                        if c1 and more:
                            scaled_k(n1, c1, g1)
                        if prev:
                            gated(*before)
                            low(*before[:2])
                        if more2:
                            system16(n2, c2)
                        if c == NC - 1 and not last:
                            split_kqv(n + 2)
                        if more2:
                            first_inverse(n2, c2)
                        root(n, c)
                        if c == 1 and not end:
                            split_go(n + 1, 1 - g)
                        if c1 and more:
                            scaled_q(n1, c1, g1)
                        if not (end and c >= NC - 3):
                            strengths(*later(n, c, 3), (h, g) if c == 0 else ((h, 1) if g == 0 else (h + 1, 0)))
                        if more2:
                            system(n2, c2)

            body(0, True, False)
            with pool.Fori(1, NH - 1) as h:
                body(h, False, False)
            body(NH - 1, False, True)
            gated(G * NH - 1, NC - 1, G - 1)
            low(G * NH - 1, NC - 1)

        @block.vector
        def _(dve):
            pr = prod[:, :].rearrange("p (u x) -> p u x", u=U)

            def decays(n, c):
                t, par = NC * n + c, c % 2
                dve.wait_ge(m["pool_diag"], t + 1)
                dve.wait_ge(m[f"dma_decay{par}"], 16 * (NC // 2 * n + c // 2 + 1))
                need(dve, m["act_kdec"], t)
                need(dve, m["dve_mix"], t)
                nc.vector.tensor_tensor_scan(prod[:, :], decay[:, par], diag[:, :, :].rearrange("p u x -> p (u x)"),
                                             0.0, ALU.mult, ALU.add).then_inc(m["dve_scan"], 1)

            def system(n, c):
                t, par = NC * n + c, c % 2
                dve.wait_ge(m["pe_gram"], 2 * t + 1)
                dve.wait_ge(m["dve_scan"], t + 1)
                need(dve, m["pe_aw"], t - 1)
                nc.vector.tensor_tensor(at[:, par], units(TURN), pr[:, :, 0:C], ALU.mult).then_inc(m["dve_at"], 1)

            def mixing(n, c):
                t, par = NC * n + c, c % 2
                dve.wait_ge(m["pe_gram"], 2 * t + 2)
                need(dve, m["pe_o"], t - 1)
                nc.vector.tensor_tensor(mix[:, par], units(TURN), pr[:, :, 1:CX], ALU.mult).then_inc(m["dve_mix"], 1)

            def level(n, c, j):
                t = NC * n + c
                mb = LEVELS[j]
                nb = P // (2 * mb)
                dve.wait_ge(m["pe_y"], NL * t + j + 1)
                nc.vector.tensor_tensor(
                    even(y16[:, j], mb),
                    bank[DIFF][:, 0:U * C // 2].rearrange("p (u b m) -> p u b m", u=U, m=mb),
                    masks[:, j].rearrange("p (o b m) -> p o b m", o=1, m=mb).broadcast_to([P, U, nb, mb]),
                    ALU.mult).then_inc(m["dve_y"], 1)

            def right_side(n, c):
                s = NC * n + c
                dve.wait_ge(m["pe_kz"], nz(n, c) + 1)
                dve.wait_ge(m["act_vt"], s + 1)
                need(dve, m["act_rhs16"], s)
                need(dve, m["dve_res"], s)
                nc.vector.tensor_tensor(rhs[:, :, :], vt[:, :, :], units(SOLVE), ALU.subtract)\
                    .then_inc(m["dve_rhs"], 1)

            def residual(n, c):
                s = NC * n + c
                dve.wait_ge(m["pe_aw"], s + 1)
                dve.wait_ge(m["act_rhs16"], s + 1)
                nc.vector.tensor_tensor(res16[:, :, :], (rhs if c else vt)[:, :, :], units(SOLVE), ALU.subtract)\
                    .then_inc(m["dve_res"], 1)

            def corrected(n, c):
                s = NC * n + c
                dve.wait_ge(m["pe_tr"], s + 1)
                nc.vector.tensor_tensor(wv[:, :, :], wv[:, :, :], units(SOLVE), ALU.add).then_inc(m["dve_w"], 1)

            def new_state(n, c):
                s = NC * n + c
                dve.wait_ge(m["pe_z"], s + 1)
                if c:
                    dve.wait_ge(m["pool_zs"], nz(n, c) + 1)
                    need(dve, m["pe_kz"], nz(n, c) + 1)
                    dve.wait_ge(m["pe_o"], s + 1)
                    nc.vector.tensor_tensor(z[:, :, :], zs[:, :, :], units(UPD), ALU.add).then_inc(m["dve_z"], 1)
                else:
                    need(dve, m["pe_o"], s)
                    nc.vector.tensor_copy(z[:, :, :], units(UPD)).then_inc(m["dve_z"], 1)

            def statistics(n, c):
                s = NC * n + c
                dve.wait_ge(m["pe_o"], s + 1)
                need(dve, m["dve_mv"], U * s)
                for u in range(U):
                    nc.vector.bn_stats(bn[:, u], bank[OUT][:, u * D:(u + 1) * D]).then_inc(m["dve_bn"], 1)

            def aggregated(n, c):
                s = NC * n + c
                for u in range(U):
                    nc.vector.bn_aggr(mv[:, u], bn[:, u]).then_inc(m["dve_mv"], 1)
                dve.wait_ge(m["dve_mv"], U * (s + 1))
                need(dve, m["pool_rstd"], s)
                nc.vector.tensor_scalar(var[:, :], mv[:, :, 1], EPS / D, None, ALU.add).then_inc(m["dve_var"], 1)

            def shifts(n, c):
                s = NC * n + c
                dve.wait_ge(m["pool_rstd"], s + 1)
                need(dve, m["act_on"], s)
                nc.vector.scalar_tensor_tensor(out=shift[:, :], in0=mv[:, :, 0], scalar=-1.0, in1=rstd[:, :],
                                               op0=ALU.mult, op1=ALU.mult).then_inc(m["dve_shift"], 1)

            def output(n, c, g, k):
                dve.wait_ge(m["pe_wo"], KT * (NC * n + c) + k + 1)
                x = xs[k][:, g, :, c * C:(c + 1) * C]
                nc.vector.scalar_tensor_tensor(out=x, in0=units(UPD), scalar=1.0 / WS, in1=x,
                                               op0=ALU.mult, op1=ALU.add).then_inc(m["dve_out"], 1)

            def tap(q, i, j, par, d):
                dst = (kb, qb, vb)[i][:, par, j]
                if d == 1:
                    dve.wait_ge(m["act_acc"], q + 1)
                else:
                    dve.wait_ge(m["dve_tap"], 2 * q + d - 1)
                nc.vector.scalar_tensor_tensor(
                    out=dst[:, d:S], in0=bank[PJ[j % 2]][:, 0:S - d], scalar=prs[:, par, i, TAPS - 1 - d:TAPS - d],
                    in1=dst[:, d:S], op0=ALU.mult, op1=ALU.add)\
                    .then_inc(m["dve_tap"] if d < TAPS - 1 else m["dve_conv"], 1)

            def taps(n, g, h):
                dve.wait_ge(m[f"dma_prm{g}"], 96 * (h + 1))
                need(dve, m["dve_conv"], 3 * U * (n - 1))
                need(dve, m["act_acc"], 3 * U * (n - 1))
                nc.vector.tensor_scalar(prs[:, g], prm[:, g, :, 0:TAPS], 1.0 / WS, None, ALU.mult)\
                    .then_inc(m["dve_prs"], 1)

            taps(0, 0, 0)
            dve.wait_ge(m["dve_prs"], 1)
            for i in range(3):
                for j in range(U):
                    for d in range(1, TAPS):
                        tap(U * i + j, i, j, 0, d)
            dve.wait_ge(m["pool_ready"], 1)
            decays(0, 0)
            system(0, 0)
            mixing(0, 0)
            taps(1, 1, 0)
            level(0, 0, 0)
            decays(0, 1)
            system(0, 1)
            for j in range(1, NL):
                level(0, 0, j)
                if j == 1:
                    mixing(0, 1)

            def body(h, first, last):
                for g in range(G):
                    n = G * h + g
                    for c in range(NC):
                        end = last and g == G - 1
                        more = not (end and c == NC - 1)
                        prev = not (first and g == 0 and c == 0)
                        n1, c1 = later(n, c, 1)
                        n2, c2 = later(n, c, 2)
                        more2 = not (end and c >= NC - 2)
                        before = (n, c - 1, g) if c else (n - 1, NC - 1, 1 - g)
                        q0 = 3 * U * (n + 1) + U * c

                        def mine(j, d):
                            tap(q0 + j, c, j, 1 - g, d)

                        def carried(d):
                            tap(q0 - 1, c - 1, U - 1, 1 - g, d)

                        if c == 0 and not end:
                            dve.wait_ge(m["dve_prs"], n + 2)
                        if c:
                            right_side(n, c)
                        if c and not end:
                            carried(1)
                        if more:
                            level(n1, c1, 0)
                        if c and not end:
                            carried(2)
                            carried(3)
                        if more2:
                            decays(n2, c2)
                        residual(n, c)
                        if more:
                            level(n1, c1, 1)
                        corrected(n, c)
                        if c < NC - 1 and not end:
                            mine(0, 1)
                            mine(0, 2)
                        if more:
                            level(n1, c1, 2)
                        if c < NC - 1 and not end:
                            mine(0, 3)
                            mine(1, 1)
                        statistics(n, c)
                        if more:
                            level(n1, c1, 3)
                        if c < NC - 1 and not end:
                            mine(1, 2)
                        if more2:
                            system(n2, c2)
                        if c < NC - 1 and not end:
                            mine(1, 3)
                        if more:
                            level(n1, c1, 4)
                        need(dve, m["dve_bn"], U * (NC * n + c + 1))
                        need(dve, m["dve_shift"], NC * n + c)
                        new_state(n, c)
                        aggregated(n, c)
                        if more2:
                            mixing(n2, c2)
                        if c < NC - 1 and not end:
                            mine(2, 1)
                        if more:
                            level(n1, c1, 5)
                        if prev:
                            output(*before, 0)
                        if c < NC - 1 and not end:
                            mine(2, 2)
                        shifts(n, c)
                        if c < NC - 1 and not end:
                            mine(2, 3)
                        if prev:
                            output(*before, 1)
                        if c == NC - 1 and not last:
                            taps(n + 2, g, h + 1)

            body(0, True, False)
            with dve.Fori(1, NH - 1) as h:
                body(h, False, False)
            body(NH - 1, False, True)
            for k in range(KT):
                output(G * NH - 1, NC - 1, G - 1, k)
            dve.wait_ge(m["dve_out"], KT * STEPS)

        @block.scalar
        def _(act):
            def split_kqv(n):
                act.wait_ge(m["dma_kqv"], 48 * (n + 1))
                nc.scalar.activation(w_kqv[:, :, :, :], w_kqv[:, :, :, :], ACT.Copy, scale=WS)\
                    .then_inc(m["act_w64"], 1)
                act.wait_ge(m["act_w64"], n + 1)
                need(act, m["pe_pj"], 16 * (n - 1) + 12 if not isinstance(n, int) or n else 0)
                nc.scalar.activation(kqv16[:, 0], w_kqv[:, :, :, :], ACT.Copy).then_inc(m["act_wh"], 1)

            def split_go(n, g):
                act.wait_ge(m["dma_go"], 32 * (n + 1))
                nc.scalar.activation(w_go[:, :], w_go[:, :], ACT.Copy, scale=WS).then_inc(m["act_go64"], 1)
                act.wait_ge(m["act_go64"], n + 1)
                need(act, m["pe_pj"], 16 * n)
                need(act, m["pe_wo"], KT * NC * (n - 1))
                nc.scalar.activation(gate16[:, 0], w_go[:, 0:KT * D], ACT.Copy).then_inc(m["act_goh"], 1)
                nc.scalar.activation(wo16[:, g, 0], w_go[:, KT * D:], ACT.Copy).then_inc(m["act_goh"], 1)

            def acc(q, npj, i, j, par, n):
                act.wait_ge(m["pe_pj"], npj + 1)
                if j == 0:
                    act.wait_ge(m["dve_prs"], n + 1)
                    need(act, m["pe_gram"], 2 * NC * (n - 1))
                    need(act, m[("pool_kg", "pool_qg", "pe_vt")[i]], (NC - 1 if i < 2 else NC) * (n - 1))
                    need(act, m["pe_kt"], NC * (n - 1))
                nc.scalar.activation((kb, qb, vb)[i][:, par, j], bank[PJ[j % 2]][:, :], ACT.Identity,
                                     bias=prm[:, par, i, TAPS:], scale=prs[:, par, i, TAPS - 1:TAPS])\
                    .then_inc(m["act_acc"], 1)

            def silu(q, i, j, par):
                dst = (kb, qb, vb)[i][:, par, j]
                act.wait_ge(m["dve_conv"], q + 1)
                nc.scalar.activation(dst, dst, ACT.Silu).then_inc(m["act_silu"], 1)

            def gate(n, g, j):
                act.wait_ge(m["pe_pj"], 16 * n + 12 + j + 1)
                if j == 0:
                    need(act, m["pool_og"], NC * (n - 1))
                nc.scalar.activation(gb[:, g, j], bank[PJ[j % 2]][:, :], ACT.Sigmoid, scale=1.0 / WS)\
                    .then_inc(m["act_gate"], 1)

            def kdecayed(n, c):
                t, par = NC * n + c, c % 2
                act.wait_ge(m["pe_kt"], t + 1)
                need(act, m["pe_z"], t - 1)
                for u in range(U):
                    ins = nc.scalar.activation(kdec[:, par, u], bank[TURN][:, u * D:(u + 1) * D], ACT.Copy,
                                               scale=prod[:, (u + 1) * CX - 1:(u + 1) * CX])
                ins.then_inc(m["act_kdec"], 1)

            def first_inverse(n, c):
                t = NC * n + c
                act.wait_ge(m["pe_l0"], t + 1)
                need(act, m["pe_y"], NL * t)
                nc.scalar.activation(t16[:, :, :], units(DIFF), ACT.Copy).then_inc(m["act_t0"], 1)

            half = U * C // 2

            def level(n, c, j):
                mb = LEVELS[j]
                act.wait_ge(m["pe_t"], NL * (NC * n + c) + j + 1)
                nc.scalar.activation(even(t16[:, :, :], mb),
                                     bank[LEV][:, 0:half].rearrange("p (u b m) -> p u b m", u=U, m=mb),
                                     ACT.Copy).then_inc(m["act_t"], 1)

            def level_turned(n, c, j):
                mb, par = LEVELS[j], c % 2
                act.wait_ge(m["pe_t"], NL * (NC * n + c) + j + 1)
                nc.scalar.activation(odd(tt16[:, par], mb),
                                     bank[LEV][:, half:].rearrange("p (u b m) -> p u b m", u=U, m=mb),
                                     ACT.Copy).then_inc(m["act_tt"], 1)

            def values(n, c):
                s = NC * n + c
                act.wait_ge(m["pe_vt"], s + 1)
                need(act, m["dve_res"], s)
                need(act, m["act_rhs16"], s)
                nc.scalar.activation(vt[:, :, :], units(TURN), ACT.Copy).then_inc(m["act_vt"], 1)

            def right_side(n, c):
                s = NC * n + c
                if c:
                    act.wait_ge(m["dve_rhs"], nz(n, c) + 1)
                else:
                    act.wait_ge(m["act_vt"], s + 1)
                need(act, m["pe_w0"], s)
                nc.scalar.activation(rhs16[:, :, :], (rhs if c else vt)[:, :, :], ACT.Copy)\
                    .then_inc(m["act_rhs16"], 1)

            def first_solution(n, c):
                s = NC * n + c
                act.wait_ge(m["pe_w0"], s + 1)
                need(act, m["pe_o"], s)
                need(act, m["pe_z"], s)
                nc.scalar.activation(wv[:, :, :], units(SOLVE), ACT.Copy).then_inc(m["act_w0"], 1)

            def normed(n, c):
                s = NC * n + c
                act.wait_ge(m["dve_shift"], s + 1)
                need(act, m["pe_ot"], s)
                for u in range(U):
                    ins = nc.scalar.activation(on[:, u], bank[OUT][:, u * D:(u + 1) * D], ACT.Identity,
                                               bias=shift[:, u:u + 1], scale=rstd[:, u:u + 1])
                ins.then_inc(m["act_on"], 1)

            def affine(n, c):
                s = NC * n + c
                act.wait_ge(m["pe_ot"], s + 1)
                need(act, m["pool_ol"], s)
                nc.scalar.activation(oa[:, :, :], units(TURN), ACT.Identity, bias=lnb[:, :], scale=lnw[:, :])\
                    .then_inc(m["act_oa"], 1)

            def high(n, c):
                s = NC * n + c
                act.wait_ge(m["pool_og"], s + 1)
                need(act, m["pe_wo"], KT * s)
                nc.scalar.activation(oh[:, :, :], oa[:, :, :], ACT.Copy).then_inc(m["act_oh"], 1)

            split_kqv(0)
            for q in range(3 * U + 1):
                if q < 3 * U:
                    acc(q, q, q // U, q % U, 0, 0)
                if q == U:
                    split_go(0, 0)
                if q:
                    silu(q - 1, (q - 1) // U, (q - 1) % U, 0)
            for j in range(U):
                gate(0, 0, j)
            act.wait_ge(m["dma_const"], 32)
            kdecayed(0, 0)
            first_inverse(0, 0)
            values(0, 0)
            for j in range(NL):
                if j < NL - 1:
                    level(0, 0, j)
                level_turned(0, 0, j)
                if j == 2:
                    kdecayed(0, 1)
            split_kqv(1)

            def body(h, first, last):
                for g in range(G):
                    n = G * h + g
                    for c in range(NC):
                        end = last and g == G - 1
                        more = not (end and c == NC - 1)
                        prev = not (first and g == 0 and c == 0)
                        before = (n, c - 1) if c else (n - 1, NC - 1)
                        n1, c1 = later(n, c, 1)
                        n2, c2 = later(n, c, 2)
                        more2 = not (end and c >= NC - 2)
                        q0 = 3 * U * (n + 1) + U * c
                        pj0 = 4 * U * (n + 1) + U * c

                        def tile(j):
                            if c < NC - 1:
                                acc(q0 + j, pj0 + j, c, j, 1 - g, n + 1)
                            else:
                                gate(n + 1, 1 - g, j)

                        def silu_of(j):
                            if j < 2:
                                silu(q0 + j, c, j, 1 - g)
                            else:
                                silu(q0 - U + j, c - 1, j, 1 - g)

                        if more:
                            first_inverse(n1, c1)
                        right_side(n, c)
                        if not end and c == NC - 1:
                            silu_of(2)
                        first_solution(n, c)
                        if more:
                            level(n1, c1, 0)
                        if prev:
                            normed(*before)
                        if not end and 0 < c < NC - 1:
                            silu_of(2)
                        if not end and c == NC - 1:
                            silu_of(3)
                        if more:
                            level_turned(n1, c1, 0)
                        if not end:
                            tile(0)
                        if not end and 0 < c < NC - 1:
                            silu_of(3)
                        if more:
                            level(n1, c1, 1)
                            level_turned(n1, c1, 1)
                        if prev:
                            affine(*before)
                        if not end:
                            tile(1)
                        if more:
                            level(n1, c1, 2)
                            level_turned(n1, c1, 2)
                            values(n1, c1)
                        if prev:
                            high(*before)
                        if c == 1 and not end:
                            split_go(n + 1, 1 - g)
                        if more:
                            level(n1, c1, 3)
                            level_turned(n1, c1, 3)
                        if c == NC - 1 and not last:
                            split_kqv(n + 2)
                        if not end and c < NC - 1:
                            silu_of(0)
                        if not end:
                            tile(2)
                        if more:
                            level(n1, c1, 4)
                            level_turned(n1, c1, 4)
                        if more2:
                            kdecayed(n2, c2)
                        if more:
                            level_turned(n1, c1, 5)
                        if not end:
                            tile(3)
                        if not end and c < NC - 1:
                            silu_of(1)

            body(0, True, False)
            with act.Fori(1, NH - 1) as h:
                body(h, False, False)
            body(NH - 1, False, True)
            normed(G * NH - 1, NC - 1)
            affine(G * NH - 1, NC - 1)
            high(G * NH - 1, NC - 1)

        @block.tensor
        def _(pe):
            half = U * C // 2

            def at_half(b, o, u):
                return bank[b][:, o + u * C // 2:o + (u + 1) * C // 2]

            def gram(n, c, g, i):
                t = NC * n + c
                pe.wait_ge(m["act_silu"], 3 * U * n + 2 * U)
                cols = slice(c * C, (c + 1) * C)
                if i == 0:
                    need(pe, m["act_vt"], t)
                else:
                    pe.wait_ge(m["dve_at"], t + 1)
                for u in range(U):
                    mm = pe.matmul(units(TURN)[:, u], kb[:, g, u, cols], (kb, qb)[i][:, g, u, cols],
                                   start=True, stop=True)
                mm.then_inc(m["pe_gram"], 1)

            def k_turned(n, c, g):
                pe.wait_ge(m["dve_mix"], NC * n + c + 1)
                for u in range(U):
                    mm = pe.transpose(units(TURN)[:, u], kb[:, g, u, c * C:(c + 1) * C], ident[:, :])
                mm.then_inc(m["pe_kt"], 1)

            def first_inverse(n, c):
                t, par = NC * n + c, c % 2
                pe.wait_ge(m["pool_tt"], t + 1)
                need(pe, m["dve_y"], NL * t)
                for u in range(U):
                    mm = pe.matmul(units(DIFF)[:, u], tt16[:, par, u], ident16[:, :], start=True, stop=True)
                mm.then_inc(m["pe_l0"], 1)

            def level_a(n, c, j):
                t, mb = NC * n + c, LEVELS[j]
                if j == 0:
                    pe.wait_ge(m["act_t0"], t + 1)
                else:
                    pe.wait_ge(m["act_t"], (NL - 1) * t + j)
                for u in range(U):
                    mm = pe.matmul(at_half(DIFF, 0, u), am16[:, c % 2, u], halves(t16[:, u], mb, 0), start=True, stop=True)
                mm.then_inc(m["pe_y"], 1)

            def level_b(n, c, j):
                t, par, mb = NC * n + c, c % 2, LEVELS[j]
                pe.wait_ge(m["dve_y"], NL * t + j + 1)
                need(pe, m["act_tt"], NL * t + j)
                for u in range(U):
                    if j < NL - 1:
                        pe.matmul(at_half(LEV, 0, u), tt16[:, par, u], halves(y16[:, j, u], mb, 0), start=True, stop=True)
                    mm = pe.matmul(at_half(LEV, half, u), y16[:, j, u], halves(tt16[:, par, u], mb, 1),
                                   start=True, stop=True)
                mm.then_inc(m["pe_t"], 1)

            def v_turned(n, c, g):
                s = NC * n + c
                pe.wait_ge(m["act_silu"], 3 * U * n + 3 * U)
                pe.wait_ge(m["act_kdec"], s + 1)
                need(pe, m["act_oa"], s - 1)
                for u in range(U):
                    mm = pe.transpose(units(TURN)[:, u], vb[:, g, u, c * C:(c + 1) * C], ident[:, :])
                mm.then_inc(m["pe_vt"], 1)

            def state_k(n, c):
                s, k = NC * n + c, nz(n, c)
                pe.wait_ge(m["pool_kg"], k + 1)
                pe.wait_ge(m["dve_z"], s)
                pe.wait_ge(m["dve_w"], s)
                for u in range(U):
                    mm = pe.matmul(units(SOLVE)[:, u], kg[:, u], z[:, u], start=True, stop=True)
                mm.then_inc(m["pe_kz"], 1)

            def first_solution(n, c):
                s, par = NC * n + c, c % 2
                pe.wait_ge(m["act_rhs16"], s + 1)
                pe.wait_ge(m["act_tt"], NL * (s + 1))
                need(pe, m["dve_w"], s)
                for u in range(U):
                    mm = pe.matmul(units(SOLVE)[:, u], tt16[:, par, u], rhs16[:, u], start=True, stop=True)
                mm.then_inc(m["pe_w0"], 1)

            def check_solution(n, c):
                s, par = NC * n + c, c % 2
                pe.wait_ge(m["act_w0"], s + 1)
                pe.wait_ge(m["pool_atp"], s + 1)
                for u in range(U):
                    mm = pe.matmul(units(SOLVE)[:, u], at[:, par, u], wv[:, u], start=True, stop=True)
                mm.then_inc(m["pe_aw"], 1)

            def correction(n, c):
                s, par = NC * n + c, c % 2
                pe.wait_ge(m["dve_res"], s + 1)
                for u in range(U):
                    mm = pe.matmul(units(SOLVE)[:, u], tt16[:, par, u], res16[:, u], start=True, stop=True)
                mm.then_inc(m["pe_tr"], 1)

            def update(n, c):
                s, par = NC * n + c, c % 2
                pe.wait_ge(m["dve_w"], s + 1)
                need(pe, m["dve_out"], KT * (s - 1))
                for u in range(U):
                    mm = pe.matmul(units(UPD)[:, u], kdec[:, par, u], wv[:, u], start=True, stop=True)
                mm.then_inc(m["pe_z"], 1)

            def read(n, c, u0, u1):
                s, par = NC * n + c, c % 2
                if u0 == 0:
                    pe.wait_ge(m["dve_w"], s + 1)
                    need(pe, m["act_on"], s)
                    if c:
                        pe.wait_ge(m["pool_qg"], nz(n, c) + 1)
                for u in range(u0, u1):
                    if c:
                        pe.matmul(units(OUT)[:, u], qg[:, u], z[:, u], start=True, stop=False)
                    mm = pe.matmul(units(OUT)[:, u], mix[:, par, u], wv[:, u], start=not c, stop=True)
                if u1 == U:
                    mm.then_inc(m["pe_o"], 1)

            def out_turned(n, c, more=False, final=False):
                s = NC * n + c
                pe.wait_ge(m["act_on"], s + 1)
                if not final:
                    pe.wait_ge(m["act_vt"], s + 2)
                if more:
                    pe.wait_ge(m["act_kdec"], s + 3)
                for u in range(U):
                    mm = pe.transpose(units(TURN)[:, u], on[:, u], ident[:, :])
                mm.then_inc(m["pe_ot"], 1)

            def output(n, c, g, k, final=False):
                s = NC * n + c
                pe.wait_ge(m["pool_ol"], s + 1)
                if not final:
                    pe.wait_ge(m["dve_z"], s + 2)
                need(pe, m["dve_out"], KT * s + k)
                ch = slice(k * P, (k + 1) * P)
                for i, (wh, o) in enumerate(((0, oh), (0, ol), (1, oh))):
                    mm = pe.matmul(bank[UPD][:, :], wo16[:, g, wh, ch], o[:, :, :].rearrange("p u c -> p (u c)"),
                                   start=(i == 0), stop=(i == 2))
                mm.then_inc(m["pe_wo"], 1)

            def project(i, g, j, part):
                cols = slice((G * j + g) * S, (G * j + g + 1) * S)
                terms = [(wh, k, zh) for (wh, zh) in ((0, 0), (0, 1), (1, 0)) for k in range(KT)]
                for x in range(2 * part, 2 * part + 2):
                    wh, k, zh = terms[x]
                    wt = gate16[:, wh, k * D:(k + 1) * D] if i == 3 else kqv16[:, wh, k, i]
                    mm = pe.matmul(bank[PJ[j % 2]][:, :], wt, z_in[:, zh, k, cols], start=(x == 0), stop=(x == 5))
                if part == 2:
                    mm.then_inc(m["pe_pj"], 1)

            pe.wait_ge(m["pool_wl"], 1)
            for i in range(4):
                if i == 3:
                    pe.wait_ge(m["pool_gol"], 1)
                for j in range(U):
                    q = U * i + j - 2
                    if q >= 0:
                        pe.wait_ge(*((m["dve_conv"], q + 1) if q < 3 * U else (m["act_gate"], q + 1 - 3 * U)))
                    for part in range(3):
                        project(i, 0, j, part)
            gram(0, 0, 0, 0)
            gram(0, 0, 0, 1)
            pe.wait_ge(m["pool_ready"], 1)
            k_turned(0, 0, 0)
            first_inverse(0, 0)
            v_turned(0, 0, 0)
            gram(0, 1, 0, 0)
            for j in range(NL):
                level_a(0, 0, j)
                level_b(0, 0, j)
                if j == 1:
                    gram(0, 1, 0, 1)
                if j == 2:
                    k_turned(0, 1, 0)

            def body(h, first, last):
                for g in range(G):
                    n = G * h + g
                    for c in range(NC):
                        end = last and g == G - 1
                        more = not (end and c == NC - 1)
                        prev = not (first and g == 0 and c == 0)
                        before = (n, c - 1, g) if c else (n - 1, NC - 1, 1 - g)
                        n1, c1 = later(n, c, 1)
                        n2, c2 = later(n, c, 2)
                        more2 = not (end and c >= NC - 2)
                        g1 = g if c1 else 1 - g
                        g2 = g if c < NC - 2 else 1 - g

                        def piece(j, part):
                            if part == 0:
                                pe.wait_ge(*bank_free(n, c, j))
                            project(c, 1 - g, j, part)

                        if c:
                            state_k(n, c)
                        if more:
                            first_inverse(n1, c1)
                        if not end and c == 0:
                            pe.wait_ge(m["pool_wl"], n + 2)
                        if not end and c == NC - 1:
                            pe.wait_ge(m["pool_gol"], n + 2)
                        if not end:
                            piece(0, 0)
                            piece(0, 1)
                        if more:
                            level_a(n1, c1, 0)
                        first_solution(n, c)
                        if more:
                            level_b(n1, c1, 0)
                        if not end:
                            piece(0, 2)
                        check_solution(n, c)
                        if more:
                            level_a(n1, c1, 1)
                        if not end:
                            piece(1, 0)
                            piece(1, 1)
                        correction(n, c)
                        if not end:
                            piece(1, 2)
                        if more:
                            level_b(n1, c1, 1)
                        if prev:
                            out_turned(*before[:2], more)
                        read(n, c, 0, U // 2)
                        if more:
                            level_a(n1, c1, 2)
                        read(n, c, U // 2, U)
                        if more:
                            level_b(n1, c1, 2)
                            v_turned(n1, c1, g1)
                        if not end:
                            piece(2, 0)
                        if more:
                            level_a(n1, c1, 3)
                        if not end:
                            piece(2, 1)
                        if more2:
                            gram(n2, c2, g2, 0)
                        if more:
                            level_b(n1, c1, 3)
                        update(n, c)
                        if more:
                            level_a(n1, c1, 4)
                        if not end:
                            piece(2, 2)
                        if more2:
                            gram(n2, c2, g2, 1)
                        if more:
                            level_b(n1, c1, 4)
                        if not end:
                            piece(3, 0)
                        if prev:
                            output(*before, 0)
                        if more:
                            level_a(n1, c1, 5)
                        if more2:
                            k_turned(n2, c2, g2)
                        if not end:
                            piece(3, 1)
                        if more:
                            level_b(n1, c1, 5)
                        if not end:
                            piece(3, 2)
                        if prev:
                            output(*before, 1)

            body(0, True, False)
            with pe.Fori(1, NH - 1) as h:
                body(h, False, False)
            body(NH - 1, False, True)
            out_turned(G * NH - 1, NC - 1, final=True)
            for k in range(KT):
                output(G * NH - 1, NC - 1, G - 1, k, final=True)


def macaron(nc, names, aps, out):
    w = {k.removeprefix("L0_attn_").removeprefix("L0_ffn_"): v for k, v in zip(names, aps)}
    a_rows = nc.dram_tensor("decay_rows", (STEPS, U * CX), F32, kind="Internal").ap()
    g_rows = nc.dram_tensor("cumulative_rows", (STEPS, U * CX), F32, kind="Internal").ap()
    b_cols = nc.dram_tensor("strength_columns", (P, STEPS * U), F32, kind="Internal").ap()
    w_saved = nc.dram_tensor("quantised_weights", (P, 3 * KT * FF), F16, kind="Internal").ap()
    scratch = (a_rows, g_rows, b_cols, w_saved)
    with ExitStack() as ctx:
        stream = ctx.enter_context(nc.sbuf_tensor("stream", [P, KT, B * S], F32))
        with ExitStack() as inner:
            z16 = inner.enter_context(nc.sbuf_tensor("z16", [P, 2, KT, B * S], F16))
            ffn_phase(nc, True, w["x"], None, stream, z16, scratch, w)
            attention_phase(nc, stream, z16, scratch, w)
        ffn_phase(nc, False, None, out, stream, None, scratch, w)


_INS = ["L0_attn_x", "L0_attn_Wq", "L0_attn_Wk", "L0_attn_Wv", "L0_attn_Wa", "L0_attn_ba", "L0_attn_Wb",
        "L0_attn_bb", "L0_attn_Wg", "L0_attn_Wo", "L0_attn_qcw", "L0_attn_qcb", "L0_attn_kcw", "L0_attn_kcb",
        "L0_attn_vcw", "L0_attn_vcb", "L0_attn_ln_w", "L0_attn_ln_b", "L0_ffn_gate_w", "L0_ffn_up_w",
        "L0_ffn_down_w", "L0_ffn_gate_scale", "L0_ffn_up_scale", "L0_ffn_down_scale"]


def kernel(**inputs):
    import concourse.bacc as bacc
    from concourse.bass_utils import run_bass_kernel_spmd

    nc = bacc.Bacc("TRN2", target_bir_lowering=False, num_devices=1)
    arrays, aps = {}, []
    for name in _INS:
        a = np.ascontiguousarray(inputs[name])
        arrays[f"in_{name}"] = a
        aps.append(nc.dram_tensor(f"in_{name}", a.shape, mybir.dt.from_np(a.dtype), kind="ExternalInput").ap())
    out = nc.dram_tensor("out", (B, S, H), F32, kind="ExternalOutput").ap()
    macaron(nc, _INS, aps, out)
    r = run_bass_kernel_spmd(nc, [arrays], core_ids=[0])
    return r.results[0]["out"]
```
